# Optimizing a Trainium2 kernel written in Bass

```python
import numpy as np
import jax
import jax.numpy as jnp

def _softmax(x, axis=-1):
    return jax.nn.softmax(x, axis=axis)

def _gelu(x):
    return jax.nn.gelu(x, approximate=True)

def _silu(x):
    return jax.nn.silu(x)

def _sigmoid(x):
    return jax.nn.sigmoid(x)

def _layernorm(x, axis=-1, eps=1e-05):
    m = jnp.mean(x, axis=axis, keepdims=True)
    v = jnp.var(x, axis=axis, keepdims=True)
    return (x - m) / jnp.sqrt(v + eps)

def _scatter_add(tgt, idx, src, axis=0):
    return tgt.at[idx].add(src)

def _segment_sum(src, seg, n):
    return jax.ops.segment_sum(src, seg, n)
kernel_name = 'mk_decoder_postln_d1_seqx_r8_0f99c6'

def setup_inputs(seed: int=0):
    np.random.seed(seed)
    _w = jnp.asarray

    def _rec_inputs():
        import jax
        import jax.numpy as jnp
        _rk = jax.random.key(seed)
        x = -0.0002928 + 1 * jax.random.normal(jax.random.fold_in(_rk, 1), (64, 64, 128), jnp.float32)
        _lenS = 64 - jax.random.randint(jax.random.fold_in(_rk, 7), (64,), 0, max(1, 64 // 4) + 1, jnp.int32)
        _lenS2 = 64 - jax.random.randint(jax.random.fold_in(_rk, 8), (64,), 0, max(1, 64 // 4) + 1, jnp.int32)
        _ctx_1024P = jax.random.normal(jax.random.fold_in(_rk, 11), (64, 16, 128), jnp.float32)
        _ctx_1024c = jax.random.dirichlet(jax.random.fold_in(_rk, 511), 0.3 * jnp.ones((16,), jnp.float32), (64, 64))
        _ctx_1024t = jnp.einsum('bsk,bkd->bsd', _ctx_1024c, _ctx_1024P)
        _ctx_1024t = _ctx_1024t * jax.lax.rsqrt(jnp.mean(jnp.square(_ctx_1024t)) + 1e-12) * 0.953939
        ctx_1024 = -1.39393e-06 + 0.999914 * (_ctx_1024t + 0.3 * jax.random.normal(jax.random.fold_in(_rk, 611), (64, 64, 128), jnp.float32))
        return (x, ctx_1024)
    x, ctx_1024 = _rec_inputs()

    def _L0_attn_setup():
        import jax, jax.numpy as jnp
        import numpy as np
        B_, S_, D_, N_, R_ = (2, 256, 128, 16, 64)

        def _layernorm(y, g, b, eps=1e-05):
            mu = jnp.mean(y, axis=-1, keepdims=True)
            var = jnp.mean(jnp.square(y - mu), axis=-1, keepdims=True)
            return (y - mu) * jax.lax.rsqrt(var + eps) * g + b
        key = jax.random.key(seed)
        ks = jax.random.split(key, 12)
        x = jax.random.normal(ks[0], (B_, S_, D_), dtype=jnp.float32)
        W_dtw = jax.random.normal(ks[1], (R_, D_), dtype=jnp.float32) * (1.0 / np.sqrt(D_))
        W_dt = jax.random.normal(ks[2], (D_, R_), dtype=jnp.float32) * (1.0 / np.sqrt(R_))
        b_dt = jnp.zeros((D_,), dtype=jnp.float32)
        A_log = jnp.log(jax.random.uniform(ks[3], (D_, N_), minval=0.5, maxval=1.5, dtype=jnp.float32))
        W_B = jax.random.normal(ks[4], (N_, D_), dtype=jnp.float32) * (1.0 / np.sqrt(D_))
        W_C = jax.random.normal(ks[5], (N_, D_), dtype=jnp.float32) * (1.0 / np.sqrt(D_))
        Dp = jnp.ones((D_,), dtype=jnp.float32)
        ln_g = jnp.ones((D_,), dtype=jnp.float32)
        ln_b = jnp.zeros((D_,), dtype=jnp.float32)
        W_out = jax.random.normal(ks[6], (D_, D_), dtype=jnp.float32) * (1.0 / np.sqrt(D_))
        return {'x': x, 'W_dtw': W_dtw, 'W_dt': W_dt, 'b_dt': b_dt, 'A_log': A_log, 'W_B': W_B, 'W_C': W_C, 'Dp': Dp, 'ln_g': ln_g, 'ln_b': ln_b, 'W_out': W_out}
    _L0_attn_all = _L0_attn_setup()
    _L0_attn_in = {k: v for k, v in _L0_attn_all.items() if k in ('W_dtw', 'W_dt', 'b_dt', 'A_log', 'W_B', 'W_C', 'Dp', 'ln_g', 'ln_b', 'W_out')}
    del _L0_attn_all

    def _L0_xattn_setup():
        import jax, jax.numpy as jnp
        import numpy as np
        B, S, H, NH = (2, 256, 128, 4)
        DH = H // NH
        EPS = 1e-06

        def _parallel_stabilized(qh, kh, vh, ig, fg):
            log_fg = jax.nn.log_sigmoid(fg)
            cs = jnp.cumsum(log_fg, axis=2)
            ltr = jnp.tril(jnp.ones((qh.shape[2], qh.shape[2]), dtype=bool))
            log_fg_mat = jnp.where(ltr, cs - jnp.swapaxes(cs, 2, 3), -jnp.inf)
            log_D = log_fg_mat + jnp.swapaxes(ig, 2, 3)
            max_log_D = jnp.max(log_D, axis=-1, keepdims=True)
            D = jnp.exp(log_D - max_log_D)
            qk = jnp.einsum('bhsd,bhtd->bhst', qh, kh) / jnp.sqrt(jnp.float32(DH))
            C = qk * D
            normalizer = jnp.maximum(jnp.abs(jnp.sum(C, axis=-1, keepdims=True)), jnp.exp(-max_log_D))
            return jnp.einsum('bhst,bhtd->bhsd', C / (normalizer + EPS), vh)
        key = jax.random.key(seed)
        ks = jax.random.split(key, 6)
        q = jax.random.normal(ks[0], (B, S, H), dtype=jnp.float32)
        k = jax.random.normal(ks[1], (B, S, H), dtype=jnp.float32)
        v = jax.random.normal(ks[2], (B, S, H), dtype=jnp.float32)
        igate_kernel = jax.random.normal(ks[3], (3 * H, NH), dtype=jnp.float32) * 0.02
        fgate_kernel = jax.random.normal(ks[4], (3 * H, NH), dtype=jnp.float32) * 0.02
        igate_bias = jax.random.normal(ks[5], (NH,), dtype=jnp.float32) * 0.1
        fgate_bias = jnp.linspace(3.0, 6.0, NH, dtype=jnp.float32)
        outnorm_scale = jnp.ones((H,), dtype=jnp.float32)
        return {'q': q, 'k': k, 'v': v, 'igate_kernel': igate_kernel, 'igate_bias': igate_bias, 'fgate_kernel': fgate_kernel, 'fgate_bias': fgate_bias, 'outnorm_scale': outnorm_scale}
    _L0_xattn_all = _L0_xattn_setup()
    _L0_xattn_in = {k: v for k, v in _L0_xattn_all.items() if k in ('igate_kernel', 'igate_bias', 'fgate_kernel', 'fgate_bias', 'outnorm_scale')}
    del _L0_xattn_all

    def _L0_ffn_setup():
        import jax, jax.numpy as jnp
        import numpy as np
        TOP_K = 2
        key = jax.random.key(seed)
        ks = jax.random.split(key, 5)
        B, T, D, F, E = (4, 256, 128, 512, 8)
        s = 0.02
        return {'x': jax.random.normal(ks[0], (B, T, D), jnp.float32), 'gate_w': jax.random.normal(ks[1], (D, E), jnp.float32) * s, 'w1': jax.random.normal(ks[2], (E, D, F), jnp.float32) * s, 'w3': jax.random.normal(ks[3], (E, D, F), jnp.float32) * s, 'w2': jax.random.normal(ks[4], (E, F, D), jnp.float32) * s}
    _L0_ffn_all = _L0_ffn_setup()
    _L0_ffn_in = {k: v for k, v in _L0_ffn_all.items() if k in ('gate_w', 'w1', 'w3', 'w2')}
    del _L0_ffn_all
    return {'x': x, 'ctx_1024': ctx_1024, 'L0_attn_W_dtw': _L0_attn_in['W_dtw'], 'L0_attn_W_dt': _L0_attn_in['W_dt'], 'L0_attn_b_dt': _L0_attn_in['b_dt'], 'L0_attn_A_log': _L0_attn_in['A_log'], 'L0_attn_W_B': _L0_attn_in['W_B'], 'L0_attn_W_C': _L0_attn_in['W_C'], 'L0_attn_Dp': _L0_attn_in['Dp'], 'L0_attn_ln_g': _L0_attn_in['ln_g'], 'L0_attn_ln_b': _L0_attn_in['ln_b'], 'L0_attn_W_out': _L0_attn_in['W_out'], 'L0_xattn_igate_kernel': _L0_xattn_in['igate_kernel'], 'L0_xattn_igate_bias': _L0_xattn_in['igate_bias'], 'L0_xattn_fgate_kernel': _L0_xattn_in['fgate_kernel'], 'L0_xattn_fgate_bias': _L0_xattn_in['fgate_bias'], 'L0_xattn_outnorm_scale': _L0_xattn_in['outnorm_scale'], 'L0_ffn_gate_w': _L0_ffn_in['gate_w'], 'L0_ffn_w1': _L0_ffn_in['w1'], 'L0_ffn_w3': _L0_ffn_in['w3'], 'L0_ffn_w2': _L0_ffn_in['w2']}

def reference(x, ctx_1024, L0_attn_W_dtw, L0_attn_W_dt, L0_attn_b_dt, L0_attn_A_log, L0_attn_W_B, L0_attn_W_C, L0_attn_Dp, L0_attn_ln_g, L0_attn_ln_b, L0_attn_W_out, L0_xattn_igate_kernel, L0_xattn_igate_bias, L0_xattn_fgate_kernel, L0_xattn_fgate_bias, L0_xattn_outnorm_scale, L0_ffn_gate_w, L0_ffn_w1, L0_ffn_w3, L0_ffn_w2):
    import jax
    import jax.numpy as jnp

    def _L0_attn_ref(x, W_dtw, W_dt, b_dt, A_log, W_B, W_C, Dp, ln_g, ln_b, W_out):
        import jax, jax.numpy as jnp
        import numpy as np
        B_, S_, D_, N_, R_ = (2, 256, 128, 16, 64)

        def _layernorm(y, g, b, eps=1e-05):
            mu = jnp.mean(y, axis=-1, keepdims=True)
            var = jnp.mean(jnp.square(y - mu), axis=-1, keepdims=True)
            return (y - mu) * jax.lax.rsqrt(var + eps) * g + b
        dt = jnp.einsum('bsd,rd->bsr', x, W_dtw)
        delta = jax.nn.softplus(jnp.einsum('bsr,dr->bsd', dt, W_dt) + b_dt)
        Bm = jnp.einsum('bsd,nd->bsn', x, W_B)
        Cm = jnp.einsum('bsd,nd->bsn', x, W_C)
        A = -jnp.exp(A_log)

        def step(h, inp):
            d_t, b_t, c_t, x_t = inp
            dA = jnp.exp(d_t[..., None] * A)
            h = dA * h + d_t[..., None] * b_t[:, None, :] * x_t[..., None]
            y_t = jnp.sum(h * c_t[:, None, :], axis=-1)
            return (h, y_t)
        h0 = jnp.zeros((x.shape[0], x.shape[2], A.shape[1]), dtype=x.dtype)
        xs = (jnp.swapaxes(delta, 0, 1), jnp.swapaxes(Bm, 0, 1), jnp.swapaxes(Cm, 0, 1), jnp.swapaxes(x, 0, 1))
        _, ys = jax.lax.scan(step, h0, xs)
        y = jnp.swapaxes(ys, 0, 1) + Dp * x
        y = _layernorm(y, ln_g, ln_b)
        return jnp.einsum('bsd,ed->bse', y, W_out)

    def _L0_xattn_ref(q, k, v, igate_kernel, igate_bias, fgate_kernel, fgate_bias, outnorm_scale):
        import jax, jax.numpy as jnp
        import numpy as np
        B, S, H, NH = (2, 256, 128, 4)
        DH = H // NH
        EPS = 1e-06

        def _parallel_stabilized(qh, kh, vh, ig, fg):
            log_fg = jax.nn.log_sigmoid(fg)
            cs = jnp.cumsum(log_fg, axis=2)
            ltr = jnp.tril(jnp.ones((qh.shape[2], qh.shape[2]), dtype=bool))
            log_fg_mat = jnp.where(ltr, cs - jnp.swapaxes(cs, 2, 3), -jnp.inf)
            log_D = log_fg_mat + jnp.swapaxes(ig, 2, 3)
            max_log_D = jnp.max(log_D, axis=-1, keepdims=True)
            D = jnp.exp(log_D - max_log_D)
            qk = jnp.einsum('bhsd,bhtd->bhst', qh, kh) / jnp.sqrt(jnp.float32(DH))
            C = qk * D
            normalizer = jnp.maximum(jnp.abs(jnp.sum(C, axis=-1, keepdims=True)), jnp.exp(-max_log_D))
            return jnp.einsum('bhst,bhtd->bhsd', C / (normalizer + EPS), vh)
        Bq, Sq, Hq = q.shape
        x = jnp.concatenate([q, k, v], axis=-1)
        ig = x @ igate_kernel + igate_bias
        fg = x @ fgate_kernel + fgate_bias
        ig = jnp.transpose(ig, (0, 2, 1))[..., None]
        fg = jnp.transpose(fg, (0, 2, 1))[..., None]
        qh = jnp.transpose(q.reshape(Bq, Sq, NH, DH), (0, 2, 1, 3))
        kh = jnp.transpose(k.reshape(Bq, Sq, NH, DH), (0, 2, 1, 3))
        vh = jnp.transpose(v.reshape(Bq, Sq, NH, DH), (0, 2, 1, 3))
        h = _parallel_stabilized(qh, kh, vh, ig, fg)
        mean = jnp.mean(h, axis=-1, keepdims=True)
        var = jnp.mean((h - mean) ** 2, axis=-1, keepdims=True)
        h_norm = (h - mean) * jax.lax.rsqrt(var + 1e-05)
        h_norm = h_norm * outnorm_scale.reshape(1, NH, 1, DH)
        out = jnp.transpose(h_norm, (0, 2, 1, 3)).reshape(Bq, Sq, Hq)
        return out

    def _L0_ffn_ref(x, gate_w, w1, w3, w2):
        import jax, jax.numpy as jnp
        import numpy as np
        TOP_K = 2
        logits = jnp.einsum('btd,de->bte', x, gate_w)
        probs = jax.nn.softmax(logits, axis=-1)
        expert_weights, expert_indices = jax.lax.top_k(probs, TOP_K)
        expert_weights = expert_weights / expert_weights.sum(-1, keepdims=True)
        E = w1.shape[0]
        out = jnp.zeros_like(x)
        for i in range(E):
            wi = jnp.where(expert_indices == i, expert_weights, 0.0).sum(-1)
            h = jax.nn.silu(jnp.einsum('btd,df->btf', x, w1[i])) * jnp.einsum('btd,df->btf', x, w3[i])
            out = out + jnp.einsum('btf,fd->btd', h, w2[i]) * wi[..., None]
        return out
    x = _layernorm(x + _L0_attn_ref(x, L0_attn_W_dtw, L0_attn_W_dt, L0_attn_b_dt, L0_attn_A_log, L0_attn_W_B, L0_attn_W_C, L0_attn_Dp, L0_attn_ln_g, L0_attn_ln_b, L0_attn_W_out), axis=-1)
    x = _layernorm(x + _L0_xattn_ref(x, ctx_1024, ctx_1024, L0_xattn_igate_kernel, L0_xattn_igate_bias, L0_xattn_fgate_kernel, L0_xattn_fgate_bias, L0_xattn_outnorm_scale), axis=-1)
    x = _layernorm(x + _L0_ffn_ref(x, L0_ffn_gate_w, L0_ffn_w1, L0_ffn_w3, L0_ffn_w2), axis=-1)
    return x

_drawn_inputs = setup_inputs


def setup_inputs(seed=0):
    import zlib

    import numpy as np

    out = dict(_drawn_inputs(seed))
    spreads = {'L0_attn_b_dt': (0.0, 0.1),
     'L0_attn_Dp': (1.0, 0.2),
     'L0_attn_ln_g': (1.0, 0.2),
     'L0_attn_ln_b': (0.0, 0.1),
     'L0_xattn_outnorm_scale': (1.0, 0.2)}
    factors = {'L0_xattn_igate_bias': 8.0,
     'L0_xattn_fgate_kernel': 5.082,
     'L0_ffn_gate_w': 7.794,
     'L0_ffn_w1': 6.856,
     'L0_ffn_w3': 6.809,
     'L0_ffn_w2': 6.828}
    for name, (base, spread) in spreads.items():
        noise = np.random.default_rng([zlib.crc32(name.encode()), seed]).standard_normal(out[name].shape)
        drawn = base * np.exp(spread * noise) if base else spread * noise
        out[name] = jnp.asarray(drawn.astype(out[name].dtype))
    for name, factor in factors.items():
        out[name] = (out[name] * factor).astype(out[name].dtype)
    return out
```

```python
import concourse.bass as bass
from concourse import mybir
from contextlib import ExitStack


def decoder_layer(nc, x_tok, x_T, ctx_tok, ctx_T, W_dtw_T, W_dt_T, b_dt, A_log, W_BC_T, Dp, ln_g, ln_b, W_out_T,
                  gate_kernel, gate_bias, outnorm, router_w, w1, w3, w2, out):
    f32, bf16, i32 = mybir.dt.float32, mybir.dt.bfloat16, mybir.dt.int32
    ALU, ACT, AX = mybir.AluOpType, mybir.ActivationFunctionType, mybir.AxisListType
    ds = bass.ds
    P = 128
    D, T = x_T.shape
    S = 64
    N = A_log.shape[1]
    R = W_dtw_T.shape[1]
    CH = 512
    NCH = T // CH
    TB = CH // P
    H = 4
    NT = T // P
    BIG = 1.0e30

    ctx = ExitStack()
    with ctx:
        def sb(name, shape, dt=f32):
            return ctx.enter_context(nc.sbuf_tensor(name, shape, dt))

        def pb(name, shape):
            return ctx.enter_context(nc.psum_tensor(name, shape, f32))

        def sem(name):
            return ctx.enter_context(nc.semaphore(name))

        wdtw = sb("wdtw", [D, R])
        wdt = sb("wdt", [R, D])
        bdt = sb("bdt", [D, 1])
        alog = sb("alog", [D, N])
        Aneg = sb("Aneg", [D, N])
        wbc = sb("wbc", [D, 2 * N])
        dp = sb("dp", [D, 1])
        lng = sb("lng", [D, 1])
        lnb = sb("lnb", [D, 1])
        wout = sb("wout", [D, D])
        gk = sb("gk", [P, 3, 2 * H])
        gkv = sb("gkv", [P, 2 * H])
        gbias = sb("gbias", [P, 2 * H])
        ident = sb("ident", [P, P])
        center = sb("center", [P, P])
        gw = sb("gw", [D, D])
        lnb_rep = sb("lnb_rep", [D, P])
        diag_dp = sb("diag_dp", [D, D])
        proj = sb("proj", [D, 2 * D])
        cvec = sb("cvec", [P, D])
        sel = sb("sel", [96, 2 * N, P], bf16)
        eps5 = sb("eps5", [P, 1])
        PAD = CH
        xT = sb("xT", [D, T])
        dx = sb("dx", [D, T + PAD])
        decay = sb("decay", [D, T + PAD])
        bcs = sb("bcs", [96, T + PAD], bf16)
        dt_sb = sb("dt_sb", [R, CH])
        bc32 = sb("bc32", [2 * N, CH])
        res1 = sb("res1", [2 * N, CH])
        u = sb("u", [D, 2, CH])
        h = sb("h", [D, 2, CH])
        c_sb = sb("c_sb", [D, 2, CH])
        hc = sb("hc", [D, 2, CH])
        y_sb = sb("y_sb", [D, CH])
        p_sb = sb("p_sb", [P, TB, D])
        xbuf = sb("xbuf", [P, TB, D])
        xc = sb("xc", [P, TB, D])
        z = sb("z", [P, TB, D])
        st = sb("st", [P, TB, 6])
        mv = sb("mv", [P, TB, 2])
        lv = sb("lv", [P, TB])
        rstd = sb("rstd", [P, TB])
        st2 = sb("st2", [P, TB, 6])
        mv2 = sb("mv2", [P, TB, 2])
        lv2 = sb("lv2", [P, TB])
        rstd2 = sb("rstd2", [P, TB])
        x1_st = sb("x1_st", [P, TB, D])
        x1T_st = sb("x1T_st", [D, CH])
        cT_st = sb("cT_st", [D, CH])
        x1_all = sb("x1_all", [P, NCH + 1, TB, D])
        x1T_all = sb("x1T_all", [D, T + PAD])
        gates = sb("gates", [P, NCH + 1, TB, 2 * H])

        NG = NT * H
        gabs = sb("gabs", [P, NG])
        gexp = sb("gexp", [P, NG])
        glog = sb("glog", [P, NG])
        lfg = sb("lfg", [P, NG])
        tri = sb("tri", [P, P])
        cs_sb = sb("cs_sb", [P, NG])
        g_sb = sb("g_sb", [P, NG])
        fence = sb("fence", [P, P])
        mrow = sb("mrow", [P, P])
        nlog = sb("nlog", [P, NG])
        floor_ = sb("floor_", [P, NG])
        maskT = sb("maskT", [P, S])
        onorm = sb("onorm", [P, D])
        x1c = sb("x1c", [P, TB, D])
        x1Tc = sb("x1Tc", [D, CH])
        cTc = sb("cTc", [D, CH])
        V1 = sb("V1", [P, TB * H, S // 2 + 1])
        lmask, Dm, Cm, mb = (v[:].rearrange("p a c -> p (a c)") for v in (u, h, c_sb, hc))
        rs = sb("rs", [P, TB * H])
        rinv = sb("rinv", [P, TB * H])
        hsum = sb("hsum", [P, TB * H])
        vsum = sb("vsum", [P, TB * H])
        vlog = sb("vlog", [P, TB * H])
        vrs = sb("vrs", [P, TB * H])
        hv = sb("hv", [P, TB * H, S // 2])
        cen = sb("cen", [P, TB * H, S // 2])
        sq = sb("sq", [P, TB * H, S // 2])
        flat3 = lambda v: v[:].rearrange("p a b -> p (a b)")
        pabs, pexp, plog, prel = flat3(hv), flat3(cen), flat3(sq), flat3(x1c)
        delta = x1Tc[:]
        E, F = w1.shape[0], w1.shape[2]
        FB = F // P
        x2_st = sb("x2_st", [P, TB, D])
        x2T_st = sb("x2T_st", [D, CH])
        rw = sb("rw", [D, E])
        logits = sb("logits", [P, NCH, TB, E])
        w1_sb = decay[:, 0:E * F].rearrange("p (e f) -> p e f", e=E)
        w3_sb = sb("w3_sb", [D, E, F])
        w2_sb = x1T_all[:, 0:E * F].rearrange("p (e f d) -> p e f d", e=E, f=FB)
        rank = sb("rank", [P, E])
        top = sb("top", [P, 2, NT])
        tie = sb("tie", [P, NT, E])
        tmax = sb("tmax", [P, NT])
        hot = sb("hot", [P, 2, NT, E])
        rest = sb("rest", [P, NT, E])
        share = sb("share", [P, 2, NT])
        wi = sb("wi", [P, NCH, TB, E])
        sil = u
        hT = x1_all[:].rearrange("p c b d -> p (c b d)")[:, 0:2 * FB * CH].rearrange("p (a f c) -> p a f c", a=2, f=FB)
        acc = sb("acc", [P, TB, D])
        zf = sb("zf", [P, TB, D])
        x2_all = xT
        x2T_all = dx
        m_dram = nc.dram_tensor("m_dram", (NG, P), f32, kind="Internal").ap()

        pa = pb("pa", [P, 2, CH])
        pB = pb("pB", [P, 2, CH])
        pC = pb("pC", [P, 2, CH])
        py = pb("py", [P, CH])
        pq = pb("pq", [P, CH])

        ld_w, ld_x, ld_g = sem("ld_w"), sem("ld_x"), sem("ld_g")
        s_memset, s_const, s_const2 = sem("s_memset"), sem("s_const"), sem("s_const2")
        s_setup_pe, s_proj, s_aexp = sem("s_setup_pe"), sem("s_proj"), sem("s_aexp")
        s_A = sem("s_A")
        s_dtp, s_dts, s_pre, s_bcp = sem("s_dtp"), sem("s_dts"), sem("s_pre"), sem("s_bcp")
        s_abs, s_ex, s_log, s_rel, s_dl, s_dx, s_dec = (sem("s_abs"), sem("s_ex"), sem("s_log"), sem("s_rel"),
                                                        sem("s_dl"), sem("s_dx"), sem("s_dec"))
        s_b1, s_b2, s_b3, s_b4 = sem("s_b1"), sem("s_b2"), sem("s_b3"), sem("s_b4")
        B_ready, C_ready, a_ready, C_copied = sem("B_ready"), sem("C_ready"), sem("a_ready"), sem("C_copied")
        u_done, h_done, hc_done, y_acc = sem("u_done"), sem("h_done"), sem("hc_done"), sem("y_acc")
        y_copied, p_done, p_copied, st_done = sem("y_copied"), sem("p_done"), sem("p_copied"), sem("st_done")
        mv_done, lv_done, rs_done, z_done = sem("mv_done"), sem("lv_done"), sem("rs_done"), sem("z_done")
        xc_done = sem("xc_done")
        st2_done, mv2_done, lv2_done, rs2_done, x1_done = (sem("st2_done"), sem("mv2_done"), sem("lv2_done"),
                                                           sem("rs2_done"), sem("x1_done"))
        x1T_done, x1T_copied, g_done, g_copied = sem("x1T_done"), sem("x1T_copied"), sem("g_done"), sem("g_copied")
        ld_chunk, ld_ctx, x1_kept, x1T_kept = sem("ld_chunk"), sem("ld_ctx"), sem("x1_kept"), sem("x1T_kept")
        s_reset = sem("s_reset")
        s_bc = sem("s_bc")
        s_out = sem("s_out")
        x_blocks = x_tok.rearrange("(c b p) d -> p c b d", p=P, b=TB)
        out_blocks = out.rearrange("(c b p) d -> p c b d", p=P, b=TB)
        passed, act_step, b_free, hv_done, stb_done = sem("passed"), sem("act_step"), sem("b_free"), sem("hv_done"), sem("stb_done")
        gate_step, g_const, m_ready, m_stored, E_ready = (sem("gate_step"), sem("g_const"), sem("m_ready"),
                                                          sem("m_stored"), sem("E_ready"))
        b_x1, b_x1T, b_cT, b_v, b_mb = sem("b_x1"), sem("b_x1T"), sem("b_cT"), sem("b_v"), sem("b_mb")
        qk_done, lm1, lm2, D_done, C_done, av_done = (sem("qk_done"), sem("lm1"), sem("lm2"), sem("D_done"),
                                                      sem("C_done"), sem("av_done"))
        n_step, cen_done, sq_done, vsum_done, vlog_done, vrs_done = (sem("n_step"), sem("cen_done"), sem("sq_done"),
                                                                     sem("vsum_done"), sem("vlog_done"), sem("vrs_done"))
        sc_done, zb_done, mvb_done, lvb_done, rsb_done, x2_done = (sem("sc_done"), sem("zb_done"), sem("mvb_done"),
                                                                   sem("lvb_done"), sem("rsb_done"), sem("x2_done"))
        x2T_done, x2T_copied, lg_done, lg_copied, x2_kept, x2T_kept = (sem("x2T_done"), sem("x2T_copied"),
                                                                       sem("lg_done"), sem("lg_copied"),
                                                                       sem("x2_kept"), sem("x2T_kept"))
        ld_f, r_step, r_exp, wi_ready = sem("ld_f"), sem("r_step"), sem("r_exp"), sem("wi_ready")
        h_up, sil_done, hT_done, dn_done, acc_done = (sem("h_up"), sem("sil_done"), sem("hT_done"), sem("dn_done"),
                                                      sem("acc_done"))
        f_step, f_mv, f_lv, f_rs, f_z, f_out = (sem("f_step"), sem("f_mv"), sem("f_lv"), sem("f_rs"), sem("f_z"),
                                                sem("f_out"))

        ONE = 1
        primed = (s_dts, s_b2, s_abs, s_rel, s_pre, s_dl, z_done, g_copied, p_done, x1T_kept, x1_kept, x1T_done, h_done,
                  b_free, lm2, C_done, hv_done, lg_copied, x2_kept, x2T_kept, hT_done, acc_done, s_out)

        def close_wait(engine):
            engine.sem_inc(passed, 1)

        block = ctx.enter_context(nc.Block())

        @block.sync
        def _(sp):
            for started in primed:
                sp.sem_inc(started, ONE)
            for dst, src in ((wdtw[:], W_dtw_T), (wdt[:], W_dt_T), (bdt[:], b_dt), (alog[:], A_log),
                             (wbc[:], W_BC_T), (dp[:], Dp), (lng[:], ln_g), (lnb[:], ln_b), (wout[:], W_out_T),
                             (gk[:], gate_kernel.rearrange("(s p) g -> p s g", p=P)),
                             (gbias[:], gate_bias.broadcast_to([P, 2 * H]))):
                sp.dma_start(dst, src).then_inc(ld_w, 16)
            sp.dma_start(xT[:, :], x_T).then_inc(ld_x, 16)
            sp.dma_start(xbuf[:], x_blocks[:, 0]).then_inc(ld_chunk, 16)
            sp.dma_start(cT_st[:], ctx_T[:, 0:CH]).then_inc(ld_ctx, 16)
            sp.dma_start(onorm[:], outnorm.broadcast_to([P, D])).then_inc(ld_f, 16)
            sp.dma_start(rw[:], router_w).then_inc(ld_f, 16)
            sp.dma_start(w3_sb[:], w3.rearrange("e d f -> d e f")).then_inc(ld_f, 16)

            def keep(c):
                sp.wait_ge(x1_done, c + 1)
                sp.dma_start(x1_all[:, ds(c, 1)].rearrange("p c b d -> p (c b) d"), x1_st[:]).then_inc(x1_kept, 16)
                sp.wait_ge(x1T_copied, c + 1)
                close_wait(sp)
                sp.dma_start(x1T_all[:, ds(c * CH, CH)], x1T_st[:]).then_inc(x1T_kept, 16)

            with sp.Fori(0, NCH) as c:
                sp.wait_ge(xc_done, c + 1)
                sp.dma_start(xbuf[:], x_blocks[:, ds(c, 1)].rearrange("p c b d -> p (c b) d")).then_inc(ld_chunk, 16)
                keep(c)
                sp.wait_ge(g_done, c + 1)
                sp.dma_start(cT_st[:], ctx_T[:, ds(c * CH, CH)]).then_inc(ld_ctx, 16)
            keep(NCH)
            sp.wait_ge(x1_kept, 16 * (NCH + 1) + ONE)
            sp.wait_ge(x1T_kept, 16 * (NCH + 1) + ONE)
            sp.wait_ge(g_copied, NCH + 1 + ONE)
            sp.wait_ge(m_ready, 1)
            sp.dma_start(m_dram, mrow[:]).then_inc(m_stored, 16)
            sp.wait_ge(m_stored, 16)
            sp.wait_ge(a_ready, NCH * N + 2)
            sp.dma_start(w1_sb, w1.rearrange("e d f -> d e f")).then_inc(ld_f, 16)
            m_v = m_dram.rearrange("(c n) (j s) -> j c n s", n=TB * H, j=2)
            c_blocks = ctx_tok.rearrange("(c b p) d -> p c b d", p=P, b=TB)
            with sp.Fori(0, NCH) as c:
                sp.wait_ge(b_free, c + ONE)
                close_wait(sp)
                sp.dma_start(x1c[:], x1_all[:, ds(c + 1, 1)].rearrange("p c b d -> p (c b) d")).then_inc(b_x1, 16)
                sp.dma_start(x1Tc[:], x1T_all[:, ds(c * CH + CH, CH)]).then_inc(b_x1, 16)
                sp.dma_start(cTc[:], ctx_T[:, ds(c * CH, CH)]).then_inc(b_x1, 16)
                for j in range(2):
                    sp.dma_start(hc[:].rearrange("p a (m s) -> p (a m) s", s=S)[64 * j:64 * j + 64],
                                 m_v[j, ds(c, 1)].broadcast_to([64, TB * H, S])
                                 ).then_inc(b_mb, 16)
                for b in range(TB):
                    sp.dma_start(V1[:, H * b:H * b + H, 0:S // 2],
                                 c_blocks[:, ds(c, 1), b].rearrange("p c (h e) -> p (c h) e", h=H)).then_inc(b_v, 16)
                sp.wait_ge(x2_done, c + 1)
                close_wait(sp)
                sp.dma_start(x2_all[:, ds(c * CH, CH)], x2_st[:].rearrange("p b d -> p (b d)")).then_inc(x2_kept, 16)
                sp.wait_ge(x2T_copied, c + 1)
                close_wait(sp)
                sp.dma_start(x2T_all[:, ds(c * CH, CH)], x2T_st[:]).then_inc(x2T_kept, 16)
            sp.wait_ge(b_free, NCH + ONE)
            sp.dma_start(w2_sb, w2.rearrange("e (b p) d -> p e b d", p=P)).then_inc(ld_f, 16)
            with sp.Fori(0, NCH) as c:
                sp.wait_ge(f_z, c + 1)
                close_wait(sp)
                sp.dma_start(out_blocks[:, ds(c, 1)].rearrange("p c b d -> p (c b) d"), zf[:]).then_inc(s_out, 16)
            sp.wait_ge(s_out, 16 * NCH + ONE)

        @block.gpsimd
        def _(pool):
            nc.gpsimd.memset(ident[:], 0.0).then_inc(s_memset, 1)
            nc.gpsimd.memset(sel[:], 0.0).then_inc(s_memset, 1)
            nc.gpsimd.memset(eps5[:], 1e-5).then_inc(s_const, 1)
            pool.wait_ge(s_memset, 2)
            nc.gpsimd.affine_select(out=ident[:], in_=ident[:], compare_op=ALU.not_equal, fill=1.0, base=0,
                                    pattern=[[-1, P]], channel_multiplier=1).then_inc(s_const, 1)
            for part in range(3):
                pool.wait_ge(s_const, 2 + part)
                v = sel[2 * N * part:2 * N * (part + 1), :, :]
                nc.gpsimd.affine_select(out=v, in_=v, compare_op=ALU.not_equal, fill=1.0, base=0,
                                        pattern=[[-1, 2 * N], [0, P]], channel_multiplier=1).then_inc(s_const, 1)
            pool.wait_ge(s_const, 5)
            nc.gpsimd.memset(dx[:, T:], 0.0).then_inc(s_const, 1)
            nc.gpsimd.memset(decay[:, T:], 0.0).then_inc(s_const, 1)
            pool.wait_ge(s_const, 7)
            nc.gpsimd.memset(bcs[:, T:], 0.0).then_inc(s_const, 1)
            pool.wait_ge(s_const, 8)
            nc.gpsimd.tensor_scalar(center[:], ident[:], -1.0 / D, None, ALU.add).then_inc(s_const, 1)
            pool.sem_inc(hc_done, 2)

            def residual(c):
                pool.wait_ge(ld_chunk, 16 * (c + 1))
                pool.wait_ge(z_done, c + ONE)
                pool.wait_ge(s_proj, 1)
                nc.gpsimd.tensor_tensor(xc[:], xbuf[:], cvec[:].unsqueeze(1).to_broadcast([P, TB, D]),
                                        ALU.add).then_inc(xc_done, 1)

            with pool.Fori(0, NCH) as c:
                for n in range(N):
                    k = c * N + n
                    if n == 1:
                        residual(c)
                    pool.wait_ge(h_done, k + 1 + ONE)
                    pool.wait_ge(C_copied, k + 1)
                    pool.wait_ge(y_acc, k + 1)
                    nc.gpsimd.tensor_tensor(hc[:, n % 2], h[:, n % 2], c_sb[:, n % 2], ALU.mult).then_inc(hc_done, 1)
            residual(NCH)
            pool.wait_ge(hc_done, NCH * N + 2)
            nc.gpsimd.memset(tri[:], 1.0).then_inc(g_const, 1)
            nc.gpsimd.memset(fence[:], 0.0).then_inc(g_const, 1)
            nc.gpsimd.memset(maskT[:], 0.0).then_inc(g_const, 1)
            nc.gpsimd.memset(V1[:, :, S // 2:], 1.0).then_inc(g_const, 1)
            nc.gpsimd.memset(acc[:], 0.0).then_inc(g_const, 1)
            pool.wait_ge(g_const, 5)
            nc.gpsimd.memset(fence[:, 0:P:S], -BIG).then_inc(g_const, 1)
            for e in range(E):
                nc.gpsimd.memset(rank[:, e:e + 1], float(E - e)).then_inc(g_const, 1)
            nc.gpsimd.affine_select(out=tri[:], in_=tri[:], compare_op=ALU.is_ge, fill=0.0, base=0,
                                    pattern=[[1, P]], channel_multiplier=-1).then_inc(g_const, 1)
            pool.wait_ge(g_const, 7 + E)
            nc.gpsimd.memset(tri[0:S, S:P], 0.0).then_inc(g_const, 1)
            pool.wait_ge(g_const, 8 + E)
            for j in range(2):
                nc.gpsimd.affine_select(out=maskT[S * j:S * j + S], in_=maskT[S * j:S * j + S], compare_op=ALU.is_ge,
                                        fill=-BIG, base=0, pattern=[[1, S]],
                                        channel_multiplier=-1).then_inc(g_const, 1)
                pool.wait_ge(g_const, 9 + E + j)
            v16 = [P, TB * H, S]
            with pool.Fori(0, NCH) as c:
                pool.wait_ge(b_mb, 32 * c + 32)
                pool.wait_ge(lm2, c + ONE)
                nc.gpsimd.tensor_tensor(lmask.rearrange("p (m s) -> p m s", s=S), maskT[:].unsqueeze(1).to_broadcast(v16),
                                        mb.rearrange("p (m s) -> p m s", s=S), ALU.subtract).then_inc(lm1, 1)
                pool.wait_ge(cen_done, c + 1)
                nc.gpsimd.tensor_tensor(sq[:], cen[:], cen[:], ALU.mult).then_inc(sq_done, 1)
                pool.wait_ge(sc_done, 2 * c + 1)
                nc.gpsimd.tensor_tensor(z[:], hv[:].rearrange("p (b h) e -> p b (h e)", b=TB), x1c[:],
                                        ALU.add).then_inc(zb_done, 1)

        @block.tensor
        def _(pe):
            pe.wait_ge(s_setup_pe, 1)
            nc.tensor.matmul(pq[:, 0:D], center[:], gw[:], start=True, stop=True)
            nc.tensor.matmul(pq[:, D:2 * D], lnb_rep[:], wout[:], start=True, stop=True).then_inc(s_const2, 1)
            pe.wait_ge(s_proj, 1)
            pe.wait_ge(ld_x, 16)
            with pe.Fori(0, NCH) as c:
                x_c = xT[:, ds(c * CH, CH)]
                pe.wait_ge(s_dts, c + ONE)
                close_wait(pe)
                nc.tensor.matmul(pa[0:R, 0], wdtw[:], x_c, start=True, stop=True).then_inc(s_dtp, 1)
                pe.wait_ge(s_b2, c + ONE)
                close_wait(pe)
                nc.tensor.matmul(pa[0:2 * N, 1], wbc[:], x_c, start=True, stop=True).then_inc(s_bcp, 1)
                pe.wait_ge(s_dts, c + 1 + ONE)
                pe.wait_ge(s_abs, c + ONE)
                pe.wait_ge(s_rel, c + ONE)
                nc.tensor.matmul(pB[:, 0], wdt[:], dt_sb[:], start=True, stop=True).then_inc(s_pre, 1)

            def spread(k, n, tok):
                nc.tensor.matmul(pB[:, n % 2], sel[:, n, :], bcs[:, tok], start=True, stop=True).then_inc(B_ready, 1)

            def spread_c(k, n, tok):
                nc.tensor.matmul(pC[:, n % 2], sel[:, N + n, :], bcs[:, tok], start=True, stop=True).then_inc(C_ready, 1)

            pe.wait_ge(s_b4, NCH)
            pe.wait_ge(s_pre, NCH + ONE)
            pe.wait_ge(s_rel, NCH + ONE)
            for n in range(2):
                spread(n, n, slice(0, CH))
                spread_c(n, n, slice(0, CH))

            def project(c, half):
                pe.wait_ge(y_copied, c + 1)
                if half == 1:
                    pe.wait_ge(st_done, 2 * c + 1)
                    pe.wait_ge(p_copied, 2 * c + 1)
                else:
                    pe.wait_ge(g_copied, c + ONE)
                for b in range(2):
                    last = nc.tensor.matmul(pq[:, b * 2 * D:(b + 1) * 2 * D], y_sb[:, (2 * half + b) * P:(2 * half + b + 1) * P],
                                            proj[:], start=True, stop=True)
                last.then_inc(p_done, 1)

            def transposes(c):
                pe.wait_ge(x1_done, c + 1)
                pe.wait_ge(st_done, 2 * c + 2)
                pe.wait_ge(p_copied, 2 * c + 2)
                for b in range(TB):
                    last = nc.tensor.transpose(pq[:, b * P:(b + 1) * P], x1_st[:, b], ident[:])
                last.then_inc(x1T_done, 1)

            def gate_products(c):
                pe.wait_ge(x1T_copied, c + 1)
                pe.wait_ge(ld_ctx, 16 * (c + 1))
                for b in range(TB):
                    o = pq[:, b * 2 * H:(b + 1) * 2 * H]
                    nc.tensor.matmul(o, x1T_st[:, b * P:(b + 1) * P], gk[:, 0], start=True, stop=False)
                    last = nc.tensor.matmul(o, cT_st[:, b * P:(b + 1) * P], gkv[:], start=False, stop=True)
                last.then_inc(g_done, 1)

            def tail(c, n):
                if n == 2:
                    project(c, 0)
                if n == 4:
                    project(c, 1)
                if n == 11:
                    transposes(c)
                if n == 13:
                    gate_products(c)

            with pe.Fori(0, NCH) as c:
                for n in range(N):
                    k = c * N + n
                    nxt = ds(c * CH, CH) if n < N - 2 else ds(c * CH + CH, CH)
                    m = (n + 2) % N
                    tail(c, n)
                    pe.wait_ge(u_done, k + 1)
                    spread(k + 2, m, nxt)
                    pe.wait_ge(C_copied, k + 1)
                    spread_c(k + 2, m, nxt)
                    pe.wait_ge(hc_done, k + 3)
                    if n == 0:
                        pe.wait_ge(y_copied, c + 1)
                        nc.tensor.matmul(py[:], diag_dp[:], xT[:, ds(c * CH, CH)], start=True, stop=False)
                    nc.tensor.matmul(py[:], ident[:], hc[:, n % 2], start=False, stop=(n == N - 1)).then_inc(y_acc, 1)
            for n in range(N):
                tail(NCH, n)
            pe.wait_ge(gate_step, 1)
            pe.wait_ge(g_const, 10 + E)
            nc.tensor.matmul(pq[:, 0:NG], tri[:], lfg[:], start=True, stop=True).then_inc(gate_step, 1)
            pe.wait_ge(gate_step, 3)
            nc.tensor.transpose(pC[:, 0, 0:P], g_sb[:], ident[:]).then_inc(gate_step, 1)
            pe.wait_ge(gate_step, 5)
            nc.tensor.transpose(pC[:, 1, 0:P], mrow[:], ident[:]).then_inc(gate_step, 1)
            pe.wait_ge(E_ready, 1)
            HD = D // H
            with pe.Fori(0, NCH) as c:
                pe.wait_ge(b_x1, 48 * c + 48)
                pe.wait_ge(C_done, c + ONE)
                for hh in range(H):
                    bank = (pa if hh < 2 else pB)[:, hh % 2]
                    rows = slice(HD * hh, HD * hh + HD)
                    for b in range(TB):
                        for j in range(2):
                            t0 = b * P + S * j
                            last = nc.tensor.matmul(bank[S * j:S * j + S, b * S:b * S + S], cTc[rows, t0:t0 + S],
                                                    x1Tc[rows, t0:t0 + S], start=True, stop=True)
                last.then_inc(qk_done, 1)
                pe.wait_ge(C_done, c + 1 + ONE)
                pe.wait_ge(b_v, 16 * TB * (c + 1))
                pe.wait_ge(hv_done, c + ONE)
                close_wait(pe)
                for b in range(TB):
                    for j in range(2):
                        for hh in range(H):
                            m = b * H + hh
                            last = nc.tensor.matmul(pC[S * j:S * j + S, b // 2, ((b % 2) * H + hh) * (HD + 1):((b % 2) * H + hh + 1) * (HD + 1)],
                                                    Cm[S * j:S * j + S, m * S:m * S + S], V1[S * j:S * j + S, m],
                                                    start=True, stop=True)
                last.then_inc(av_done, 1)
                pe.wait_ge(x2_done, c + 1)
                pe.wait_ge(lg_copied, c + ONE)
                for b in range(TB):
                    last = nc.tensor.transpose(pq[:, b * P:(b + 1) * P], x2_st[:, b], ident[:])
                last.then_inc(x2T_done, 1)
                pe.wait_ge(x2T_copied, c + 1)
                for b in range(TB):
                    last = nc.tensor.matmul(py[:, b * E:(b + 1) * E], x2T_st[:, b * P:(b + 1) * P], rw[:], start=True,
                                            stop=True)
                last.then_inc(lg_done, 1)
            pe.wait_ge(x2T_kept, 16 * NCH + ONE)
            pe.wait_ge(ld_f, 80)
            pe.wait_ge(r_step, 100)
            NU = E * FB
            with pe.Fori(0, NCH) as c:
                x_c = x2T_all[:, ds(c * CH, CH)]

                def down(e):
                    pe.wait_ge(hT_done, c * NU + (e + 1) * FB)
                    pe.wait_ge(acc_done, c * E + e - 1 + ONE + 1)
                    for b in range(TB):
                        for f in range(FB):
                            last = nc.tensor.matmul((pC, pC)[0][:, e % 2, b * D:(b + 1) * D], hT[:, e % 2, f, b * P:(b + 1) * P],
                                                    w2_sb[:, e, f], start=(f == 0), stop=(f == FB - 1))
                    last.then_inc(dn_done, 1)

                for e in range(E):
                    for f in range(FB):
                        i = e * FB + f
                        pe.wait_ge(hT_done, c * NU + i - 1 + ONE + 1)
                        close_wait(pe)
                        nc.tensor.matmul(pa[:, i % 2], w1_sb[:, e, f * P:(f + 1) * P], x_c, start=True, stop=True)
                        nc.tensor.matmul(pB[:, i % 2], w3_sb[:, e, f * P:(f + 1) * P], x_c, start=True,
                                         stop=True).then_inc(h_up, 1)
                    if e > 0:
                        down(e - 1)
                down(E - 1)

        @block.scalar
        def _(act):
            nc.scalar.preload_act_table_set("natural_log_exp_and_others")
            act.wait_ge(ld_w, 16 * 11)
            nc.scalar.activation(Aneg[:], alog[:], ACT.Exp).then_inc(s_aexp, 1)
            with act.Fori(0, NCH) as c:
                act.wait_ge(s_dtp, c + 1)
                act.wait_ge(s_pre, c + ONE)
                nc.scalar.copy(dt_sb[:], pa[0:R, 0]).then_inc(s_dts, 1)
                act.wait_ge(s_rel, c + 1 + ONE)
                nc.scalar.activation(pabs, pB[:, 0], ACT.Abs, bias=bdt[:]).then_inc(s_abs, 1)
                act.wait_ge(s_abs, c + 1 + ONE)
                nc.scalar.activation(pexp, pabs, ACT.Exp, scale=-1.0).then_inc(s_ex, 1)
                act.wait_ge(s_ex, c + 1)
                act.wait_ge(s_dl, c + ONE)
                nc.scalar.activation(plog, pexp, ACT.Ln, bias=1.0).then_inc(s_log, 1)

            def decay_exp(n, tok):
                close_wait(act)
                nc.scalar.activation(pa[:, n % 2], decay[:, tok], ACT.Exp, scale=Aneg[:, n:n + 1]).then_inc(a_ready, 1)

            def copy_c(n):
                nc.scalar.copy(c_sb[:, n % 2], pC[:, n % 2]).then_inc(C_copied, 1)

            act.wait_ge(s_dec, NCH)
            act.wait_ge(s_A, 2)
            act.wait_ge(s_b2, NCH + ONE)
            for n in range(2):
                decay_exp(n, slice(0, CH))
                act.wait_ge(C_ready, n + 1)
                copy_c(n)

            def tail(c, n):
                if n == 1:
                    act.wait_ge(y_acc, c * N + 2)
                    act.wait_ge(p_done, 2 * c + ONE)
                    nc.scalar.copy(y_sb[:], py[:]).then_inc(y_copied, 1)
                if n in (3, 5):
                    half = (n - 3) // 2
                    act.wait_ge(p_done, 2 * c + half + 1 + ONE)
                    act.wait_ge(z_done, c + ONE)
                    act.wait_ge(st_done, 2 * c + half + 1)
                    nc.scalar.copy(p_sb[:, 2 * half:2 * half + 2], pq[:].rearrange("p (b e) -> p b e", b=2)[:, :, 0:D]
                                   ).then_inc(p_copied, 1)
                if n == 7:
                    act.wait_ge(mv_done, c + 1)
                    act.wait_ge(z_done, c + ONE)
                    nc.scalar.activation(lv[:], mv[:, :, 1], ACT.Ln, bias=eps5[:]).then_inc(lv_done, 1)
                    act.wait_ge(lv_done, c + 1)
                    nc.scalar.activation(rstd[:], lv[:], ACT.Exp, scale=-0.5).then_inc(rs_done, 1)
                if n == 10:
                    act.wait_ge(mv2_done, c + 1)
                    nc.scalar.activation(lv2[:], mv2[:, :, 1], ACT.Ln, bias=eps5[:]).then_inc(lv2_done, 1)
                    act.wait_ge(lv2_done, c + 1)
                    nc.scalar.activation(rstd2[:], lv2[:], ACT.Exp, scale=-0.5).then_inc(rs2_done, 1)
                if n == 12:
                    act.wait_ge(x1T_done, c + 1 + ONE)
                    act.wait_ge(x1T_kept, 16 * c + ONE)
                    nc.scalar.copy(x1T_st[:], pq[:]).then_inc(x1T_copied, 1)

            with act.Fori(0, NCH) as c:
                for n in range(N):
                    k = c * N + n
                    nxt = ds(c * CH, CH) if n < N - 2 else ds(c * CH + CH, CH)
                    tail(c, n)
                    act.wait_ge(h_done, k + 1 + ONE)
                    decay_exp((n + 2) % N, nxt)
                    act.wait_ge(C_ready, k + 3)
                    act.wait_ge(hc_done, k + 3)
                    copy_c((n + 2) % N)
            for n in range(N):
                tail(NCH, n)
            act.wait_ge(g_copied, NCH + 1 + ONE)
            fg = gates[:, 1:].rearrange("p c b g -> p (c b) g")[:, :, H:2 * H]
            v3 = "p (n h) -> p n h"
            nc.scalar.activation(gabs[:].rearrange(v3, h=H), fg, ACT.Abs).then_inc(act_step, 1)
            act.wait_ge(act_step, 1)
            nc.scalar.activation(gexp[:], gabs[:], ACT.Exp, scale=-1.0).then_inc(act_step, 1)
            act.wait_ge(act_step, 2)
            nc.scalar.activation(glog[:], gexp[:], ACT.Ln, bias=1.0).then_inc(act_step, 1)
            act.wait_ge(gate_step, 7)
            nc.scalar.activation(floor_[:], nlog[:], ACT.Exp, scale=-1.0).then_inc(E_ready, 1)
            with act.Fori(0, NCH) as c:
                act.wait_ge(lm2, c + 1 + ONE)
                act.wait_ge(C_done, c + ONE)
                nc.scalar.activation(Dm, lmask, ACT.Exp).then_inc(D_done, 1)
                act.wait_ge(vsum_done, c + 1)
                nc.scalar.activation(vlog[:], vsum[:], ACT.Ln, scale=float(H) / D, bias=eps5[:]).then_inc(vlog_done, 1)
                act.wait_ge(vlog_done, c + 1)
                nc.scalar.activation(vrs[:], vlog[:], ACT.Exp, scale=-0.5).then_inc(vrs_done, 1)
                act.wait_ge(mvb_done, c + 1)
                nc.scalar.activation(lv[:], mv[:, :, 1], ACT.Ln, bias=eps5[:]).then_inc(lvb_done, 1)
                act.wait_ge(lvb_done, c + 1)
                nc.scalar.activation(rstd[:], lv[:], ACT.Exp, scale=-0.5).then_inc(rsb_done, 1)
                act.wait_ge(x2T_done, c + 1)
                act.wait_ge(x2T_kept, 16 * c + ONE)
                nc.scalar.copy(x2T_st[:], pq[:]).then_inc(x2T_copied, 1)
            act.wait_ge(r_step, 50)
            nc.scalar.activation(share[:, 1], share[:, 0], ACT.Exp).then_inc(r_exp, 1)
            with act.Fori(0, NCH) as c:
                for e in range(E):
                    for f in range(FB):
                        i = e * FB + f
                        act.wait_ge(h_up, c * E * FB + i + 1)
                        act.wait_ge(hT_done, c * E * FB + i - 1 + ONE + 1)
                        nc.scalar.activation(sil[:, i % 2], pa[:, i % 2], ACT.Silu).then_inc(sil_done, 1)
                act.wait_ge(f_mv, c + 1)
                nc.scalar.activation(lv2[:], lv[:], ACT.Sqrt).then_inc(f_rs, 1)

        @block.vector
        def _(dve):
            dve.wait_ge(ld_w, 16 * 11)
            dve.wait_ge(s_const, 9)
            nc.vector.memset(py[:], 0.0).then_inc(y_acc, 2)
            nc.vector.tensor_scalar(gw[:], wout[:], lng[:], None, ALU.mult)
            nc.vector.tensor_copy(lnb_rep[:], lnb[:].to_broadcast([D, P]))
            nc.vector.tensor_scalar(diag_dp[:], ident[:], dp[:], None, ALU.mult)
            nc.vector.tensor_copy(proj[:, D:2 * D], ident[:])
            nc.vector.tensor_tensor(gkv[:], gk[:, 1], gk[:, 2], ALU.add).then_inc(s_setup_pe, 1)
            dve.wait_ge(s_aexp, 1)
            nc.vector.tensor_scalar(Aneg[:], Aneg[:], -1.0, -1e-27, ALU.mult, ALU.min).then_inc(s_A, 2)
            dve.wait_ge(s_const2, 1)
            nc.vector.tensor_copy(proj[:, 0:D], pq[:, 0:D])
            nc.vector.tensor_copy(cvec[:], pq[:, D:2 * D]).then_inc(s_proj, 1)
            dve.wait_ge(ld_x, 16)
            with dve.Fori(0, NCH) as c:
                tok = ds(c * CH, CH)
                dve.wait_ge(s_bcp, c + 1)
                close_wait(dve)
                nc.vector.tensor_copy(bcs[0:32, tok], pa[0:2 * N, 1]).then_inc(s_b1, 1)
                dve.wait_ge(s_pre, c + 1 + ONE)
                nc.vector.tensor_scalar(prel, pB[:, 0], bdt[:], 0.0, ALU.add, ALU.max).then_inc(s_rel, 1)
                dve.wait_ge(s_b1, c + 1)
                nc.vector.tensor_tensor(res1[:], pa[0:2 * N, 1], bcs[0:32, tok], ALU.subtract).then_inc(s_b2, 1)
                dve.wait_ge(s_rel, c + 1 + ONE)
                dve.wait_ge(s_log, c + 1)
                nc.vector.tensor_tensor(delta, prel, plog, ALU.add).then_inc(s_dl, 1)
                dve.wait_ge(s_b2, c + 1 + ONE)
                close_wait(dve)
                nc.vector.tensor_copy(bcs[32:64, tok], res1[:]).then_inc(s_b3, 1)
                dve.wait_ge(s_dl, c + 1 + ONE)
                nc.vector.tensor_tensor(dx[:, tok], delta, xT[:, tok], ALU.mult).then_inc(s_dx, 1)
                dve.wait_ge(s_b3, c + 1)
                close_wait(dve)
                nc.vector.tensor_copy(bc32[:], bcs[32:64, tok]).then_inc(s_bc, 1)
                dve.wait_ge(s_dx, c + 1)
                nc.vector.memset(delta.rearrange("p (b s) -> p b s", s=S)[:, :, 0:1], BIG).then_inc(s_reset, 1)
                dve.wait_ge(s_reset, c + 1)
                close_wait(dve)
                nc.vector.tensor_copy(decay[:, tok], delta).then_inc(s_dec, 1)
                dve.wait_ge(s_bc, c + 1)
                nc.vector.tensor_tensor(bcs[64:96, tok], res1[:], bc32[:], ALU.subtract).then_inc(s_b4, 1)

            def product(n, tok):
                nc.vector.tensor_tensor(u[:, n % 2], dx[:, tok], pB[:, n % 2], ALU.mult).then_inc(u_done, 1)

            dve.wait_ge(s_dx, NCH)
            dve.wait_ge(B_ready, 1)
            product(0, slice(0, CH))

            def stats(src, dst, sems, value, blocks):
                for b in blocks:
                    last = nc.vector.bn_stats(dst[:, b], src(b))
                last.then_inc(sems, 1)
                dve.wait_ge(sems, value)
                close_wait(dve)

            def tail(c, n):
                if n in (3, 5):
                    half = (n - 3) // 2
                    dve.wait_ge(p_done, 2 * c + half + 1 + ONE)
                    stats(lambda b: pq[:, (b % 2) * 2 * D + D:(b % 2) * 2 * D + 2 * D], st, st_done, 2 * c + half + 1,
                          (2 * half, 2 * half + 1))
                if n == 6:
                    for b in range(TB):
                        last = nc.vector.bn_aggr(mv[:, b], st[:, b])
                    last.then_inc(mv_done, 1)
                if n == 8:
                    dve.wait_ge(rs_done, c + 1)
                    dve.wait_ge(p_copied, 2 * c + 2)
                    dve.wait_ge(xc_done, c + 1)
                    for b in range(TB):
                        last = nc.vector.scalar_tensor_tensor(z[:, b], p_sb[:, b], rstd[:, b:b + 1], xc[:, b],
                                                              ALU.mult, ALU.add)
                    last.then_inc(z_done, 1)
                if n == 9:
                    dve.wait_ge(z_done, c + 1 + ONE)
                    stats(lambda b: z[:, b], st2, st2_done, c + 1, range(TB))
                    for b in range(TB):
                        last = nc.vector.bn_aggr(mv2[:, b], st2[:, b])
                    last.then_inc(mv2_done, 1)
                if n == 11:
                    dve.wait_ge(rs2_done, c + 1)
                    dve.wait_ge(x1_kept, 16 * c + ONE)
                    dve.wait_ge(x1T_done, c + ONE)
                    for b in range(TB):
                        last = nc.vector.tensor_scalar(x1_st[:, b], z[:, b], mv2[:, b, 0:1], rstd2[:, b:b + 1],
                                                       ALU.subtract, ALU.mult)
                    last.then_inc(x1_done, 1)
                if n == 14:
                    dve.wait_ge(g_done, c + 1)
                    nc.vector.tensor_tensor(gates[:, ds(c, 1)].rearrange("p c b g -> p (c b) g"),
                                            pq[:, 0:TB * 2 * H].rearrange("p (b g) -> p b g", b=TB),
                                            gbias[:].unsqueeze(1).to_broadcast([P, TB, 2 * H]),
                                            ALU.add).then_inc(g_copied, 1)

            with dve.Fori(0, NCH) as c:
                for n in range(N):
                    k = c * N + n
                    nxt = ds(c * CH, CH) if n < N - 1 else ds(c * CH + CH, CH)
                    tail(c, n)
                    dve.wait_ge(B_ready, k + 2)
                    dve.wait_ge(h_done, k + ONE)
                    product((n + 1) % N, nxt)
                    dve.wait_ge(a_ready, k + 1)
                    dve.wait_ge(u_done, k + 1)
                    dve.wait_ge(hc_done, k + 1)
                    nc.vector.tensor_tensor_scan(h[:, n % 2], pa[:, n % 2], u[:, n % 2], 0.0, ALU.mult,
                                                 ALU.add).then_inc(h_done, 1)
            for n in range(N):
                tail(NCH, n)
            v3 = "p (n h) -> p n h"
            gv = gates[:, 1:].rearrange("p c b g -> p (c b) g")
            dve.wait_ge(g_copied, NCH + 1 + ONE)
            dve.wait_ge(act_step, 3)
            nc.vector.scalar_tensor_tensor(lfg[:].rearrange(v3, h=H), gv[:, :, H:2 * H], 0.0, glog[:].rearrange(v3, h=H),
                                           ALU.min, ALU.subtract).then_inc(gate_step, 1)
            dve.wait_ge(gate_step, 2)
            nc.vector.tensor_copy(cs_sb[:], pq[:, 0:NG])
            nc.vector.tensor_tensor(g_sb[:].rearrange(v3, h=H), gv[:, :, 0:H], pq[:, 0:NG].rearrange(v3, h=H),
                                    ALU.subtract).then_inc(gate_step, 1)
            dve.wait_ge(gate_step, 4)
            nc.vector.tensor_tensor_scan(mrow[:], fence[:], pC[:, 0, 0:P], 0.0, ALU.add, ALU.max).then_inc(gate_step, 1)
            dve.wait_ge(gate_step, 5)
            nc.vector.engine_nop().then_inc(m_ready, 1)
            dve.wait_ge(gate_step, 6)
            nc.vector.tensor_tensor(nlog[:], cs_sb[:], pC[:, 1, 0:NG], ALU.add).then_inc(gate_step, 1)
            dve.wait_ge(E_ready, 1)
            HD = D // H
            M = TB * H
            NSTEP = 6
            with dve.Fori(0, NCH) as c:
                dve.wait_ge(lm1, c + 1)
                g_c = g_sb[:, ds(c * M, M)].unsqueeze(2).to_broadcast([P, M, S])
                lm = lmask.rearrange("p (m s) -> p m s", s=S)
                close_wait(dve)
                nc.vector.tensor_tensor(lm, lm, g_c, ALU.add).then_inc(lm2, 1)
                dve.wait_ge(D_done, c + 1)
                dve.wait_ge(qk_done, c + 1)
                scale = float(HD) ** -0.5
                for hh in range(H):
                    bank = (pa if hh < 2 else pB)[:, hh % 2, 0:TB * S].rearrange("p (b s) -> p b s", s=S)
                    pick = lambda v: v.rearrange("p (b h s) -> p h b s", h=H, s=S)[:, hh]
                    last = nc.vector.scalar_tensor_tensor(pick(Cm), bank, scale, pick(Dm), ALU.mult, ALU.mult)
                last.then_inc(C_done, 1)
                dve.wait_ge(av_done, c + 1)
                pav = pC[:, :, 0:(M // 2) * (HD + 1)].rearrange("p a (m e) -> p a m e", e=HD + 1)
                two = lambda v: v.rearrange("p (a m) -> p a m", a=2)
                s0 = c * NSTEP
                close_wait(dve)
                nc.vector.tensor_tensor(two(rs[:]), pav[:, :, :, HD], two(floor_[:, ds(c * M, M)]),
                                        ALU.max).then_inc(n_step, 1)
                dve.wait_ge(n_step, s0 + 1)
                nc.vector.scalar_tensor_tensor(two(rs[:]), pav[:, :, :, HD], -1.0, two(rs[:]),
                                               ALU.mult, ALU.max).then_inc(n_step, 1)
                dve.wait_ge(n_step, s0 + 2)
                nc.vector.tensor_scalar(rs[:], rs[:], 1e-6, None, ALU.add).then_inc(n_step, 1)
                dve.wait_ge(n_step, s0 + 3)
                nc.vector.reciprocal(rinv[:], rs[:]).then_inc(n_step, 1)
                dve.wait_ge(n_step, s0 + 4)
                nc.vector.tensor_tensor(hv[:].rearrange("p (a m) e -> p a m e", a=2), pav[:, :, :, 0:HD],
                                        two(rinv[:]).unsqueeze(3).to_broadcast([P, 2, M // 2, HD]),
                                        ALU.mult).then_inc(hv_done, 1)
                dve.wait_ge(hv_done, c + 1 + ONE)
                nc.vector.tensor_reduce(hsum[:], hv[:], AX.X, ALU.add).then_inc(n_step, 1)
                dve.wait_ge(n_step, s0 + 5)
                nc.vector.scalar_tensor_tensor(cen[:], hsum[:].unsqueeze(2).to_broadcast([P, M, HD]), -1.0 / HD, hv[:],
                                               ALU.mult, ALU.add).then_inc(cen_done, 1)
                dve.wait_ge(sq_done, c + 1)
                nc.vector.tensor_reduce(vsum[:], sq[:], AX.X, ALU.add).then_inc(vsum_done, 1)
                dve.wait_ge(vrs_done, c + 1)
                nc.vector.tensor_tensor(cen[:], cen[:], vrs[:].unsqueeze(2).to_broadcast([P, M, HD]),
                                        ALU.mult).then_inc(n_step, 1)
                dve.wait_ge(n_step, s0 + 6)
                nc.vector.tensor_tensor(hv[:].rearrange("p (b h) e -> p b (h e)", b=TB),
                                        cen[:].rearrange("p (b h) e -> p b (h e)", b=TB),
                                        onorm[:].unsqueeze(1).to_broadcast([P, TB, D]), ALU.mult).then_inc(sc_done, 2)
                dve.wait_ge(zb_done, c + 1)
                for b in range(TB):
                    last = nc.vector.bn_stats(st[:, b], z[:, b])
                last.then_inc(stb_done, 1)
                dve.wait_ge(stb_done, c + 1)
                close_wait(dve)
                for b in range(TB):
                    last = nc.vector.bn_aggr(mv[:, b], st[:, b])
                last.then_inc(mvb_done, 1)
                dve.wait_ge(rsb_done, c + 1)
                dve.wait_ge(x2_kept, 16 * c + ONE)
                for b in range(TB):
                    last = nc.vector.tensor_scalar(x2_st[:, b], z[:, b], mv[:, b, 0:1], rstd[:, b:b + 1],
                                                   ALU.subtract, ALU.mult)
                last.then_inc(x2_done, 1)
                dve.wait_ge(lg_done, c + 1)
                close_wait(dve)
                nc.vector.tensor_copy(logits[:, ds(c, 1)].rearrange("p c b e -> p (c b e)"), py[:, 0:TB * E]
                                      ).then_inc(lg_copied, 1)
                dve.wait_ge(lg_copied, c + 1 + ONE)
                dve.sem_inc(b_free, 1)
            step = [0]

            def link(ins):
                step[0] += 1
                ins.then_inc(r_step, 1)
                dve.wait_ge(r_step, step[0])

            wide = [P, NT, E]
            lg = logits[:].rearrange("p c b e -> p (c b) e")
            dve.wait_ge(lg_copied, NCH + ONE)
            src = lg
            for i in range(2):
                link(nc.vector.tensor_reduce(top[:, i], src, AX.X, ALU.max))
                link(nc.vector.tensor_tensor(tie[:], src, top[:, i].unsqueeze(2).to_broadcast(wide), ALU.is_equal))
                link(nc.vector.tensor_tensor(tie[:], tie[:], rank[:].unsqueeze(1).to_broadcast(wide), ALU.mult))
                link(nc.vector.tensor_reduce(tmax[:], tie[:], AX.X, ALU.max))
                link(nc.vector.tensor_tensor(hot[:, i], tie[:], tmax[:].unsqueeze(2).to_broadcast(wide), ALU.is_equal))
                if i == 0:
                    link(nc.vector.scalar_tensor_tensor(rest[:], hot[:, 0], -BIG, lg, ALU.mult, ALU.add))
                    src = rest[:]
            link(nc.vector.tensor_tensor(share[:, 0], top[:, 1], top[:, 0], ALU.subtract))
            ready = 50 - step[0]
            dve.sem_inc(r_step, ready)
            dve.wait_ge(r_exp, 1)
            step[0] = 50
            link(nc.vector.tensor_scalar(tmax[:], share[:, 1], 1.0, None, ALU.add))
            link(nc.vector.reciprocal(share[:, 0], tmax[:]))
            link(nc.vector.tensor_tensor(share[:, 1], share[:, 1], share[:, 0], ALU.mult))
            for i in range(2):
                link(nc.vector.tensor_tensor(hot[:, i], hot[:, i], share[:, i].unsqueeze(2).to_broadcast(wide), ALU.mult))
            link(nc.vector.tensor_tensor(wi[:].rearrange("p c b e -> p (c b) e"), hot[:, 0], hot[:, 1], ALU.add))
            dve.sem_inc(r_step, 100 - step[0])
            with dve.Fori(0, NCH) as c:
                def gather(e):
                    dve.wait_ge(dn_done, c * E + e + 1)
                    dve.wait_ge(acc_done, c * E + e + ONE)
                    close_wait(dve)
                    for b in range(TB):
                        src = x2_all[:, ds(c * CH + b * D, D)] if e == 0 else acc[:, b]
                        last = nc.vector.scalar_tensor_tensor(acc[:, b], pC[:, e % 2, b * D:(b + 1) * D],
                                                              wi[:, ds(c, 1), b, e:e + 1].rearrange("p c e -> p (c e)"), src, ALU.mult, ALU.add)
                    last.then_inc(acc_done, 1)

                for e in range(E):
                    for f in range(FB):
                        i = e * FB + f
                        dve.wait_ge(sil_done, c * E * FB + i + 1)
                        if e >= 2 or True:
                            dve.wait_ge(dn_done, c * E + e - 1) if e >= 1 else None
                        nc.vector.tensor_tensor(hT[:, e % 2, f], sil[:, i % 2], pB[:, i % 2], ALU.mult).then_inc(hT_done, 1)
                    if e > 0:
                        gather(e - 1)
                gather(E - 1)
                dve.wait_ge(acc_done, c * E + E + ONE)
                for b in range(TB):
                    last = nc.vector.bn_stats(st[:, b], acc[:, b])
                last.then_inc(f_step, 1)
                dve.wait_ge(f_step, 3 * c + 1)
                close_wait(dve)
                for b in range(TB):
                    last = nc.vector.bn_aggr(mv[:, b], st[:, b])
                last.then_inc(f_step, 1)
                dve.wait_ge(f_step, 3 * c + 2)
                nc.vector.tensor_scalar(lv[:], mv[:, :, 1], 1e-5, None, ALU.add).then_inc(f_mv, 1)
                dve.wait_ge(f_rs, c + 1)
                nc.vector.reciprocal(rstd[:], lv2[:]).then_inc(f_step, 1)
                dve.wait_ge(f_step, 3 * c + 3)
                dve.wait_ge(s_out, 16 * c + ONE)
                for b in range(TB):
                    last = nc.vector.tensor_scalar(zf[:, b], acc[:, b], mv[:, b, 0:1], rstd[:, b:b + 1],
                                                   ALU.subtract, ALU.mult)
                last.then_inc(f_z, 1)


_LAYOUT = [
    ("x_tok", lambda i: i["x"].reshape(4096, 128)),
    ("x_T", lambda i: i["x"].reshape(4096, 128).T),
    ("ctx_tok", lambda i: i["ctx_1024"].reshape(4096, 128)),
    ("ctx_T", lambda i: i["ctx_1024"].reshape(4096, 128).T),
    ("W_dtw_T", lambda i: i["L0_attn_W_dtw"].T),
    ("W_dt_T", lambda i: i["L0_attn_W_dt"].T),
    ("b_dt", lambda i: i["L0_attn_b_dt"][:, None]),
    ("A_log", lambda i: i["L0_attn_A_log"]),
    ("W_BC_T", "bc"),
    ("Dp", lambda i: i["L0_attn_Dp"][:, None]),
    ("ln_g", lambda i: i["L0_attn_ln_g"][:, None]),
    ("ln_b", lambda i: i["L0_attn_ln_b"][:, None]),
    ("W_out_T", lambda i: i["L0_attn_W_out"].T),
    ("gate_kernel", "gk"),
    ("gate_bias", "gb"),
    ("outnorm", lambda i: i["L0_xattn_outnorm_scale"][None, :]),
    ("router_w", lambda i: i["L0_ffn_gate_w"]),
    ("w1", lambda i: i["L0_ffn_w1"]),
    ("w3", lambda i: i["L0_ffn_w3"]),
    ("w2", lambda i: i["L0_ffn_w2"]),
]


def kernel(**inputs):
    import numpy as np
    import concourse.bacc as bacc
    from concourse.bass_utils import run_bass_kernel_spmd

    i = {k: np.asarray(v) for k, v in inputs.items()}
    joined = {
        "bc": lambda: np.concatenate([i["L0_attn_W_B"].T, i["L0_attn_W_C"].T], axis=1),
        "gk": lambda: np.concatenate([i["L0_xattn_igate_kernel"], i["L0_xattn_fgate_kernel"]], axis=1),
        "gb": lambda: np.concatenate([i["L0_xattn_igate_bias"], i["L0_xattn_fgate_bias"]])[None, :],
    }
    nc = bacc.Bacc("TRN2", target_bir_lowering=False, num_devices=1)
    arrays, args = {}, []
    for name, make in _LAYOUT:
        a = np.ascontiguousarray(joined[make]() if isinstance(make, str) else make(i))
        arrays[f"in_{name}"] = a
        args.append(nc.dram_tensor(f"in_{name}", a.shape, mybir.dt.from_np(a.dtype), kind="ExternalInput").ap())
    args.append(nc.dram_tensor("out_0", (4096, 128), mybir.dt.float32, kind="ExternalOutput").ap())
    decoder_layer(nc, *args)
    r = run_bass_kernel_spmd(nc, [arrays], core_ids=[0])
    return r.results[0]["out_0"].reshape(64, 64, 128)
```

```python
import concourse.bass as bass
from concourse import mybir
from contextlib import ExitStack


def decoder_layer(nc, x_tok, x_T, ctx_tok, ctx_T, W_dtw_T, W_dt_T, b_dt, A_log, W_BC_T, Dp, ln_g, ln_b, W_out_T,
                  gate_kernel, gate_bias, outnorm, router_w, w1, w3, w2, out):
    f32, bf16, i32 = mybir.dt.float32, mybir.dt.bfloat16, mybir.dt.int32
    ALU, ACT, AX = mybir.AluOpType, mybir.ActivationFunctionType, mybir.AxisListType
    ds = bass.ds
    P = 128
    D, T = x_T.shape
    S = 64
    N = A_log.shape[1]
    R = W_dtw_T.shape[1]
    CH = 512
    NCH = T // CH
    TB = CH // P
    H = 4
    NT = T // P
    BIG = 1.0e30

    ctx = ExitStack()
    with ctx:
        def sb(name, shape, dt=f32):
            return ctx.enter_context(nc.sbuf_tensor(name, shape, dt))

        def pb(name, shape):
            return ctx.enter_context(nc.psum_tensor(name, shape, f32))

        def sem(name):
            return ctx.enter_context(nc.semaphore(name))

        wdtw = sb("wdtw", [D, R])
        wdt = sb("wdt", [R, D])
        bdt = sb("bdt", [D, 1])
        alog = sb("alog", [D, N])
        Aneg = sb("Aneg", [D, N])
        wbc = sb("wbc", [D, 2 * N])
        dp = sb("dp", [D, 1])
        lng = sb("lng", [D, 1])
        lnb = sb("lnb", [D, 1])
        wout = sb("wout", [D, D])
        gk = sb("gk", [P, 3, 2 * H])
        gkv = sb("gkv", [P, 2 * H])
        gbias = sb("gbias", [P, 2 * H])
        ident = sb("ident", [P, P])
        center = sb("center", [P, P])
        gw = sb("gw", [D, D])
        lnb_rep = sb("lnb_rep", [D, P])
        diag_dp = sb("diag_dp", [D, D])
        proj = sb("proj", [D, 2 * D])
        cvec = sb("cvec", [P, D])
        sel = sb("sel", [96, 2 * N, P], bf16)
        eps5 = sb("eps5", [P, 1])
        PAD = CH
        xT = sb("xT", [D, T])
        dx = sb("dx", [D, T + PAD])
        decay = sb("decay", [D, T + PAD])
        bcs = sb("bcs", [96, T + PAD], bf16)
        dt_sb = sb("dt_sb", [R, CH])
        bc32 = sb("bc32", [2 * N, CH])
        res1 = sb("res1", [2 * N, CH])
        u = sb("u", [D, 2, CH])
        h = sb("h", [D, 2, CH])
        c_sb = sb("c_sb", [D, 2, CH])
        hc = sb("hc", [D, 2, CH])
        y_sb = sb("y_sb", [D, CH])
        p_sb = sb("p_sb", [P, TB, D])
        xbuf = sb("xbuf", [P, TB, D])
        xc = sb("xc", [P, TB, D])
        z = sb("z", [P, TB, D])
        st = sb("st", [P, TB, 6])
        mv = sb("mv", [P, TB, 2])
        lv = sb("lv", [P, TB])
        rstd = sb("rstd", [P, TB])
        st2 = sb("st2", [P, TB, 6])
        mv2 = sb("mv2", [P, TB, 2])
        lv2 = sb("lv2", [P, TB])
        rstd2 = sb("rstd2", [P, TB])
        x1_st = sb("x1_st", [P, TB, D])
        x1T_st = sb("x1T_st", [D, CH])
        cT_st = sb("cT_st", [D, CH])
        x1_all = sb("x1_all", [P, NCH + 1, TB, D])
        x1T_all = sb("x1T_all", [D, T + PAD])
        gates = sb("gates", [P, NCH + 1, TB, 2 * H])

        NG = NT * H
        gabs = sb("gabs", [P, NG])
        gexp = sb("gexp", [P, NG])
        glog = sb("glog", [P, NG])
        lfg = sb("lfg", [P, NG])
        tri = sb("tri", [P, P])
        cs_sb = sb("cs_sb", [P, NG])
        g_sb = sb("g_sb", [P, NG])
        fence = sb("fence", [P, P])
        mrow = sb("mrow", [P, P])
        nlog = sb("nlog", [P, NG])
        floor_ = sb("floor_", [P, NG])
        maskT = sb("maskT", [P, S])
        onorm = sb("onorm", [P, D])
        x1c = sb("x1c", [P, TB, D])
        x1Tc = sb("x1Tc", [D, CH])
        cTc = sb("cTc", [D, CH])
        V1 = sb("V1", [P, TB * H, S // 2 + 1])
        lmask, Dm, Cm, mb = (v[:].rearrange("p a c -> p (a c)") for v in (u, h, c_sb, hc))
        rs = sb("rs", [P, TB * H])
        rinv = sb("rinv", [P, TB * H])
        hsum = sb("hsum", [P, TB * H])
        vsum = sb("vsum", [P, TB * H])
        vlog = sb("vlog", [P, TB * H])
        vrs = sb("vrs", [P, TB * H])
        hv = sb("hv", [P, TB * H, S // 2])
        cen = sb("cen", [P, TB * H, S // 2])
        sq = sb("sq", [P, TB * H, S // 2])
        flat3 = lambda v: v[:].rearrange("p a b -> p (a b)")
        pabs, pexp, plog, prel = flat3(hv), flat3(cen), flat3(sq), flat3(x1c)
        delta = x1Tc[:]
        E, F = w1.shape[0], w1.shape[2]
        FB = F // P
        K2 = 2
        REG = T + P
        NTIL = K2 * T // P + E
        NTAB = NTIL + 1
        SPARE = NTAB - K2 * T // P
        ROW = D + 2
        x2r = sb("x2r", [P, K2, TB, ROW])
        x2T_st = sb("x2T_st", [D, CH])
        rw = sb("rw", [D, E])
        w1_sb = decay[:, 0:E * F].rearrange("p (e f) -> p e f", e=E)
        w3_sb = sb("w3_sb", [D, E, F])
        w2_sb = x1T_all[:, 0:E * F].rearrange("p (e f d) -> p e f d", e=E, f=FB)
        rank = sb("rank", [P, E])
        lgc = sb("lgc", [P, TB, E])
        top = sb("top", [P, K2, TB])
        tie = sb("tie", [P, TB, E])
        tmax = sb("tmax", [P, TB])
        hot = sb("hot", [P, K2, TB, E])
        rest = sb("rest", [P, TB, E])
        mask = sb("mask", [P, TB, E], bf16)
        tri_s = sb("tri_s", [P, P], bf16)
        ones = sb("ones", [P, P], bf16)
        share = sb("share", [P, 3, TB])
        pos = sb("pos", [P, TB, E])
        carry = sb("carry", [P, E])
        hp = sb("hp", [P, K2 * TB, E])
        posf = sb("posf", [P, K2 * TB])
        idx = sb("idx", [P, K2 * TB], i32)
        destf = sb("destf", [P, K2, TB])
        regbase = sb("regbase", [P, E])
        cnt = sb("cnt", [P, E])
        kstep = sb("kstep", [P, E, T // P])
        kcmp = sb("kcmp", [P, E, T // P])
        ntl = sb("ntl", [P, E])
        cum = sb("cum", [P, E])
        onesf = sb("onesf", [P, E])
        skip = sb("skip", [P, E])
        zif = sb("zif", [P, E])
        zidx = sb("zidx", [P, E], i32)
        pcol = sb("pcol", [P, 1])
        zrow = sb("zrow", [P, E + SPARE, ROW])
        tix = sb("tix", [P, NTAB])
        tge, tw = (v[:].rearrange("p a c -> p (a c)")[:, 0:NTAB * E].rearrange("p (n e) -> p n e", e=E) for v in (u, c_sb))
        tsum = sb("tsum", [P, 2, NTAB])
        eoff = sb("eoff", [P, NTAB], i32)
        rowt = sb("rowt", [P, NTAB], i32)
        ffn = x1_all[:].rearrange("p c b d -> p (c b d)")
        xin = ffn[:, 0:4 * D].rearrange("p (a d) -> p a d", a=4)
        xgT = ffn[:, 512:1024].rearrange("p (a d) -> p a d", a=4)
        hs = ffn[:, 1024:2048].rearrange("p (a f) -> p a f", a=2)
        hT = ffn[:, 2048:3072].rearrange("p (a f) -> p a f", a=2)
        yt = ffn[:, 3072:3584].rearrange("p (a d) -> p a d", a=4)
        sil = u
        meta = sb("meta", [P, 4, 2])
        y0b, y1b, zf = h, c_sb, hc
        x2_all = xT
        w1_flat = decay[:, 0:E * F]
        w3_flat = w3_sb[:].rearrange("p e f -> p (e f)")
        w2_flat = x1T_all[:, 0:E * F]
        xg_dram = nc.dram_tensor("xg_dram", (E * REG + SPARE * P, ROW), f32, kind="Internal").ap()
        y2_dram = nc.dram_tensor("y2_dram", (K2 * T + (E + SPARE) * P, D), f32, kind="Internal").ap()
        m_dram = nc.dram_tensor("m_dram", (NG, P), f32, kind="Internal").ap()

        pa = pb("pa", [P, 2, CH])
        pB = pb("pB", [P, 2, CH])
        pC = pb("pC", [P, 2, CH])
        py = pb("py", [P, CH])
        pq = pb("pq", [P, CH])

        ld_w, ld_x, ld_g = sem("ld_w"), sem("ld_x"), sem("ld_g")
        s_memset, s_const, s_const2 = sem("s_memset"), sem("s_const"), sem("s_const2")
        s_setup_pe, s_proj, s_aexp = sem("s_setup_pe"), sem("s_proj"), sem("s_aexp")
        s_A = sem("s_A")
        s_dtp, s_dts, s_pre, s_bcp = sem("s_dtp"), sem("s_dts"), sem("s_pre"), sem("s_bcp")
        s_abs, s_ex, s_log, s_rel, s_dl, s_dx, s_dec = (sem("s_abs"), sem("s_ex"), sem("s_log"), sem("s_rel"),
                                                        sem("s_dl"), sem("s_dx"), sem("s_dec"))
        s_b1, s_b2, s_b3, s_b4 = sem("s_b1"), sem("s_b2"), sem("s_b3"), sem("s_b4")
        B_ready, C_ready, a_ready, C_copied = sem("B_ready"), sem("C_ready"), sem("a_ready"), sem("C_copied")
        u_done, h_done, hc_done, y_acc = sem("u_done"), sem("h_done"), sem("hc_done"), sem("y_acc")
        y_copied, p_done, p_copied, st_done = sem("y_copied"), sem("p_done"), sem("p_copied"), sem("st_done")
        mv_done, lv_done, rs_done, z_done = sem("mv_done"), sem("lv_done"), sem("rs_done"), sem("z_done")
        xc_done = sem("xc_done")
        st2_done, mv2_done, lv2_done, rs2_done, x1_done = (sem("st2_done"), sem("mv2_done"), sem("lv2_done"),
                                                           sem("rs2_done"), sem("x1_done"))
        x1T_done, x1T_copied, g_done, g_copied = sem("x1T_done"), sem("x1T_copied"), sem("g_done"), sem("g_copied")
        ld_chunk, ld_ctx, x1_kept, x1T_kept = sem("ld_chunk"), sem("ld_ctx"), sem("x1_kept"), sem("x1T_kept")
        s_reset = sem("s_reset")
        s_bc = sem("s_bc")
        s_out = sem("s_out")
        x_blocks = x_tok.rearrange("(c b p) d -> p c b d", p=P, b=TB)
        out_blocks = out.rearrange("(c b p) d -> p c b d", p=P, b=TB)
        passed, act_step, b_free, hv_done, stb_done = sem("passed"), sem("act_step"), sem("b_free"), sem("hv_done"), sem("stb_done")
        sc_sem, r_step, r_exp, mask_done, rk_done, x2r_done, idx_done = (sem("sc_sem"), sem("r_step"), sem("r_exp"),
                                                                         sem("mask_done"), sem("rk_done"),
                                                                         sem("x2r_done"), sem("idx_done"))
        t_step, tab_done, zero_out, x_in, m_in, xT_tr, xT_cp = (sem("t_step"), sem("tab_done"), sem("zero_out"),
                                                                [sem(f"x_in{r}") for r in range(4)], [sem(f"m_in{r}") for r in range(4)], sem("xT_tr"), sem("xT_cp"))
        up_done, sil_done, mul_done, hT_tr, hT_cp, dn_done, y_cp, y_out = (
            sem("up_done"), sem("sil_done"), sem("mul_done"), sem("hT_tr"), sem("hT_cp"), sem("dn_done"), sem("y_cp"),
            [sem(f"y_out{r}") for r in range(4)])
        y_in, zsum, fst, fmv, frs, fz, spread_rdy = ([sem(f"y_in{r}") for r in range(2)], sem("zsum"), sem("fst"), sem("fmv"), sem("frs"),
                                                     sem("fz"), sem("spread_rdy"))
        gate_step, g_const, m_ready, m_stored, E_ready = (sem("gate_step"), sem("g_const"), sem("m_ready"),
                                                          sem("m_stored"), sem("E_ready"))
        b_x1, b_x1T, b_cT, b_v, b_mb = sem("b_x1"), sem("b_x1T"), sem("b_cT"), sem("b_v"), sem("b_mb")
        qk_done, lm1, lm2, D_done, C_done, av_done = (sem("qk_done"), sem("lm1"), sem("lm2"), sem("D_done"),
                                                      sem("C_done"), sem("av_done"))
        n_step, cen_done, sq_done, vsum_done, vlog_done, vrs_done = (sem("n_step"), sem("cen_done"), sem("sq_done"),
                                                                     sem("vsum_done"), sem("vlog_done"), sem("vrs_done"))
        sc_done, zb_done, mvb_done, lvb_done, rsb_done, x2_done = (sem("sc_done"), sem("zb_done"), sem("mvb_done"),
                                                                   sem("lvb_done"), sem("rsb_done"), sem("x2_done"))
        x2T_done, x2T_copied, lg_done, lg_copied, x2_kept, x2T_kept = (sem("x2T_done"), sem("x2T_copied"),
                                                                       sem("lg_done"), sem("lg_copied"),
                                                                       sem("x2_kept"), sem("x2T_kept"))
        ld_f = sem("ld_f")

        ONE = 1
        primed = (hT_cp, s_dts, s_b2, s_abs, s_rel, s_pre, s_dl, z_done, g_copied, p_done, x1T_kept, x1_kept, x1T_done, h_done,
                  b_free, lm2, C_done, hv_done, lg_copied, x2_kept, r_exp)

        def close_wait(engine):
            engine.sem_inc(passed, 1)

        block = ctx.enter_context(nc.Block())

        @block.sync
        def _(sp):
            for started in primed:
                sp.sem_inc(started, ONE)
            sp.sem_inc(mul_done, 2)
            sp.sem_inc(dn_done, 1)
            sp.sem_inc(y_cp, 2)
            sp.sem_inc(xT_tr, 4)
            for dst, src in ((wdtw[:], W_dtw_T), (wdt[:], W_dt_T), (bdt[:], b_dt), (alog[:], A_log),
                             (wbc[:], W_BC_T), (dp[:], Dp), (lng[:], ln_g), (lnb[:], ln_b), (wout[:], W_out_T),
                             (gk[:], gate_kernel.rearrange("(s p) g -> p s g", p=P)),
                             (gbias[:], gate_bias.broadcast_to([P, 2 * H]))):
                sp.dma_start(dst, src).then_inc(ld_w, 16)
            sp.dma_start(xT[:, :], x_T).then_inc(ld_x, 16)
            sp.dma_start(xbuf[:], x_blocks[:, 0]).then_inc(ld_chunk, 16)
            sp.dma_start(cT_st[:], ctx_T[:, 0:CH]).then_inc(ld_ctx, 16)
            sp.dma_start(onorm[:], outnorm.broadcast_to([P, D])).then_inc(ld_f, 16)
            sp.dma_start(rw[:], router_w).then_inc(ld_f, 16)
            sp.dma_start(w3_sb[:], w3.rearrange("e d f -> d e f")).then_inc(ld_f, 16)

            def keep(c):
                sp.wait_ge(x1_done, c + 1)
                sp.dma_start(x1_all[:, ds(c, 1)].rearrange("p c b d -> p (c b) d"), x1_st[:]).then_inc(x1_kept, 16)
                sp.wait_ge(x1T_copied, c + 1)
                close_wait(sp)
                sp.dma_start(x1T_all[:, ds(c * CH, CH)], x1T_st[:]).then_inc(x1T_kept, 16)

            with sp.Fori(0, NCH) as c:
                sp.wait_ge(xc_done, c + 1)
                sp.dma_start(xbuf[:], x_blocks[:, ds(c, 1)].rearrange("p c b d -> p (c b) d")).then_inc(ld_chunk, 16)
                keep(c)
                sp.wait_ge(g_done, c + 1)
                sp.dma_start(cT_st[:], ctx_T[:, ds(c * CH, CH)]).then_inc(ld_ctx, 16)
            keep(NCH)
            sp.wait_ge(x1_kept, 16 * (NCH + 1) + ONE)
            sp.wait_ge(x1T_kept, 16 * (NCH + 1) + ONE)
            sp.wait_ge(g_copied, NCH + 1 + ONE)
            sp.wait_ge(m_ready, 1)
            sp.dma_start(m_dram, mrow[:]).then_inc(m_stored, 16)
            sp.wait_ge(m_stored, 16)
            sp.wait_ge(a_ready, NCH * N + 2)
            sp.dma_start(w1_sb, w1.rearrange("e d f -> d e f")).then_inc(ld_f, 16)
            m_v = m_dram.rearrange("(c n) (j s) -> j c n s", n=TB * H, j=2)
            c_blocks = ctx_tok.rearrange("(c b p) d -> p c b d", p=P, b=TB)
            with sp.Fori(0, NCH) as c:
                sp.wait_ge(b_free, c + ONE)
                close_wait(sp)
                sp.dma_start(x1c[:], x1_all[:, ds(c + 1, 1)].rearrange("p c b d -> p (c b) d")).then_inc(b_x1, 16)
                sp.dma_start(x1Tc[:], x1T_all[:, ds(c * CH + CH, CH)]).then_inc(b_x1, 16)
                sp.dma_start(cTc[:], ctx_T[:, ds(c * CH, CH)]).then_inc(b_x1, 16)
                for j in range(2):
                    sp.dma_start(hc[:].rearrange("p a (m s) -> p (a m) s", s=S)[64 * j:64 * j + 64],
                                 m_v[j, ds(c, 1)].broadcast_to([64, TB * H, S])
                                 ).then_inc(b_mb, 16)
                for b in range(TB):
                    sp.dma_start(V1[:, H * b:H * b + H, 0:S // 2],
                                 c_blocks[:, ds(c, 1), b].rearrange("p c (h e) -> p (c h) e", h=H)).then_inc(b_v, 16)
                sp.wait_ge(x2_done, c + 1)
                close_wait(sp)
                sp.dma_start(x2_all[:, ds(c * CH, CH)].rearrange("p (b d) -> p b d", b=TB),
                             x2r[:, 0, :, 0:D]).then_inc(x2_kept, 16)
            sp.wait_ge(b_free, NCH + ONE)
            sp.dma_start(w2_sb, w2.rearrange("e (b p) d -> p e b d", p=P)).then_inc(ld_f, 16)
            sp.wait_ge(tab_done, 1)
            sp.dma_start(xg_dram[E * REG:, :].rearrange("(n p) r -> p n r", p=P),
                         zrow[:, E:]).then_inc(zero_out, 16)
            sp.wait_ge(zero_out, 16)
            sp.wait_ge(sc_sem, 128 * NCH + 16 * E + 16)
            sp.wait_ge(x2_kept, 16 * NCH + ONE)

            def load_x(q, slot):
                i = 4 * q + slot
                sp.wait_ge(xT_tr, i - 3 + 4)
                close_wait(sp)
                row = sp.value_load(rowt[0:1, ds(i, 1)], min_val=0, max_val=E * REG + (SPARE - 1) * P)
                sp.dma_start(xin[:, slot % 4], xg_dram[ds(row, P), 0:D]).then_inc(x_in[slot % 4], 16)

            def load_meta(q, slot):
                i = 4 * q + slot
                sp.wait_ge(y_out[slot % 4], 16 * (q + slot // 4 + 1))
                close_wait(sp)
                row = sp.value_load(rowt[0:1, ds(i, 1)], min_val=0, max_val=E * REG + (SPARE - 1) * P)
                sp.dma_start(meta[:, slot % 4], xg_dram[ds(row, P), D:ROW]).then_inc(m_in[slot % 4], 16)

            sp.wait_ge(tab_done, 2)
            load_x(0, 0)
            with sp.Fori(0, NTIL // 4) as it:
                for r in range(4):
                    i = it * 4 + r
                    load_x(it, r + 1)
                    load_meta(it, r)
            for r in range(4):
                sp.wait_ge(y_out[r], 16 * (NTIL // 4 + 1))
            y_blocks = y2_dram[0:K2 * T].rearrange("(k c b p) d -> k p c b d", k=K2, p=P, b=TB)
            v4 = "p (b d) -> p b d"

            def fetch(c, slot):
                sp.dma_start(y0b[:, slot].rearrange(v4, b=TB), y_blocks[0][:, ds(c, 1)].rearrange("p c b d -> p (c b) d")
                             ).then_inc(y_in[slot], 16)
                sp.dma_start(y1b[:, slot].rearrange(v4, b=TB), y_blocks[1][:, ds(c, 1)].rearrange("p c b d -> p (c b) d")
                             ).then_inc(y_in[slot], 16)

            def store(c, slot):
                sp.wait_ge(fz, c + 1)
                close_wait(sp)
                sp.dma_start(out_blocks[:, ds(c, 1)].rearrange("p c b d -> p (c b) d"),
                             zf[:, slot].rearrange(v4, b=TB)).then_inc(s_out, 16)

            fetch(0, 0)
            fetch(1, 1)
            with sp.Fori(0, NCH // 2 - 1) as it:
                for r in range(2):
                    store(it * 2 + r, r)
                    fetch(it * 2 + r + 2, r)
            store(NCH - 2, 0)
            store(NCH - 1, 1)
            sp.wait_ge(s_out, 16 * NCH)

        @block.gpsimd
        def _(pool):
            nc.gpsimd.memset(ident[:], 0.0).then_inc(s_memset, 1)
            nc.gpsimd.memset(sel[:], 0.0).then_inc(s_memset, 1)
            nc.gpsimd.memset(eps5[:], 1e-5).then_inc(s_const, 1)
            pool.wait_ge(s_memset, 2)
            nc.gpsimd.affine_select(out=ident[:], in_=ident[:], compare_op=ALU.not_equal, fill=1.0, base=0,
                                    pattern=[[-1, P]], channel_multiplier=1).then_inc(s_const, 1)
            for part in range(3):
                pool.wait_ge(s_const, 2 + part)
                v = sel[2 * N * part:2 * N * (part + 1), :, :]
                nc.gpsimd.affine_select(out=v, in_=v, compare_op=ALU.not_equal, fill=1.0, base=0,
                                        pattern=[[-1, 2 * N], [0, P]], channel_multiplier=1).then_inc(s_const, 1)
            pool.wait_ge(s_const, 5)
            nc.gpsimd.memset(dx[:, T:], 0.0).then_inc(s_const, 1)
            nc.gpsimd.memset(decay[:, T:], 0.0).then_inc(s_const, 1)
            pool.wait_ge(s_const, 7)
            nc.gpsimd.memset(bcs[:, T:], 0.0).then_inc(s_const, 1)
            pool.wait_ge(s_const, 8)
            nc.gpsimd.tensor_scalar(center[:], ident[:], -1.0 / D, None, ALU.add).then_inc(s_const, 1)
            pool.sem_inc(hc_done, 2)

            def residual(c):
                pool.wait_ge(ld_chunk, 16 * (c + 1))
                pool.wait_ge(z_done, c + ONE)
                pool.wait_ge(s_proj, 1)
                nc.gpsimd.tensor_tensor(xc[:], xbuf[:], cvec[:].unsqueeze(1).to_broadcast([P, TB, D]),
                                        ALU.add).then_inc(xc_done, 1)

            with pool.Fori(0, NCH) as c:
                for n in range(N):
                    k = c * N + n
                    if n == 1:
                        residual(c)
                    pool.wait_ge(h_done, k + 1 + ONE)
                    pool.wait_ge(C_copied, k + 1)
                    pool.wait_ge(y_acc, k + 1)
                    nc.gpsimd.tensor_tensor(hc[:, n % 2], h[:, n % 2], c_sb[:, n % 2], ALU.mult).then_inc(hc_done, 1)
            residual(NCH)
            pool.wait_ge(hc_done, NCH * N + 2)
            nc.gpsimd.memset(tri[:], 1.0).then_inc(g_const, 1)
            nc.gpsimd.memset(fence[:], 0.0).then_inc(g_const, 1)
            nc.gpsimd.memset(maskT[:], 0.0).then_inc(g_const, 1)
            nc.gpsimd.memset(V1[:, :, S // 2:], 1.0).then_inc(g_const, 1)
            nc.gpsimd.memset(zrow[:, :, 0:D], 0.0).then_inc(g_const, 1)
            nc.gpsimd.memset(zrow[:, :, D + 1:], 0.0).then_inc(g_const, 1)
            nc.gpsimd.memset(ones[:], 1.0).then_inc(g_const, 1)
            nc.gpsimd.memset(onesf[:], 1.0).then_inc(g_const, 1)
            nc.gpsimd.memset(tri_s[:], 1.0).then_inc(g_const, 1)
            pool.wait_ge(g_const, 9)
            nc.gpsimd.memset(fence[:, 0:P:S], -BIG).then_inc(g_const, 1)
            imprecise = dict(allow_small_or_imprecise_dtypes=True)
            nc.gpsimd.iota(rank[:], pattern=[[-1, E]], base=E, channel_multiplier=0, **imprecise).then_inc(g_const, 1)
            nc.gpsimd.iota(regbase[:], pattern=[[REG, E]], base=0, channel_multiplier=0, **imprecise).then_inc(g_const, 1)
            nc.gpsimd.iota(carry[:], pattern=[[REG, E]], base=0, channel_multiplier=0, **imprecise).then_inc(g_const, 1)
            nc.gpsimd.iota(destf[:], pattern=[[T, K2], [P, TB]], base=0, channel_multiplier=1,
                           **imprecise).then_inc(g_const, 1)
            nc.gpsimd.iota(kstep[:], pattern=[[0, E], [P, T // P]], base=0, channel_multiplier=0,
                           **imprecise).then_inc(g_const, 1)
            nc.gpsimd.iota(tix[:], pattern=[[1, NTAB]], base=0, channel_multiplier=0, **imprecise).then_inc(g_const, 1)
            nc.gpsimd.iota(pcol[:], pattern=[[0, 1]], base=0, channel_multiplier=1, **imprecise).then_inc(g_const, 1)
            nc.gpsimd.iota(zrow[:, :, D].bitcast(i32), pattern=[[P, E + SPARE]], base=K2 * T,
                           channel_multiplier=1).then_inc(g_const, 1)
            nc.gpsimd.affine_select(out=tri_s[:], in_=tri_s[:], compare_op=ALU.is_gt, fill=0.0, base=0,
                                    pattern=[[1, P]], channel_multiplier=-1).then_inc(g_const, 1)
            nc.gpsimd.affine_select(out=tri[:], in_=tri[:], compare_op=ALU.is_ge, fill=0.0, base=0,
                                    pattern=[[1, P]], channel_multiplier=-1).then_inc(g_const, 1)
            pool.wait_ge(g_const, 20)
            nc.gpsimd.memset(tri[0:S, S:P], 0.0).then_inc(g_const, 1)
            pool.wait_ge(g_const, 21)
            for j in range(2):
                nc.gpsimd.affine_select(out=maskT[S * j:S * j + S], in_=maskT[S * j:S * j + S], compare_op=ALU.is_ge,
                                        fill=-BIG, base=0, pattern=[[1, S]],
                                        channel_multiplier=-1).then_inc(g_const, 1)
                pool.wait_ge(g_const, 22 + j)
            nothing = bass.IndirectOffsetOnAxis(ap=zrow[:, 0, D:D + 1].bitcast(i32), axis=0)
            nc.gpsimd.indirect_dma_start(out=xg_dram, out_offset=nothing, in_=zrow[:, 0], in_offset=None).then_inc(sc_sem, 16)
            for ahead in range(4):
                nc.gpsimd.indirect_dma_start(out=y2_dram, out_offset=nothing, in_=zrow[:, 0, 0:D],
                                             in_offset=None).then_inc(y_out[ahead], 16)
                pool.wait_ge(y_out[ahead], 16)
            pool.wait_ge(sc_sem, 16)
            v16 = [P, TB * H, S]
            with pool.Fori(0, NCH) as c:
                pool.wait_ge(b_mb, 32 * c + 32)
                pool.wait_ge(lm2, c + ONE)
                nc.gpsimd.tensor_tensor(lmask.rearrange("p (m s) -> p m s", s=S), maskT[:].unsqueeze(1).to_broadcast(v16),
                                        mb.rearrange("p (m s) -> p m s", s=S), ALU.subtract).then_inc(lm1, 1)
                pool.wait_ge(cen_done, c + 1)
                nc.gpsimd.tensor_tensor(sq[:], cen[:], cen[:], ALU.mult).then_inc(sq_done, 1)
                pool.wait_ge(sc_done, 2 * c + 1)
                nc.gpsimd.tensor_tensor(z[:], hv[:].rearrange("p (b h) e -> p b (h e)", b=TB), x1c[:],
                                        ALU.add).then_inc(zb_done, 1)
                pool.wait_ge(x2r_done, 2 * c + 2)
                pool.wait_ge(idx_done, c + 1)
                close_wait(pool)
                for k in range(K2):
                    for b in range(TB):
                        m = k * TB + b
                        nc.gpsimd.indirect_dma_start(
                            out=xg_dram, out_offset=bass.IndirectOffsetOnAxis(ap=idx[:, m:m + 1], axis=0),
                            in_=x2r[:, k, b], in_offset=None).then_inc(sc_sem, 16)
            pool.wait_ge(tab_done, 1)
            for e in range(E):
                nc.gpsimd.indirect_dma_start(
                    out=xg_dram, out_offset=bass.IndirectOffsetOnAxis(ap=zidx[:, e:e + 1], axis=0),
                    in_=zrow[:, e], in_offset=None).then_inc(sc_sem, 16)

            def scatter(q, slot):
                i = 4 * q + slot
                pool.wait_ge(y_cp, i + 1 + 2)
                pool.wait_ge(m_in[slot % 4], 16 * (q + slot // 4 + 1))
                close_wait(pool)
                nc.gpsimd.indirect_dma_start(
                    out=y2_dram, out_offset=bass.IndirectOffsetOnAxis(ap=meta[:, slot % 4, 0:1].bitcast(i32), axis=0),
                    in_=yt[:, slot % 4], in_offset=None).then_inc(y_out[slot % 4], 16)

            with pool.Fori(0, NTIL // 4) as it:
                for r in range(4):
                    scatter(it, r)

        @block.tensor
        def _(pe):
            pe.wait_ge(s_setup_pe, 1)
            nc.tensor.matmul(pq[:, 0:D], center[:], gw[:], start=True, stop=True)
            nc.tensor.matmul(pq[:, D:2 * D], lnb_rep[:], wout[:], start=True, stop=True).then_inc(s_const2, 1)
            pe.wait_ge(s_proj, 1)
            pe.wait_ge(ld_x, 16)
            with pe.Fori(0, NCH) as c:
                x_c = xT[:, ds(c * CH, CH)]
                pe.wait_ge(s_dts, c + ONE)
                close_wait(pe)
                nc.tensor.matmul(pa[0:R, 0], wdtw[:], x_c, start=True, stop=True).then_inc(s_dtp, 1)
                pe.wait_ge(s_b2, c + ONE)
                close_wait(pe)
                nc.tensor.matmul(pa[0:2 * N, 1], wbc[:], x_c, start=True, stop=True).then_inc(s_bcp, 1)
                pe.wait_ge(s_dts, c + 1 + ONE)
                pe.wait_ge(s_abs, c + ONE)
                pe.wait_ge(s_rel, c + ONE)
                nc.tensor.matmul(pB[:, 0], wdt[:], dt_sb[:], start=True, stop=True).then_inc(s_pre, 1)

            def spread(k, n, tok):
                nc.tensor.matmul(pB[:, n % 2], sel[:, n, :], bcs[:, tok], start=True, stop=True).then_inc(B_ready, 1)

            def spread_c(k, n, tok):
                nc.tensor.matmul(pC[:, n % 2], sel[:, N + n, :], bcs[:, tok], start=True, stop=True).then_inc(C_ready, 1)

            pe.wait_ge(s_b4, NCH)
            pe.wait_ge(s_pre, NCH + ONE)
            pe.wait_ge(s_rel, NCH + ONE)
            for n in range(2):
                spread(n, n, slice(0, CH))
                spread_c(n, n, slice(0, CH))

            def project(c, half):
                pe.wait_ge(y_copied, c + 1)
                if half == 1:
                    pe.wait_ge(st_done, 2 * c + 1)
                    pe.wait_ge(p_copied, 2 * c + 1)
                else:
                    pe.wait_ge(g_copied, c + ONE)
                for b in range(2):
                    last = nc.tensor.matmul(pq[:, b * 2 * D:(b + 1) * 2 * D], y_sb[:, (2 * half + b) * P:(2 * half + b + 1) * P],
                                            proj[:], start=True, stop=True)
                last.then_inc(p_done, 1)

            def transposes(c):
                pe.wait_ge(x1_done, c + 1)
                pe.wait_ge(st_done, 2 * c + 2)
                pe.wait_ge(p_copied, 2 * c + 2)
                for b in range(TB):
                    last = nc.tensor.transpose(pq[:, b * P:(b + 1) * P], x1_st[:, b], ident[:])
                last.then_inc(x1T_done, 1)

            def gate_products(c):
                pe.wait_ge(x1T_copied, c + 1)
                pe.wait_ge(ld_ctx, 16 * (c + 1))
                for b in range(TB):
                    o = pq[:, b * 2 * H:(b + 1) * 2 * H]
                    nc.tensor.matmul(o, x1T_st[:, b * P:(b + 1) * P], gk[:, 0], start=True, stop=False)
                    last = nc.tensor.matmul(o, cT_st[:, b * P:(b + 1) * P], gkv[:], start=False, stop=True)
                last.then_inc(g_done, 1)

            def tail(c, n):
                if n == 2:
                    project(c, 0)
                if n == 4:
                    project(c, 1)
                if n == 11:
                    transposes(c)
                if n == 13:
                    gate_products(c)

            with pe.Fori(0, NCH) as c:
                for n in range(N):
                    k = c * N + n
                    nxt = ds(c * CH, CH) if n < N - 2 else ds(c * CH + CH, CH)
                    m = (n + 2) % N
                    tail(c, n)
                    pe.wait_ge(u_done, k + 1)
                    spread(k + 2, m, nxt)
                    pe.wait_ge(C_copied, k + 1)
                    spread_c(k + 2, m, nxt)
                    pe.wait_ge(hc_done, k + 3)
                    if n == 0:
                        pe.wait_ge(y_copied, c + 1)
                        nc.tensor.matmul(py[:], diag_dp[:], xT[:, ds(c * CH, CH)], start=True, stop=False)
                    nc.tensor.matmul(py[:], ident[:], hc[:, n % 2], start=False, stop=(n == N - 1)).then_inc(y_acc, 1)
            for n in range(N):
                tail(NCH, n)
            pe.wait_ge(gate_step, 1)
            pe.wait_ge(g_const, 23)
            nc.tensor.matmul(pq[:, 0:NG], tri[:], lfg[:], start=True, stop=True).then_inc(gate_step, 1)
            pe.wait_ge(gate_step, 3)
            nc.tensor.transpose(pC[:, 0, 0:P], g_sb[:], ident[:]).then_inc(gate_step, 1)
            pe.wait_ge(gate_step, 5)
            nc.tensor.transpose(pC[:, 1, 0:P], mrow[:], ident[:]).then_inc(gate_step, 1)
            pe.wait_ge(E_ready, 1)
            HD = D // H
            with pe.Fori(0, NCH) as c:
                pe.wait_ge(b_x1, 48 * c + 48)
                pe.wait_ge(C_done, c + ONE)
                for hh in range(H):
                    bank = (pa if hh < 2 else pB)[:, hh % 2]
                    rows = slice(HD * hh, HD * hh + HD)
                    for b in range(TB):
                        for j in range(2):
                            t0 = b * P + S * j
                            last = nc.tensor.matmul(bank[S * j:S * j + S, b * S:b * S + S], cTc[rows, t0:t0 + S],
                                                    x1Tc[rows, t0:t0 + S], start=True, stop=True)
                last.then_inc(qk_done, 1)
                pe.wait_ge(C_done, c + 1 + ONE)
                pe.wait_ge(b_v, 16 * TB * (c + 1))
                pe.wait_ge(hv_done, c + ONE)
                close_wait(pe)
                for b in range(TB):
                    for j in range(2):
                        for hh in range(H):
                            m = b * H + hh
                            last = nc.tensor.matmul(pC[S * j:S * j + S, b // 2, ((b % 2) * H + hh) * (HD + 1):((b % 2) * H + hh + 1) * (HD + 1)],
                                                    Cm[S * j:S * j + S, m * S:m * S + S], V1[S * j:S * j + S, m],
                                                    start=True, stop=True)
                last.then_inc(av_done, 1)
                pe.wait_ge(x2_done, c + 1)
                pe.wait_ge(lg_copied, c + ONE)
                for b in range(TB):
                    last = nc.tensor.transpose(pq[:, b * P:(b + 1) * P], x2r[:, 0, b, 0:D], ident[:])
                last.then_inc(x2T_done, 1)
                pe.wait_ge(x2T_copied, c + 1)
                for b in range(TB):
                    last = nc.tensor.matmul(py[:, b * E:(b + 1) * E], x2T_st[:, b * P:(b + 1) * P], rw[:], start=True,
                                            stop=True)
                last.then_inc(lg_done, 1)
                pe.wait_ge(mask_done, c + 1)
                pe.wait_ge(x2T_copied, c + 1)
                nc.tensor.matmul(pq[:, 0:TB * E], tri_s[:], mask[:].rearrange("p b e -> p (b e)"), start=True, stop=False)
                for b in range(TB):
                    left = TB - 1 - b
                    if left:
                        nc.tensor.matmul(pq[:, (b + 1) * E:TB * E].rearrange("p (b e) -> p b e", e=E), ones[:],
                                         mask[:, b].unsqueeze(1).to_broadcast([P, left, E]), start=False, stop=left == 1)
                for b in range(TB):
                    last = nc.tensor.matmul(py[:, TB * E:(TB + 1) * E], ones[:], mask[:, b], start=(b == 0),
                                            stop=(b == TB - 1))
                last.then_inc(rk_done, 1)
            pe.wait_ge(ld_f, 64)
            pe.wait_ge(tab_done, 2)
            tiles = dict(min_val=0, max_val=(E - 1) * F)

            def up(q, slot):
                i = 4 * q + slot
                pe.wait_ge(xT_cp, i + 1)
                pe.wait_ge(mul_done, i - 1 + 2)
                close_wait(pe)
                eo = pe.value_load(eoff[0:1, ds(i, 1)], **tiles)
                lhs = xgT[:, slot % 4]
                nc.tensor.matmul(pa[:, slot % 2], lhs, w1_flat[:, ds(eo, F)], start=True, stop=True)
                nc.tensor.matmul(pB[:, slot % 2], lhs, w3_flat[:, ds(eo, F)], start=True, stop=True).then_inc(up_done, 1)

            def turn_h(q, slot):
                i = 4 * q + slot
                pe.wait_ge(mul_done, i + 1 + 2)
                pe.wait_ge(hT_cp, i + ONE)
                for f in range(FB):
                    last = nc.tensor.transpose(pC[:, 0, f * P:(f + 1) * P], hs[:, slot % 2, f * P:(f + 1) * P], ident[:])
                last.then_inc(hT_tr, 1)

            def down(q, slot):
                i = 4 * q + slot
                pe.wait_ge(hT_cp, i + 1 + ONE)
                pe.wait_ge(y_cp, i - 1 + 2)
                close_wait(pe)
                eo = pe.value_load(eoff[0:1, ds(i, 1)], **tiles)
                o = (pC[:, 1] if slot % 2 else py[:])[:, 0:D]
                for f in range(FB):
                    last = nc.tensor.matmul(o, hT[:, slot % 2, f * P:(f + 1) * P], w2_flat[:, ds(eo + f * D, D)],
                                            start=(f == 0), stop=(f == FB - 1))
                last.then_inc(dn_done, 1)

            def turn_x(q, slot):
                i = 4 * q + slot
                pe.wait_ge(x_in[slot % 4], 16 * (q + slot // 4 + 1))
                pe.wait_ge(xT_cp, i)
                nc.tensor.transpose(pq[:, 0:P], xin[:, slot % 4], ident[:]).then_inc(xT_tr, 1)

            pe.wait_ge(x_in[0], 16)
            nc.tensor.transpose(pq[:, 0:P], xin[:, 0], ident[:]).then_inc(xT_tr, 1)
            turn_x(0, 1)
            up(0, 0)
            up(0, 1)
            turn_h(0, 0)
            turn_x(0, 2)
            with pe.Fori(0, (NTIL - 4) // 4) as it:
                for r in range(4):
                    i = it * 4 + 1 + r
                    up(it, r + 2)
                    turn_h(it, r + 1)
                    down(it, r)
                    turn_x(it, r + 3)
            for i in range(NTIL - 3, NTIL):
                if i + 1 < NTIL:
                    up(0, i + 1)
                turn_h(0, i)
                down(0, i - 1)
                if i + 2 < NTIL:
                    turn_x(0, i + 2)
            down(0, NTIL - 1)

        @block.scalar
        def _(act):
            nc.scalar.preload_act_table_set("natural_log_exp_and_others")
            act.wait_ge(ld_w, 16 * 11)
            nc.scalar.activation(Aneg[:], alog[:], ACT.Exp).then_inc(s_aexp, 1)
            with act.Fori(0, NCH) as c:
                act.wait_ge(s_dtp, c + 1)
                act.wait_ge(s_pre, c + ONE)
                nc.scalar.copy(dt_sb[:], pa[0:R, 0]).then_inc(s_dts, 1)
                act.wait_ge(s_rel, c + 1 + ONE)
                nc.scalar.activation(pabs, pB[:, 0], ACT.Abs, bias=bdt[:]).then_inc(s_abs, 1)
                act.wait_ge(s_abs, c + 1 + ONE)
                nc.scalar.activation(pexp, pabs, ACT.Exp, scale=-1.0).then_inc(s_ex, 1)
                act.wait_ge(s_ex, c + 1)
                act.wait_ge(s_dl, c + ONE)
                nc.scalar.activation(plog, pexp, ACT.Ln, bias=1.0).then_inc(s_log, 1)

            def decay_exp(n, tok):
                close_wait(act)
                nc.scalar.activation(pa[:, n % 2], decay[:, tok], ACT.Exp, scale=Aneg[:, n:n + 1]).then_inc(a_ready, 1)

            def copy_c(n):
                nc.scalar.copy(c_sb[:, n % 2], pC[:, n % 2]).then_inc(C_copied, 1)

            act.wait_ge(s_dec, NCH)
            act.wait_ge(s_A, 2)
            act.wait_ge(s_b2, NCH + ONE)
            for n in range(2):
                decay_exp(n, slice(0, CH))
                act.wait_ge(C_ready, n + 1)
                copy_c(n)

            def tail(c, n):
                if n == 1:
                    act.wait_ge(y_acc, c * N + 2)
                    act.wait_ge(p_done, 2 * c + ONE)
                    nc.scalar.copy(y_sb[:], py[:]).then_inc(y_copied, 1)
                if n in (3, 5):
                    half = (n - 3) // 2
                    act.wait_ge(p_done, 2 * c + half + 1 + ONE)
                    act.wait_ge(z_done, c + ONE)
                    act.wait_ge(st_done, 2 * c + half + 1)
                    nc.scalar.copy(p_sb[:, 2 * half:2 * half + 2], pq[:].rearrange("p (b e) -> p b e", b=2)[:, :, 0:D]
                                   ).then_inc(p_copied, 1)
                if n == 7:
                    act.wait_ge(mv_done, c + 1)
                    act.wait_ge(z_done, c + ONE)
                    nc.scalar.activation(lv[:], mv[:, :, 1], ACT.Ln, bias=eps5[:]).then_inc(lv_done, 1)
                    act.wait_ge(lv_done, c + 1)
                    nc.scalar.activation(rstd[:], lv[:], ACT.Exp, scale=-0.5).then_inc(rs_done, 1)
                if n == 10:
                    act.wait_ge(mv2_done, c + 1)
                    nc.scalar.activation(lv2[:], mv2[:, :, 1], ACT.Ln, bias=eps5[:]).then_inc(lv2_done, 1)
                    act.wait_ge(lv2_done, c + 1)
                    nc.scalar.activation(rstd2[:], lv2[:], ACT.Exp, scale=-0.5).then_inc(rs2_done, 1)
                if n == 12:
                    act.wait_ge(x1T_done, c + 1 + ONE)
                    act.wait_ge(x1T_kept, 16 * c + ONE)
                    nc.scalar.copy(x1T_st[:], pq[:]).then_inc(x1T_copied, 1)

            with act.Fori(0, NCH) as c:
                for n in range(N):
                    k = c * N + n
                    nxt = ds(c * CH, CH) if n < N - 2 else ds(c * CH + CH, CH)
                    tail(c, n)
                    act.wait_ge(h_done, k + 1 + ONE)
                    decay_exp((n + 2) % N, nxt)
                    act.wait_ge(C_ready, k + 3)
                    act.wait_ge(hc_done, k + 3)
                    copy_c((n + 2) % N)
            for n in range(N):
                tail(NCH, n)
            act.wait_ge(g_copied, NCH + 1 + ONE)
            fg = gates[:, 1:].rearrange("p c b g -> p (c b) g")[:, :, H:2 * H]
            v3 = "p (n h) -> p n h"
            nc.scalar.activation(gabs[:].rearrange(v3, h=H), fg, ACT.Abs).then_inc(act_step, 1)
            act.wait_ge(act_step, 1)
            nc.scalar.activation(gexp[:], gabs[:], ACT.Exp, scale=-1.0).then_inc(act_step, 1)
            act.wait_ge(act_step, 2)
            nc.scalar.activation(glog[:], gexp[:], ACT.Ln, bias=1.0).then_inc(act_step, 1)
            act.wait_ge(gate_step, 7)
            nc.scalar.activation(floor_[:], nlog[:], ACT.Exp, scale=-1.0).then_inc(E_ready, 1)
            NR, RS = 26, 13
            with act.Fori(0, NCH) as c:
                act.wait_ge(lm2, c + 1 + ONE)
                act.wait_ge(C_done, c + ONE)
                nc.scalar.activation(Dm, lmask, ACT.Exp).then_inc(D_done, 1)
                act.wait_ge(vsum_done, c + 1)
                nc.scalar.activation(vlog[:], vsum[:], ACT.Ln, scale=float(H) / D, bias=eps5[:]).then_inc(vlog_done, 1)
                act.wait_ge(vlog_done, c + 1)
                nc.scalar.activation(vrs[:], vlog[:], ACT.Exp, scale=-0.5).then_inc(vrs_done, 1)
                act.wait_ge(mvb_done, c + 1)
                nc.scalar.activation(lv[:], mv[:, :, 1], ACT.Ln, bias=eps5[:]).then_inc(lvb_done, 1)
                act.wait_ge(lvb_done, c + 1)
                nc.scalar.activation(rstd[:], lv[:], ACT.Exp, scale=-0.5).then_inc(rsb_done, 1)
                act.wait_ge(x2T_done, c + 1)
                nc.scalar.copy(x2T_st[:], pq[:]).then_inc(x2T_copied, 1)
                nc.scalar.copy(x2r[:, 1, :, 0:D], x2r[:, 0, :, 0:D]).then_inc(x2r_done, 1)
                act.wait_ge(r_step, NR * c + RS)
                nc.scalar.activation(share[:, 1], share[:, 0], ACT.Exp).then_inc(r_exp, 1)

            def gate_act(q, slot):
                i = 4 * q + slot
                act.wait_ge(up_done, i + 1)
                act.wait_ge(mul_done, i - 1 + 2)
                nc.scalar.activation(sil[:, slot % 2], pa[:, slot % 2], ACT.Silu).then_inc(sil_done, 1)

            def copy_hT(q, slot):
                i = 4 * q + slot
                act.wait_ge(hT_tr, i + 1)
                act.wait_ge(dn_done, i - 1 + 1)
                nc.scalar.copy(hT[:, slot % 2], pC[:, 0]).then_inc(hT_cp, 1)

            def weigh(q, slot):
                i = 4 * q + slot
                act.wait_ge(dn_done, i + 1 + 1)
                act.wait_ge(m_in[slot % 4], 16 * (q + slot // 4 + 1))
                act.wait_ge(y_out[slot % 4], 16 * (q + slot // 4 + 1))
                o = (pC[:, 1] if slot % 2 else py[:])[:, 0:D]
                nc.scalar.activation(yt[:, slot % 4], o, ACT.Copy, scale=meta[:, slot % 4, 1:2]).then_inc(y_cp, 1)

            gate_act(0, 0)
            gate_act(0, 1)
            copy_hT(0, 0)
            with act.Fori(0, (NTIL - 4) // 4) as it:
                for r in range(4):
                    i = it * 4 + 1 + r
                    gate_act(it, r + 2)
                    copy_hT(it, r + 1)
                    weigh(it, r)
            for i in range(NTIL - 3, NTIL):
                if i + 1 < NTIL:
                    gate_act(0, i + 1)
                copy_hT(0, i)
                weigh(0, i - 1)
            weigh(0, NTIL - 1)
            with act.Fori(0, NCH) as c:
                act.wait_ge(fmv, c + 1)
                nc.scalar.activation(lv[:], mv[:, :, 1], ACT.Ln, bias=eps5[:]).then_inc(frs, 1)
                act.wait_ge(frs, 2 * c + 1)
                nc.scalar.activation(rstd[:], lv[:], ACT.Exp, scale=-0.5).then_inc(frs, 1)

        @block.vector
        def _(dve):
            dve.wait_ge(ld_w, 16 * 11)
            dve.wait_ge(s_const, 9)
            nc.vector.memset(py[:], 0.0).then_inc(y_acc, 2)
            nc.vector.tensor_scalar(gw[:], wout[:], lng[:], None, ALU.mult)
            nc.vector.tensor_copy(lnb_rep[:], lnb[:].to_broadcast([D, P]))
            nc.vector.tensor_scalar(diag_dp[:], ident[:], dp[:], None, ALU.mult)
            nc.vector.tensor_copy(proj[:, D:2 * D], ident[:])
            nc.vector.tensor_tensor(gkv[:], gk[:, 1], gk[:, 2], ALU.add).then_inc(s_setup_pe, 1)
            dve.wait_ge(s_aexp, 1)
            nc.vector.tensor_scalar(Aneg[:], Aneg[:], -1.0, -1e-27, ALU.mult, ALU.min).then_inc(s_A, 2)
            dve.wait_ge(s_const2, 1)
            nc.vector.tensor_copy(proj[:, 0:D], pq[:, 0:D])
            nc.vector.tensor_copy(cvec[:], pq[:, D:2 * D]).then_inc(s_proj, 1)
            dve.wait_ge(ld_x, 16)
            with dve.Fori(0, NCH) as c:
                tok = ds(c * CH, CH)
                dve.wait_ge(s_bcp, c + 1)
                close_wait(dve)
                nc.vector.tensor_copy(bcs[0:32, tok], pa[0:2 * N, 1]).then_inc(s_b1, 1)
                dve.wait_ge(s_pre, c + 1 + ONE)
                nc.vector.tensor_scalar(prel, pB[:, 0], bdt[:], 0.0, ALU.add, ALU.max).then_inc(s_rel, 1)
                dve.wait_ge(s_b1, c + 1)
                nc.vector.tensor_tensor(res1[:], pa[0:2 * N, 1], bcs[0:32, tok], ALU.subtract).then_inc(s_b2, 1)
                dve.wait_ge(s_rel, c + 1 + ONE)
                dve.wait_ge(s_log, c + 1)
                nc.vector.tensor_tensor(delta, prel, plog, ALU.add).then_inc(s_dl, 1)
                dve.wait_ge(s_b2, c + 1 + ONE)
                close_wait(dve)
                nc.vector.tensor_copy(bcs[32:64, tok], res1[:]).then_inc(s_b3, 1)
                dve.wait_ge(s_dl, c + 1 + ONE)
                nc.vector.tensor_tensor(dx[:, tok], delta, xT[:, tok], ALU.mult).then_inc(s_dx, 1)
                dve.wait_ge(s_b3, c + 1)
                close_wait(dve)
                nc.vector.tensor_copy(bc32[:], bcs[32:64, tok]).then_inc(s_bc, 1)
                dve.wait_ge(s_dx, c + 1)
                nc.vector.memset(delta.rearrange("p (b s) -> p b s", s=S)[:, :, 0:1], BIG).then_inc(s_reset, 1)
                dve.wait_ge(s_reset, c + 1)
                close_wait(dve)
                nc.vector.tensor_copy(decay[:, tok], delta).then_inc(s_dec, 1)
                dve.wait_ge(s_bc, c + 1)
                nc.vector.tensor_tensor(bcs[64:96, tok], res1[:], bc32[:], ALU.subtract).then_inc(s_b4, 1)

            def product(n, tok):
                nc.vector.tensor_tensor(u[:, n % 2], dx[:, tok], pB[:, n % 2], ALU.mult).then_inc(u_done, 1)

            dve.wait_ge(s_dx, NCH)
            dve.wait_ge(B_ready, 1)
            product(0, slice(0, CH))

            def stats(src, dst, sems, value, blocks):
                for b in blocks:
                    last = nc.vector.bn_stats(dst[:, b], src(b))
                last.then_inc(sems, 1)
                dve.wait_ge(sems, value)
                close_wait(dve)

            def tail(c, n):
                if n in (3, 5):
                    half = (n - 3) // 2
                    dve.wait_ge(p_done, 2 * c + half + 1 + ONE)
                    stats(lambda b: pq[:, (b % 2) * 2 * D + D:(b % 2) * 2 * D + 2 * D], st, st_done, 2 * c + half + 1,
                          (2 * half, 2 * half + 1))
                if n == 6:
                    for b in range(TB):
                        last = nc.vector.bn_aggr(mv[:, b], st[:, b])
                    last.then_inc(mv_done, 1)
                if n == 8:
                    dve.wait_ge(rs_done, c + 1)
                    dve.wait_ge(p_copied, 2 * c + 2)
                    dve.wait_ge(xc_done, c + 1)
                    for b in range(TB):
                        last = nc.vector.scalar_tensor_tensor(z[:, b], p_sb[:, b], rstd[:, b:b + 1], xc[:, b],
                                                              ALU.mult, ALU.add)
                    last.then_inc(z_done, 1)
                if n == 9:
                    dve.wait_ge(z_done, c + 1 + ONE)
                    stats(lambda b: z[:, b], st2, st2_done, c + 1, range(TB))
                    for b in range(TB):
                        last = nc.vector.bn_aggr(mv2[:, b], st2[:, b])
                    last.then_inc(mv2_done, 1)
                if n == 11:
                    dve.wait_ge(rs2_done, c + 1)
                    dve.wait_ge(x1_kept, 16 * c + ONE)
                    dve.wait_ge(x1T_done, c + ONE)
                    for b in range(TB):
                        last = nc.vector.tensor_scalar(x1_st[:, b], z[:, b], mv2[:, b, 0:1], rstd2[:, b:b + 1],
                                                       ALU.subtract, ALU.mult)
                    last.then_inc(x1_done, 1)
                if n == 14:
                    dve.wait_ge(g_done, c + 1)
                    nc.vector.tensor_tensor(gates[:, ds(c, 1)].rearrange("p c b g -> p (c b) g"),
                                            pq[:, 0:TB * 2 * H].rearrange("p (b g) -> p b g", b=TB),
                                            gbias[:].unsqueeze(1).to_broadcast([P, TB, 2 * H]),
                                            ALU.add).then_inc(g_copied, 1)

            with dve.Fori(0, NCH) as c:
                for n in range(N):
                    k = c * N + n
                    nxt = ds(c * CH, CH) if n < N - 1 else ds(c * CH + CH, CH)
                    tail(c, n)
                    dve.wait_ge(B_ready, k + 2)
                    dve.wait_ge(h_done, k + ONE)
                    product((n + 1) % N, nxt)
                    dve.wait_ge(a_ready, k + 1)
                    dve.wait_ge(u_done, k + 1)
                    dve.wait_ge(hc_done, k + 1)
                    nc.vector.tensor_tensor_scan(h[:, n % 2], pa[:, n % 2], u[:, n % 2], 0.0, ALU.mult,
                                                 ALU.add).then_inc(h_done, 1)
            for n in range(N):
                tail(NCH, n)
            v3 = "p (n h) -> p n h"
            gv = gates[:, 1:].rearrange("p c b g -> p (c b) g")
            dve.wait_ge(g_copied, NCH + 1 + ONE)
            dve.wait_ge(act_step, 3)
            nc.vector.scalar_tensor_tensor(lfg[:].rearrange(v3, h=H), gv[:, :, H:2 * H], 0.0, glog[:].rearrange(v3, h=H),
                                           ALU.min, ALU.subtract).then_inc(gate_step, 1)
            dve.wait_ge(gate_step, 2)
            nc.vector.tensor_copy(cs_sb[:], pq[:, 0:NG])
            nc.vector.tensor_tensor(g_sb[:].rearrange(v3, h=H), gv[:, :, 0:H], pq[:, 0:NG].rearrange(v3, h=H),
                                    ALU.subtract).then_inc(gate_step, 1)
            dve.wait_ge(gate_step, 4)
            nc.vector.tensor_tensor_scan(mrow[:], fence[:], pC[:, 0, 0:P], 0.0, ALU.add, ALU.max).then_inc(gate_step, 1)
            dve.wait_ge(gate_step, 5)
            nc.vector.engine_nop().then_inc(m_ready, 1)
            dve.wait_ge(gate_step, 6)
            nc.vector.tensor_tensor(nlog[:], cs_sb[:], pC[:, 1, 0:NG], ALU.add).then_inc(gate_step, 1)
            dve.wait_ge(E_ready, 1)
            HD = D // H
            M = TB * H
            NSTEP = 6
            NR, RS = 26, 13
            with dve.Fori(0, NCH) as c:
                dve.wait_ge(lm1, c + 1)
                g_c = g_sb[:, ds(c * M, M)].unsqueeze(2).to_broadcast([P, M, S])
                lm = lmask.rearrange("p (m s) -> p m s", s=S)
                close_wait(dve)
                nc.vector.tensor_tensor(lm, lm, g_c, ALU.add).then_inc(lm2, 1)
                dve.wait_ge(D_done, c + 1)
                dve.wait_ge(qk_done, c + 1)
                scale = float(HD) ** -0.5
                for hh in range(H):
                    bank = (pa if hh < 2 else pB)[:, hh % 2, 0:TB * S].rearrange("p (b s) -> p b s", s=S)
                    pick = lambda v: v.rearrange("p (b h s) -> p h b s", h=H, s=S)[:, hh]
                    last = nc.vector.scalar_tensor_tensor(pick(Cm), bank, scale, pick(Dm), ALU.mult, ALU.mult)
                last.then_inc(C_done, 1)
                dve.wait_ge(av_done, c + 1)
                pav = pC[:, :, 0:(M // 2) * (HD + 1)].rearrange("p a (m e) -> p a m e", e=HD + 1)
                two = lambda v: v.rearrange("p (a m) -> p a m", a=2)
                s0 = c * NSTEP
                close_wait(dve)
                nc.vector.tensor_tensor(two(rs[:]), pav[:, :, :, HD], two(floor_[:, ds(c * M, M)]),
                                        ALU.max).then_inc(n_step, 1)
                dve.wait_ge(n_step, s0 + 1)
                nc.vector.scalar_tensor_tensor(two(rs[:]), pav[:, :, :, HD], -1.0, two(rs[:]),
                                               ALU.mult, ALU.max).then_inc(n_step, 1)
                dve.wait_ge(n_step, s0 + 2)
                nc.vector.tensor_scalar(rs[:], rs[:], 1e-6, None, ALU.add).then_inc(n_step, 1)
                dve.wait_ge(n_step, s0 + 3)
                nc.vector.reciprocal(rinv[:], rs[:]).then_inc(n_step, 1)
                dve.wait_ge(n_step, s0 + 4)
                nc.vector.tensor_tensor(hv[:].rearrange("p (a m) e -> p a m e", a=2), pav[:, :, :, 0:HD],
                                        two(rinv[:]).unsqueeze(3).to_broadcast([P, 2, M // 2, HD]),
                                        ALU.mult).then_inc(hv_done, 1)
                dve.wait_ge(hv_done, c + 1 + ONE)
                nc.vector.tensor_reduce(hsum[:], hv[:], AX.X, ALU.add).then_inc(n_step, 1)
                dve.wait_ge(n_step, s0 + 5)
                nc.vector.scalar_tensor_tensor(cen[:], hsum[:].unsqueeze(2).to_broadcast([P, M, HD]), -1.0 / HD, hv[:],
                                               ALU.mult, ALU.add).then_inc(cen_done, 1)
                dve.wait_ge(sq_done, c + 1)
                nc.vector.tensor_reduce(vsum[:], sq[:], AX.X, ALU.add).then_inc(vsum_done, 1)
                dve.wait_ge(vrs_done, c + 1)
                nc.vector.tensor_tensor(cen[:], cen[:], vrs[:].unsqueeze(2).to_broadcast([P, M, HD]),
                                        ALU.mult).then_inc(n_step, 1)
                dve.wait_ge(n_step, s0 + 6)
                nc.vector.tensor_tensor(hv[:].rearrange("p (b h) e -> p b (h e)", b=TB),
                                        cen[:].rearrange("p (b h) e -> p b (h e)", b=TB),
                                        onorm[:].unsqueeze(1).to_broadcast([P, TB, D]), ALU.mult).then_inc(sc_done, 2)
                dve.wait_ge(zb_done, c + 1)
                for b in range(TB):
                    last = nc.vector.bn_stats(st[:, b], z[:, b])
                last.then_inc(stb_done, 1)
                dve.wait_ge(stb_done, c + 1)
                close_wait(dve)
                for b in range(TB):
                    last = nc.vector.bn_aggr(mv[:, b], st[:, b])
                last.then_inc(mvb_done, 1)
                dve.wait_ge(rsb_done, c + 1)
                dve.wait_ge(x2_kept, 16 * c + ONE)
                dve.wait_ge(sc_sem, 128 * c + 16)
                for b in range(TB):
                    last = nc.vector.tensor_scalar(x2r[:, 0, b, 0:D], z[:, b], mv[:, b, 0:1], rstd[:, b:b + 1],
                                                   ALU.subtract, ALU.mult)
                last.then_inc(x2_done, 1)
                dve.wait_ge(lg_done, c + 1)
                step = [0]

                def link(ins, n_inc=1):
                    step[0] += 1
                    ins.then_inc(r_step, 1)
                    dve.wait_ge(r_step, NR * c + step[0])

                wide = [P, TB, E]
                link(nc.vector.tensor_copy(lgc[:], py[:, 0:TB * E].rearrange("p (b e) -> p b e", e=E)))
                src = lgc[:]
                for k in range(K2):
                    link(nc.vector.tensor_reduce(top[:, k], src, AX.X, ALU.max))
                    link(nc.vector.tensor_tensor(tie[:], src, top[:, k].unsqueeze(2).to_broadcast(wide), ALU.is_equal))
                    link(nc.vector.tensor_tensor(tie[:], tie[:], rank[:].unsqueeze(1).to_broadcast(wide), ALU.mult))
                    link(nc.vector.tensor_reduce(tmax[:], tie[:], AX.X, ALU.max))
                    link(nc.vector.tensor_tensor(hot[:, k], tie[:], tmax[:].unsqueeze(2).to_broadcast(wide), ALU.is_equal))
                    if k == 0:
                        link(nc.vector.scalar_tensor_tensor(rest[:], hot[:, 0], -BIG, lgc[:], ALU.mult, ALU.add))
                        src = rest[:]
                link(nc.vector.tensor_tensor(share[:, 0], top[:, 1], top[:, 0], ALU.subtract))
                assert step[0] == RS
                nc.vector.tensor_tensor(mask[:], hot[:, 0], hot[:, 1], ALU.add).then_inc(mask_done, 1)
                link(nc.vector.tensor_copy(x2r[:, :, :, D].bitcast(i32), destf[:]))
                link(nc.vector.tensor_scalar(destf[:], destf[:], float(CH), None, ALU.add))
                dve.wait_ge(r_exp, c + 1 + ONE)
                link(nc.vector.tensor_scalar(share[:, 0], share[:, 1], 1.0, None, ALU.add))
                link(nc.vector.reciprocal(share[:, 2], share[:, 0]))
                link(nc.vector.tensor_copy(x2r[:, 0, :, D + 1], share[:, 2]))
                link(nc.vector.tensor_tensor(x2r[:, 1, :, D + 1], share[:, 1], share[:, 2], ALU.mult))
                dve.sem_inc(x2r_done, 1)
                dve.wait_ge(rk_done, c + 1)
                link(nc.vector.tensor_tensor(pos[:], pq[:, 0:TB * E].rearrange("p (b e) -> p b e", e=E),
                                             carry[:].unsqueeze(1).to_broadcast(wide), ALU.add))
                link(nc.vector.tensor_tensor(carry[:], carry[:], py[:, TB * E:(TB + 1) * E], ALU.add))
                for k in range(K2):
                    link(nc.vector.tensor_tensor(hp[:, k * TB:(k + 1) * TB], hot[:, k], pos[:], ALU.mult))
                link(nc.vector.tensor_reduce(posf[:], hp[:], AX.X, ALU.add))
                nc.vector.tensor_copy(idx[:], posf[:]).then_inc(idx_done, 1)
                dve.sem_inc(lg_copied, 1)
                dve.sem_inc(b_free, 1)
                dve.sem_inc(r_step, NR - step[0])
            steps = [0]

            def tlink(ins):
                steps[0] += 1
                ins.then_inc(t_step, 1)
                dve.wait_ge(t_step, steps[0])

            dve.wait_ge(idx_done, NCH)
            tlink(nc.vector.tensor_scalar(zif[:], carry[:], pcol[:], None, ALU.add))
            tlink(nc.vector.tensor_copy(zidx[:], zif[:]))
            dve.sem_inc(tab_done, 1)
            tlink(nc.vector.tensor_tensor(cnt[:], carry[:], regbase[:], ALU.subtract))
            tlink(nc.vector.tensor_tensor(kcmp[:], cnt[:].unsqueeze(2).to_broadcast([P, E, T // P]), kstep[:], ALU.is_gt))
            tlink(nc.vector.tensor_reduce(ntl[:], kcmp[:], AX.X, ALU.add))
            tlink(nc.vector.tensor_tensor_scan(cum[:], onesf[:], ntl[:], 0.0, ALU.mult, ALU.add))
            tlink(nc.vector.tensor_scalar(skip[:], ntl[:], -float(P), float(REG), ALU.mult, ALU.add))
            tshape = [P, NTAB, E]
            tlink(nc.vector.tensor_tensor(tge, tix[:].unsqueeze(2).to_broadcast(tshape),
                                          cum[:].unsqueeze(1).to_broadcast(tshape), ALU.is_ge))
            tlink(nc.vector.tensor_tensor(tw, tge, skip[:].unsqueeze(1).to_broadcast(tshape), ALU.mult))
            tlink(nc.vector.tensor_reduce(tsum[:, 0], tge, AX.X, ALU.add))
            tlink(nc.vector.tensor_reduce(tsum[:, 1], tw, AX.X, ALU.add))
            tlink(nc.vector.tensor_scalar(tsum[:, 0], tsum[:, 0], float(E - 1), float(F), ALU.min, ALU.mult))
            tlink(nc.vector.scalar_tensor_tensor(tsum[:, 1], tix[:], float(P), tsum[:, 1], ALU.mult, ALU.add))
            tlink(nc.vector.tensor_copy(eoff[:], tsum[:, 0]))
            tlink(nc.vector.tensor_copy(rowt[:], tsum[:, 1]))
            dve.sem_inc(tab_done, 1)

            def product_h(q, slot):
                i = 4 * q + slot
                dve.wait_ge(sil_done, i + 1)
                nc.vector.tensor_tensor(hs[:, slot % 2], sil[:, slot % 2], pB[:, slot % 2], ALU.mult).then_inc(mul_done, 1)

            def copy_xT(q, slot):
                i = 4 * q + slot
                dve.wait_ge(xT_tr, i + 1 + 4)
                nc.vector.tensor_copy(xgT[:, slot % 4], pq[:, 0:P]).then_inc(xT_cp, 1)

            copy_xT(0, 0)
            copy_xT(0, 1)
            product_h(0, 0)
            product_h(0, 1)
            copy_xT(0, 2)
            with dve.Fori(0, (NTIL - 4) // 4) as it:
                for r in range(4):
                    i = it * 4 + 1 + r
                    product_h(it, r + 2)
                    copy_xT(it, r + 3)
            for i in range(NTIL - 3, NTIL):
                if i + 1 < NTIL:
                    product_h(0, i + 1)
                if i + 2 < NTIL:
                    copy_xT(0, i + 2)

            def finish(it, slot):
                c = 2 * it + slot
                dve.wait_ge(y_in[slot], 32 * (it + 1))
                close_wait(dve)
                nc.vector.tensor_tensor(y0b[:, slot], y0b[:, slot], x2_all[:, ds(c * CH, CH)], ALU.add).then_inc(zsum, 1)
                dve.wait_ge(zsum, 2 * c + 1)
                nc.vector.tensor_tensor(y0b[:, slot], y0b[:, slot], y1b[:, slot], ALU.add).then_inc(zsum, 1)
                dve.wait_ge(zsum, 2 * c + 2)
                for b in range(TB):
                    last = nc.vector.bn_stats(st[:, b], y0b[:, slot, b * D:(b + 1) * D])
                last.then_inc(fst, 1)
                dve.wait_ge(fst, c + 1)
                close_wait(dve)
                for b in range(TB):
                    last = nc.vector.bn_aggr(mv[:, b], st[:, b])
                last.then_inc(fmv, 1)
                dve.wait_ge(frs, 2 * c + 2)
                for b in range(TB):
                    last = nc.vector.tensor_scalar(zf[:, slot, b * D:(b + 1) * D], y0b[:, slot, b * D:(b + 1) * D],
                                                   mv[:, b, 0:1], rstd[:, b:b + 1], ALU.subtract, ALU.mult)
                last.then_inc(fz, 1)

            with dve.Fori(0, NCH // 2) as it:
                for r in range(2):
                    finish(it, r)


_LAYOUT = [
    ("x_tok", lambda i: i["x"].reshape(4096, 128)),
    ("x_T", lambda i: i["x"].reshape(4096, 128).T),
    ("ctx_tok", lambda i: i["ctx_1024"].reshape(4096, 128)),
    ("ctx_T", lambda i: i["ctx_1024"].reshape(4096, 128).T),
    ("W_dtw_T", lambda i: i["L0_attn_W_dtw"].T),
    ("W_dt_T", lambda i: i["L0_attn_W_dt"].T),
    ("b_dt", lambda i: i["L0_attn_b_dt"][:, None]),
    ("A_log", lambda i: i["L0_attn_A_log"]),
    ("W_BC_T", "bc"),
    ("Dp", lambda i: i["L0_attn_Dp"][:, None]),
    ("ln_g", lambda i: i["L0_attn_ln_g"][:, None]),
    ("ln_b", lambda i: i["L0_attn_ln_b"][:, None]),
    ("W_out_T", lambda i: i["L0_attn_W_out"].T),
    ("gate_kernel", "gk"),
    ("gate_bias", "gb"),
    ("outnorm", lambda i: i["L0_xattn_outnorm_scale"][None, :]),
    ("router_w", lambda i: i["L0_ffn_gate_w"]),
    ("w1", lambda i: i["L0_ffn_w1"]),
    ("w3", lambda i: i["L0_ffn_w3"]),
    ("w2", lambda i: i["L0_ffn_w2"]),
]


def kernel(**inputs):
    import numpy as np
    import concourse.bacc as bacc
    from concourse.bass_utils import run_bass_kernel_spmd

    i = {k: np.asarray(v) for k, v in inputs.items()}
    joined = {
        "bc": lambda: np.concatenate([i["L0_attn_W_B"].T, i["L0_attn_W_C"].T], axis=1),
        "gk": lambda: np.concatenate([i["L0_xattn_igate_kernel"], i["L0_xattn_fgate_kernel"]], axis=1),
        "gb": lambda: np.concatenate([i["L0_xattn_igate_bias"], i["L0_xattn_fgate_bias"]])[None, :],
    }
    nc = bacc.Bacc("TRN2", target_bir_lowering=False, num_devices=1)
    arrays, args = {}, []
    for name, make in _LAYOUT:
        a = np.ascontiguousarray(joined[make]() if isinstance(make, str) else make(i))
        arrays[f"in_{name}"] = a
        args.append(nc.dram_tensor(f"in_{name}", a.shape, mybir.dt.from_np(a.dtype), kind="ExternalInput").ap())
    args.append(nc.dram_tensor("out_0", (4096, 128), mybir.dt.float32, kind="ExternalOutput").ap())
    decoder_layer(nc, *args)
    r = run_bass_kernel_spmd(nc, [arrays], core_ids=[0])
    return r.results[0]["out_0"].reshape(64, 64, 128)
```

```python
import concourse.bass as bass
from concourse import mybir
from contextlib import ExitStack


def decoder_layer(nc, x_tok, x_T, ctx_tok, ctx_T, W_dtw_T, W_dt_T, b_dt, A_log, W_BC_T, Dp, ln_g, ln_b, W_out_T,
                  gate_kernel, gate_bias, outnorm, router_w, w1, w3, w2, out):
    f32, bf16, i32 = mybir.dt.float32, mybir.dt.bfloat16, mybir.dt.int32
    ALU, ACT, AX = mybir.AluOpType, mybir.ActivationFunctionType, mybir.AxisListType
    ds = bass.ds
    P = 128
    D, T = x_T.shape
    S = 64
    N = A_log.shape[1]
    R = W_dtw_T.shape[1]
    CH = 512
    NCH = T // CH
    TB = CH // P
    H = 4
    NT = T // P
    BIG = 1.0e30
    NR, RS = 22, 13

    ctx = ExitStack()
    with ctx:
        def sb(name, shape, dt=f32):
            return ctx.enter_context(nc.sbuf_tensor(name, shape, dt))

        def pb(name, shape):
            return ctx.enter_context(nc.psum_tensor(name, shape, f32))

        def sem(name):
            return ctx.enter_context(nc.semaphore(name))

        wdtw = sb("wdtw", [D, R])
        wdt = sb("wdt", [R, D])
        bdt = sb("bdt", [D, 1])
        alog = sb("alog", [D, N])
        Aneg = sb("Aneg", [D, N])
        wbc = sb("wbc", [D, 2 * N])
        dp = sb("dp", [D, 1])
        lng = sb("lng", [D, 1])
        lnb = sb("lnb", [D, 1])
        wout = sb("wout", [D, D])
        gk = sb("gk", [P, 3, 2 * H])
        gkv = sb("gkv", [P, 2 * H])
        gbias = sb("gbias", [P, 2 * H])
        ident = sb("ident", [P, P])
        center = sb("center", [P, P])
        gw = sb("gw", [D, D])
        lnb_rep = sb("lnb_rep", [D, P])
        diag_dp = sb("diag_dp", [D, D])
        proj = sb("proj", [D, 2 * D])
        cvec = sb("cvec", [P, D])
        part_id = sb("part_id", [96, 2 * N], bf16)
        sel = sb("sel", [96, 2 * N, P], bf16)
        eps5 = sb("eps5", [P, 1])
        PAD = CH
        xT = sb("xT", [D, T])
        dx = sb("dx", [D, T + PAD])
        decay = sb("decay", [D, T + PAD])
        bcs = sb("bcs", [96, T + PAD], bf16)
        b3t = sb("b3t", [2 * N, 2, CH], bf16)
        DEPTH = 4
        LAG = 2
        u = sb("u", [D, DEPTH, CH])
        h = sb("h", [D, DEPTH, CH])
        c_sb = sb("c_sb", [D, DEPTH, CH])
        hc = sb("hc", [D, DEPTH, CH])
        y_sb = sb("y_sb", [D, CH])
        p_sb = sb("p_sb", [P, TB, D])
        xbuf = sb("xbuf", [P, TB, D])
        xc = sb("xc", [P, TB, D])
        z = sb("z", [P, TB, D])
        st = sb("st", [P, TB, 6])
        mv = sb("mv", [P, TB, 2])
        lv = sb("lv", [P, TB])
        rstd = sb("rstd", [P, TB])
        st2 = sb("st2", [P, TB, 6])
        mv2 = sb("mv2", [P, TB, 2])
        lv2 = sb("lv2", [P, TB])
        rstd2 = sb("rstd2", [P, TB])
        x1_st = sb("x1_st", [P, TB, D])
        x1T_st = sb("x1T_st", [D, CH])
        cT_st = sb("cT_st", [D, CH])
        x1_all = sb("x1_all", [P, NCH + 1, TB, D])
        x1T_all = sb("x1T_all", [D, T + PAD])
        gates = sb("gates", [P, NCH + 2, TB, 2 * H])

        NG = NT * H
        gabs = sb("gabs", [P, NG])
        gexp = sb("gexp", [P, NG])
        glog = sb("glog", [P, NG])
        lfg = sb("lfg", [P, NG])
        tri = sb("tri", [P, P])
        cs_sb = sb("cs_sb", [P, NG])
        g_sb = sb("g_sb", [P, NG])
        fence = sb("fence", [P, P])
        mrow = sb("mrow", [P, P])
        nlog = sb("nlog", [P, NG])
        floor_ = sb("floor_", [P, NG])
        maskT = sb("maskT", [P, S])
        onorm = sb("onorm", [P, D])
        x2_st = y_sb[:].rearrange("p (b d) -> p b d", b=TB)
        x1c = sb("x1c", [P, TB, D])
        x1Tc = sb("x1Tc", [D, CH])
        cTc = sb("cTc", [D, CH])
        V1 = sb("V1", [P, TB * H, S // 2 + 1])
        lmask, Dm, Cm, mb = (v[:, 0:2].rearrange("p a c -> p (a c)") for v in (u, h, c_sb, hc))
        rs = sb("rs", [P, TB * H])
        rinv = sb("rinv", [P, TB * H])
        hsum = sb("hsum", [P, TB * H])
        vsum = sb("vsum", [P, TB * H])
        vlog = sb("vlog", [P, TB * H])
        vrs = sb("vrs", [P, TB * H])
        hv = sb("hv", [P, TB * H, S // 2])
        cen = sb("cen", [P, TB * H, S // 2])
        sq = sb("sq", [P, TB * H, S // 2])
        flat = lambda v: v[:].rearrange("p a b -> p (a b)") if len(v.shape) == 3 else v[:]
        pabs, pexp, plog, prel = (hv, x1Tc), (cen, cTc), (sq, x1T_st), (x1c, x1_st)
        pabs, pexp, plog, prel = ([flat(v) for v in pair] for pair in (pabs, pexp, plog, prel))
        dt_sb = h[0:R, 0:2]
        res1 = c_sb[0:2 * N, 0:2]
        E, F = w1.shape[0], w1.shape[2]
        FB = F // P
        K2 = 2
        REG = T + P
        NTIL = K2 * T // P + E
        NTAB = NTIL + 1
        SPARE = NTAB - K2 * T // P
        ROW = D + 2
        x2r = sb("x2r", [P, K2, TB, ROW])
        x2T_st = sb("x2T_st", [D, CH])
        rw = sb("rw", [D, E])
        w1_sb = decay[:, 0:E * F].rearrange("p (e f) -> p e f", e=E)
        w3_sb = dx[:, 0:E * F].rearrange("p (e f) -> p e f", e=E)
        w2_sb = x1T_all[:, 0:E * F].rearrange("p (e f d) -> p e f d", e=E, f=FB)
        rank = sb("rank", [P, E])
        lgc = sb("lgc", [P, TB, E])
        top = sb("top", [P, K2, TB])
        tie = sb("tie", [P, TB, E])
        tmax = sb("tmax", [P, TB])
        hot = sb("hot", [P, K2, TB, E])
        rest = sb("rest", [P, TB, E])
        mask = sb("mask", [P, TB, E], bf16)
        tri_s = sb("tri_s", [P, P], bf16)
        ones = sb("ones", [P, P], bf16)
        share = sb("share", [P, 3, TB])
        pos = sb("pos", [P, TB, E])
        carry = sb("carry", [P, E])
        hp = sb("hp", [P, K2 * TB, E])
        posf = sb("posf", [P, K2 * TB])
        idx = sb("idx", [P, K2 * TB], i32)
        destf = sb("destf", [P, K2, TB])
        regbase = sb("regbase", [P, E])
        cnt = sb("cnt", [P, E])
        kstep = sb("kstep", [P, E, T // P])
        kcmp = sb("kcmp", [P, E, T // P])
        ntl = sb("ntl", [P, E])
        cum = sb("cum", [P, E])
        onesf = sb("onesf", [P, E])
        skip = sb("skip", [P, E])
        zidx = sb("zidx", [P, E], i32)
        zrow = sb("zrow", [P, E + SPARE, ROW])
        tix = sb("tix", [P, NTAB])
        tge, tw = (v[:].rearrange("p a c -> p (a c)")[:, 0:NTAB * E].rearrange("p (n e) -> p n e", e=E) for v in (u, c_sb))
        tsum = sb("tsum", [P, 2, NTAB])
        eoff = sb("eoff", [P, NTAB], i32)
        rowt = sb("rowt", [P, NTAB], i32)
        ffn = x1_all[:].rearrange("p c b d -> p (c b d)")
        xin = ffn[:, 0:4 * D].rearrange("p (a d) -> p a d", a=4)
        xgT = ffn[:, 512:1024].rearrange("p (a d) -> p a d", a=4)
        hs = ffn[:, 1024:2048].rearrange("p (a f) -> p a f", a=2)
        hT = ffn[:, 2048:3072].rearrange("p (a f) -> p a f", a=2)
        yt = ffn[:, 3072:3584].rearrange("p (a d) -> p a d", a=4)
        sil = u
        meta = sb("meta", [P, 4, 2])
        y0_all = decay[:, 0:T]
        y1_all = dx[:, 0:T]
        last_st, last_mv, last_lv, last_rs = (st, st2), (mv, mv2), (lv, lv2), (rstd, rstd2)
        last_nm = sb("last_nm", [P, 2, TB])
        x2_all = xT
        w1_flat = decay[:, 0:E * F]
        w3_flat = dx[:, 0:E * F]
        w2_flat = x1T_all[:, 0:E * F]
        xg_dram = nc.dram_tensor("xg_dram", (E * REG + SPARE * P, ROW), f32, kind="Internal").ap()
        y2_dram = nc.dram_tensor("y2_dram", (K2 * T + (E + SPARE) * P, D), f32, kind="Internal").ap()
        y_blocks = y2_dram[0:K2 * T].rearrange("(k c b p) d -> k p c b d", k=K2, p=P, b=TB)
        v4 = "p (b d) -> p b d"
        m_dram = nc.dram_tensor("m_dram", (NG, P), f32, kind="Internal").ap()

        pa = pb("pa", [P, 2, CH])
        pB = pb("pB", [P, 2, CH])
        pC = pb("pC", [P, 2, CH])
        py = pb("py", [P, CH])
        pq = pb("pq", [P, CH])

        ld_w, ld_x, ld_g = sem("ld_w"), sem("ld_x"), sem("ld_g")
        s_memset, s_const, s_const2 = sem("s_memset"), sem("s_const"), sem("s_const2")
        s_setup_pe, s_proj, s_aexp = sem("s_setup_pe"), sem("s_proj"), sem("s_aexp")
        s_A, s_ident, s_part, s_sel = sem("s_A"), sem("s_ident"), sem("s_part"), sem("s_sel")
        LW = 7
        s_dtp, s_dts, s_pre, s_bcp = sem("s_dtp"), sem("s_dts"), sem("s_pre"), sem("s_bcp")
        s_abs, s_ex, s_log, s_rel, s_dl, s_dx, s_dec = (sem("s_abs"), sem("s_ex"), sem("s_log"), sem("s_rel"),
                                                        sem("s_dl"), sem("s_dx"), sem("s_dec"))
        s_b1, s_b2, s_b3, s_b4 = sem("s_b1"), sem("s_b2"), sem("s_b3"), sem("s_b4")
        B_ready, C_ready, a_ready, C_copied = sem("B_ready"), sem("C_ready"), sem("a_ready"), sem("C_copied")
        u_done, h_done, hc_done, y_acc = sem("u_done"), sem("h_done"), sem("hc_done"), sem("y_acc")
        y_copied, p_done, p_copied, st_done = sem("y_copied"), sem("p_done"), sem("p_copied"), sem("st_done")
        mv_done, lv_done, rs_done, z_done = sem("mv_done"), sem("lv_done"), sem("rs_done"), sem("z_done")
        xc_done = sem("xc_done")
        st2_done, mv2_done, lv2_done, rs2_done, x1_done = (sem("st2_done"), sem("mv2_done"), sem("lv2_done"),
                                                           sem("rs2_done"), sem("x1_done"))
        x1T_done, x1T_copied, g_done, g_copied = sem("x1T_done"), sem("x1T_copied"), sem("g_done"), sem("g_copied")
        ld_chunk, ld_ctx, x1_kept, x1T_kept = sem("ld_chunk"), sem("ld_ctx"), sem("x1_kept"), sem("x1T_kept")
        s_reset = sem("s_reset")
        s_bc = sem("s_bc")
        s_out = sem("s_out")
        x_blocks = x_tok.rearrange("(c b p) d -> p c b d", p=P, b=TB)
        out_blocks = out.rearrange("(c b p) d -> p c b d", p=P, b=TB)
        passed, act_step, hv_done, rows_done = sem("passed"), sem("act_step"), sem("hv_done"), sem("rows_done")
        sc_sem, r_step, r_exp, mask_done, rk_done, x2r_done, idx_done = (sem("sc_sem"), sem("r_step"), sem("r_exp"),
                                                                         sem("mask_done"), sem("rk_done"),
                                                                         sem("x2r_done"), sem("idx_done"))
        t_step, tab_done, zero_out, x_in, m_in, xT_tr, xT_cp = (sem("t_step"), sem("tab_done"), sem("zero_out"),
                                                                [sem(f"x_in{r}") for r in range(4)], [sem(f"m_in{r}") for r in range(4)], sem("xT_tr"), sem("xT_cp"))
        up_done, sil_done, mul_done, hT_tr, hT_cp, dn_done, y_cp, y_out = (
            sem("up_done"), sem("sil_done"), sem("mul_done"), sem("hT_tr"), sem("hT_cp"), sem("dn_done"), sem("y_cp"),
            [sem(f"y_out{r}") for r in range(4)])
        y_in, zsum, fst, fmv, frs, fz, spread_rdy = ([sem(f"y_in{r}") for r in range(NCH)], sem("zsum"), sem("fst"), sem("fmv"), sem("frs"),
                                                     sem("fz"), sem("spread_rdy"))
        z_half = sem("z_half")
        res_done, flv, fnm = sem("res_done"), sem("flv"), sem("fnm")
        gate_step, g_const, m_ready, m_stored, E_ready = (sem("gate_step"), sem("g_const"), sem("m_ready"),
                                                          sem("m_stored"), sem("E_ready"))
        b_x1, b_x1T, b_cT, b_v, b_mb = sem("b_x1"), sem("b_x1T"), sem("b_cT"), sem("b_v"), sem("b_mb")
        qk_done, lm1, lm2, D_done, C_done, av_done = (sem("qk_done"), sem("lm1"), sem("lm2"), sem("D_done"),
                                                      sem("C_done"), sem("av_done"))
        n_step, cen_done, sq_done, vsum_done, vlog_done, vrs_done = (sem("n_step"), sem("cen_done"), sem("sq_done"),
                                                                     sem("vsum_done"), sem("vlog_done"), sem("vrs_done"))
        sc_done, zb_done, mvb_done, lvb_done, rsb_done, x2_done = (sem("sc_done"), sem("zb_done"), sem("mvb_done"),
                                                                   sem("lvb_done"), sem("rsb_done"), sem("x2_done"))
        x2T_done, x2T_copied, lg_done, lg_copied, x2_kept, x2T_kept = (sem("x2T_done"), sem("x2T_copied"),
                                                                       sem("lg_done"), sem("lg_copied"),
                                                                       sem("x2_kept"), sem("x2T_kept"))
        ld_f = sem("ld_f")

        ONE = 1
        primed = (hT_cp, z_done, x1T_copied, p_done, x1T_kept, x1_kept, x1T_done, mv_done,
                  lm2, C_done, hv_done, lg_copied, x2_kept, r_exp, D_done, x2T_done, rows_done)

        def close_wait(engine):
            engine.sem_inc(passed, 1)

        def zero_rows(engine, experts):
            for e in experts:
                row = engine.value_load(zidx[0:1, e:e + 1], min_val=e * REG, max_val=e * REG + T)
                engine.dma_start(xg_dram[ds(row, P), :], zrow[:, e]).then_inc(zero_out, 16)

        block = ctx.enter_context(nc.Block())

        @block.sync
        def _(sp):
            for started in primed:
                sp.sem_inc(started, ONE)
            sp.sem_inc(mul_done, 2)
            for two_back in (h_done, s_dts, s_b2, s_abs, s_rel, s_pre, s_b4):
                sp.sem_inc(two_back, 2)
            sp.sem_inc(dn_done, 1)
            sp.sem_inc(y_cp, 2)
            sp.sem_inc(xT_tr, 4)
            sp.dma_start(xT[:, 0:T // 2], x_T[:, 0:T // 2]).then_inc(ld_x, 16)
            for dst, src in ((wdtw[:], W_dtw_T), (wbc[:], W_BC_T), (wdt[:], W_dt_T), (bdt[:], b_dt)):
                sp.dma_start(dst, src).then_inc(ld_x, 16)
            for dst, src in ((alog[:], A_log), (dp[:], Dp), (lng[:], ln_g), (lnb[:], ln_b), (wout[:], W_out_T),
                             (gk[:], gate_kernel.rearrange("(s p) g -> p s g", p=P)),
                             (gbias[:], gate_bias.broadcast_to([P, 2 * H]))):
                sp.dma_start(dst, src).then_inc(ld_w, 16)
            sp.dma_start(xbuf[:], x_blocks[:, 0]).then_inc(ld_chunk, 16)
            sp.dma_start(cT_st[:], ctx_T[:, 0:CH]).then_inc(ld_ctx, 16)
            sp.dma_start(onorm[:], outnorm.broadcast_to([P, D])).then_inc(ld_f, 16)
            sp.dma_start(rw[:], router_w).then_inc(ld_f, 16)

            def keep(c):
                sp.wait_ge(x1_done, c + 1)
                sp.dma_start(x1_all[:, ds(c, 1)].rearrange("p c b d -> p (c b) d"), x1_st[:]).then_inc(x1_kept, 16)
                sp.wait_ge(x1T_copied, c + 1 + ONE)
                close_wait(sp)
                sp.dma_start(x1T_all[:, ds(c * CH, CH)], x1T_st[:]).then_inc(x1T_kept, 16)

            def follow(c, gated):
                sp.wait_ge(xc_done, c + 1)
                sp.dma_start(xbuf[:], x_blocks[:, ds(c, 1)].rearrange("p c b d -> p (c b) d")).then_inc(ld_chunk, 16)
                load_context(c, gated)
                keep(c)

            def load_context(c, gated):
                sp.wait_ge(g_done, c + 1)
                close_wait(sp)
                sp.dma_start(cT_st[:], ctx_T[:, ds(gated * CH, CH)]).then_inc(ld_ctx, 16)

            follow(0, 0)
            with sp.Fori(0, NCH - 1) as c:
                follow(c + 1, c)
            load_context(NCH, NCH - 1)
            keep(NCH)
            sp.wait_ge(x1_kept, 16 * (NCH + 1) + ONE)
            sp.wait_ge(x1T_kept, 16 * (NCH + 1) + ONE)
            sp.wait_ge(g_copied, NCH + 2)
            sp.wait_ge(m_ready, 1)
            sp.dma_start(m_dram, mrow[:]).then_inc(m_stored, 16)
            sp.wait_ge(m_stored, 16)
            m_v = m_dram.rearrange("(c n) (j s) -> j c n s", n=TB * H, j=2)
            c_blocks = ctx_tok.rearrange("(c b p) d -> p c b d", p=P, b=TB)

            def load_m(c, again=True):
                if again:
                    sp.wait_ge(lm1, c)
                    close_wait(sp)
                for j in range(2):
                    sp.dma_start(mb.rearrange("p (m s) -> p m s", s=S)[64 * j:64 * j + 64],
                                 m_v[j, ds(c, 1)].broadcast_to([64, TB * H, S])).then_inc(b_mb, 16)

            def load_T(c, again=True):
                if again:
                    sp.wait_ge(qk_done, c)
                    close_wait(sp)
                sp.dma_start(x1Tc[:], x1T_all[:, ds(c * CH + CH, CH)]).then_inc(b_x1T, 16)
                sp.dma_start(cTc[:], ctx_T[:, ds(c * CH, CH)]).then_inc(b_x1T, 16)

            def load_v(c, again=True):
                if again:
                    sp.wait_ge(av_done, c)
                    close_wait(sp)
                for b in range(TB):
                    sp.dma_start(V1[:, H * b:H * b + H, 0:S // 2],
                                 c_blocks[:, ds(c, 1), b].rearrange("p c (h e) -> p (c h) e", h=H)).then_inc(b_v, 16)

            def load_x1(c, again=True):
                if again:
                    sp.wait_ge(zb_done, c)
                    close_wait(sp)
                sp.dma_start(x1c[:], x1_all[:, ds(c + 1, 1)].rearrange("p c b d -> p (c b) d")).then_inc(b_x1, 16)

            def keep_x2(c):
                sp.wait_ge(x2_done, c + 1)
                close_wait(sp)
                sp.dma_start(x2_all[:, ds(c * CH, CH)].rearrange("p (b d) -> p b d", b=TB),
                             x2_st[:]).then_inc(x2_kept, 16)

            load_m(0, again=False)
            load_T(0, again=False)
            load_v(0, again=False)
            load_x1(0, again=False)
            load_m(1)
            load_T(1)
            load_v(1)
            load_m(2)
            with sp.Fori(0, NCH - 3) as c:
                load_T(c + 2)
                load_v(c + 2)
                load_x1(c + 1)
                keep_x2(c)
                load_m(c + 3)
            for c in range(NCH - 3, NCH):
                if c + 2 < NCH:
                    load_T(c + 2)
                    load_v(c + 2)
                if c + 1 < NCH:
                    load_x1(c + 1)
                keep_x2(c)
                if c == NCH - 3:
                    sp.wait_ge(a_ready, NCH * N + 2)
                    sp.dma_start(w1_sb, w1.rearrange("e d f -> d e f")).then_inc(ld_f, 16)
                    sp.wait_ge(u_done, NCH * N + 1)
                    sp.dma_start(w3_sb, w3.rearrange("e d f -> d e f")).then_inc(ld_f, 16)
                if c == NCH - 2:
                    sp.wait_ge(b_x1T, 32 * NCH)
                    sp.dma_start(w2_sb, w2.rearrange("e (b p) d -> p e b d", p=P)).then_inc(ld_f, 16)
            sp.wait_ge(tab_done, 1)
            sp.dma_start(xg_dram[E * REG:, :].rearrange("(n p) r -> p n r", p=P),
                         zrow[:, E:]).then_inc(zero_out, 16)
            zero_rows(sp, range(0, E // 2))
            sp.wait_ge(zero_out, 16 * (E + 1))
            sp.wait_ge(sc_sem, 128 * NCH + 16)
            sp.wait_ge(x2_kept, 16 * NCH + ONE)

            def load_x(q, slot):
                i = 4 * q + slot
                row = sp.value_load(rowt[0:1, ds(i, 1)], min_val=0, max_val=E * REG + (SPARE - 1) * P)
                sp.wait_ge(xT_tr, i - 3 + 4)
                close_wait(sp)
                sp.dma_start(xin[:, slot % 4], xg_dram[ds(row, P), 0:D]).then_inc(x_in[slot % 4], 16)

            def load_meta(q, slot):
                i = 4 * q + slot
                row = sp.value_load(rowt[0:1, ds(i, 1)], min_val=0, max_val=E * REG + (SPARE - 1) * P)
                sp.wait_ge(y_out[slot % 4], 16 * (q + slot // 4 + 1))
                close_wait(sp)
                sp.dma_start(meta[:, slot % 4], xg_dram[ds(row, P), D:ROW]).then_inc(m_in[slot % 4], 16)

            sp.wait_ge(tab_done, 2)
            load_x(0, 0)
            with sp.Fori(0, NTIL // 4) as it:
                for r in range(4):
                    i = it * 4 + r
                    load_x(it, r + 1)
                    load_meta(it, r)
            for r in range(4):
                sp.wait_ge(y_out[r], 16 * (NTIL // 4 + 1))
            for c in range(NCH):
                sp.dma_start(y0_all[:, c * CH:(c + 1) * CH].rearrange(v4, b=TB), y_blocks[0][:, c]).then_inc(y_in[c], 16)
            for c in range(NCH):
                sp.wait_ge(fz, c + 1)
                sp.dma_start(out_blocks[:, c], y1_all[:, c * CH:(c + 1) * CH].rearrange(v4, b=TB)).then_inc(s_out, 16)
            sp.wait_ge(s_out, 16 * NCH)

        @block.gpsimd
        def _(pool):
            nc.gpsimd.memset(part_id[:], 0.0).then_inc(s_memset, 1)
            nc.gpsimd.memset(ident[:], 0.0).then_inc(s_memset, 1)
            nc.gpsimd.memset(eps5[:], 1e-5).then_inc(s_ident, 1)
            pool.wait_ge(s_memset, 2)
            for part in range(3):
                if part:
                    pool.wait_ge(s_part, part)
                v = part_id[2 * N * part:2 * N * (part + 1)]
                nc.gpsimd.affine_select(out=v, in_=v, compare_op=ALU.not_equal, fill=1.0, base=0,
                                        pattern=[[-1, 2 * N]], channel_multiplier=1).then_inc(s_part, 1)
            pool.wait_ge(s_part, 3)
            nc.gpsimd.affine_select(out=ident[:], in_=ident[:], compare_op=ALU.not_equal, fill=1.0, base=0,
                                    pattern=[[-1, P]], channel_multiplier=1).then_inc(s_ident, 1)
            pool.wait_ge(s_ident, 2)
            nc.gpsimd.tensor_scalar(center[:], ident[:], -1.0 / D, None, ALU.add).then_inc(s_ident, 1)

            def spread_and_split(it, r):
                c = 2 * it + r
                tok = ds(c * CH, CH)
                pool.wait_ge(s_dl, c + 1)
                pool.wait_ge(s_b4, c + 2)
                close_wait(pool)
                nc.gpsimd.tensor_tensor(dx[:, tok], decay[:, tok], xT[:, tok], ALU.mult).then_inc(s_dx, 1)
                pool.wait_ge(s_b3, c + 1)
                pool.wait_ge(s_dx, c + 1)
                close_wait(pool)
                nc.gpsimd.tensor_tensor(bcs[64:96, tok], res1[:, r], b3t[:, r], ALU.subtract).then_inc(s_b4, 1)

            nc.gpsimd.memset(dx[:, T:], 0.0).then_inc(s_const, 1)
            nc.gpsimd.memset(decay[:, T:], 0.0).then_inc(s_const, 1)
            nc.gpsimd.memset(hc[:, DEPTH - LAG:], 0.0).then_inc(hc_done, DEPTH)
            pool.wait_ge(s_const, 2)
            pool.wait_ge(hc_done, DEPTH)
            nc.gpsimd.memset(bcs[:, T:], 0.0).then_inc(s_const, 1)
            pool.wait_ge(s_const, 3)
            pool.wait_ge(ld_x, 96)
            with pool.Fori(0, NCH // 2) as it:
                for r in range(2):
                    spread_and_split(it, r)
            pool.wait_ge(s_b4, NCH + 2)

            def residual(c):
                pool.wait_ge(ld_chunk, 16 * (c + 1))
                pool.wait_ge(z_done, c + ONE)
                pool.wait_ge(s_proj, 1)
                nc.gpsimd.tensor_tensor(xc[:], xbuf[:], cvec[:].unsqueeze(1).to_broadcast([P, TB, D]),
                                        ALU.add).then_inc(xc_done, 1)

            with pool.Fori(0, NCH) as c:
                for n in range(N):
                    k = c * N + n
                    if n == 1:
                        residual(c)
                    pool.wait_ge(h_done, k + 1 + 2)
                    pool.wait_ge(C_copied, k + 1)
                    pool.wait_ge(y_acc, k + 1)
                    nc.gpsimd.tensor_tensor(hc[:, n % DEPTH], h[:, n % DEPTH], c_sb[:, n % DEPTH],
                                            ALU.mult).then_inc(hc_done, 1)
            residual(NCH)
            pool.wait_ge(hc_done, NCH * N + DEPTH)
            pool.wait_ge(y_acc, NCH * N + 4)
            nc.gpsimd.memset(tri[:], 1.0).then_inc(g_const, 1)
            nc.gpsimd.memset(fence[:], 0.0).then_inc(g_const, 1)
            nc.gpsimd.memset(maskT[:], 0.0).then_inc(g_const, 1)
            nc.gpsimd.memset(V1[:, :, S // 2:], 1.0).then_inc(g_const, 1)
            nc.gpsimd.memset(zrow[:, :, 0:D], 0.0).then_inc(g_const, 1)
            nc.gpsimd.memset(zrow[:, :, D + 1:], 0.0).then_inc(g_const, 1)
            nc.gpsimd.memset(ones[:], 1.0).then_inc(g_const, 1)
            nc.gpsimd.memset(onesf[:], 1.0).then_inc(g_const, 1)
            nc.gpsimd.memset(tri_s[:], 1.0).then_inc(g_const, 1)
            pool.wait_ge(g_const, 9)
            nc.gpsimd.memset(fence[:, 0:P:S], -BIG).then_inc(g_const, 1)
            imprecise = dict(allow_small_or_imprecise_dtypes=True)
            nc.gpsimd.iota(rank[:], pattern=[[-1, E]], base=E, channel_multiplier=0, **imprecise).then_inc(g_const, 1)
            nc.gpsimd.iota(regbase[:], pattern=[[REG, E]], base=0, channel_multiplier=0, **imprecise).then_inc(g_const, 1)
            nc.gpsimd.iota(carry[:], pattern=[[REG, E]], base=0, channel_multiplier=0, **imprecise).then_inc(g_const, 1)
            nc.gpsimd.iota(destf[:], pattern=[[T, K2], [P, TB]], base=0, channel_multiplier=1,
                           **imprecise).then_inc(g_const, 1)
            nc.gpsimd.iota(kstep[:], pattern=[[0, E], [P, T // P]], base=0, channel_multiplier=0,
                           **imprecise).then_inc(g_const, 1)
            nc.gpsimd.iota(tix[:], pattern=[[1, NTAB]], base=0, channel_multiplier=0, **imprecise).then_inc(g_const, 1)
            nc.gpsimd.iota(zrow[:, :, D].bitcast(i32), pattern=[[P, E + SPARE]], base=K2 * T,
                           channel_multiplier=1).then_inc(g_const, 1)
            nc.gpsimd.affine_select(out=tri_s[:], in_=tri_s[:], compare_op=ALU.is_gt, fill=0.0, base=0,
                                    pattern=[[1, P]], channel_multiplier=-1).then_inc(g_const, 1)
            nc.gpsimd.affine_select(out=tri[:], in_=tri[:], compare_op=ALU.is_ge, fill=0.0, base=0,
                                    pattern=[[1, P]], channel_multiplier=-1).then_inc(g_const, 1)
            pool.wait_ge(g_const, 19)
            nc.gpsimd.memset(tri[0:S, S:P], 0.0).then_inc(g_const, 1)
            pool.wait_ge(g_const, 20)
            for j in range(2):
                nc.gpsimd.affine_select(out=maskT[S * j:S * j + S], in_=maskT[S * j:S * j + S], compare_op=ALU.is_ge,
                                        fill=-BIG, base=0, pattern=[[1, S]],
                                        channel_multiplier=-1).then_inc(g_const, 1)
                pool.wait_ge(g_const, 21 + j)
            nothing = bass.IndirectOffsetOnAxis(ap=zrow[:, 0, D:D + 1].bitcast(i32), axis=0)
            nc.gpsimd.indirect_dma_start(out=xg_dram, out_offset=nothing, in_=zrow[:, 0], in_offset=None).then_inc(sc_sem, 16)
            for ahead in range(4):
                nc.gpsimd.indirect_dma_start(out=y2_dram, out_offset=nothing, in_=zrow[:, 0, 0:D],
                                             in_offset=None).then_inc(y_out[ahead], 16)
                pool.wait_ge(y_out[ahead], 16)
            pool.wait_ge(sc_sem, 16)
            v16 = [P, TB * H, S]

            def start_mask(c):
                pool.wait_ge(b_mb, 32 * c + 32)
                pool.wait_ge(D_done, c + ONE)
                nc.gpsimd.tensor_tensor(lmask.rearrange("p (m s) -> p m s", s=S), maskT[:].unsqueeze(1).to_broadcast(v16),
                                        mb.rearrange("p (m s) -> p m s", s=S), ALU.subtract).then_inc(lm1, 1)

            def send_rows(c):
                pool.wait_ge(rows_done, c + 1 + ONE)
                pool.wait_ge(idx_done, c + 1)
                close_wait(pool)
                for k in range(K2):
                    for b in range(TB):
                        m = k * TB + b
                        nc.gpsimd.indirect_dma_start(
                            out=xg_dram, out_offset=bass.IndirectOffsetOnAxis(ap=idx[:, m:m + 1], axis=0),
                            in_=x2r[:, k, b], in_offset=None).then_inc(sc_sem, 16)

            for c in range(3):
                start_mask(c)
            with pool.Fori(0, NCH - 3) as c:
                start_mask(c + 3)
                send_rows(c)
            for c in range(NCH - 3, NCH):
                send_rows(c)

            def scatter(q, slot):
                i = 4 * q + slot
                pool.wait_ge(y_cp, i + 1 + 2)
                pool.wait_ge(m_in[slot % 4], 16 * (q + slot // 4 + 1))
                close_wait(pool)
                nc.gpsimd.indirect_dma_start(
                    out=y2_dram, out_offset=bass.IndirectOffsetOnAxis(ap=meta[:, slot % 4, 0:1].bitcast(i32), axis=0),
                    in_=yt[:, slot % 4], in_offset=None).then_inc(y_out[slot % 4], 16)

            with pool.Fori(0, NTIL // 4) as it:
                for r in range(4):
                    scatter(it, r)
            for c in range(NCH):
                pool.wait_ge(y_in[c], 32)
                tok = slice(c * CH, (c + 1) * CH)
                nc.gpsimd.tensor_tensor(x2_all[:, tok], x2_all[:, tok], y1_all[:, tok], ALU.add).then_inc(res_done, 1)

        @block.tensor
        def _(pe):

            def rank_product(c, r):
                pe.wait_ge(s_dts, c + 1)
                close_wait(pe)
                nc.tensor.matmul(pa[0:R, r], wdtw[:], xT[:, ds(c * CH, CH)], start=True, stop=True).then_inc(s_dtp, 1)

            def bc_delta(c, r):
                pe.wait_ge(s_dts, c + 1 + 2)
                pe.wait_ge(s_abs, c + 1)
                pe.wait_ge(s_rel, c + 1)
                nc.tensor.matmul(pB[:, r], wdt[:], dt_sb[:, r], start=True, stop=True).then_inc(s_pre, 1)
                pe.wait_ge(s_b2, c + 1)
                close_wait(pe)
                nc.tensor.matmul(pC[0:2 * N, r], wbc[:], xT[:, ds(c * CH, CH)], start=True, stop=True).then_inc(s_bcp, 1)

            pe.wait_ge(ld_x, 96)
            rank_product(0, 0)
            with pe.Fori(0, NCH // 2 - 1) as it:
                for r in range(2):
                    rank_product(2 * it + r + 1, (r + 1) % 2)
                    bc_delta(2 * it + r, r)
            rank_product(NCH - 1, 1)
            bc_delta(NCH - 2, 0)
            bc_delta(NCH - 1, 1)
            pe.wait_ge(s_setup_pe, 1)
            nc.tensor.matmul(pq[:, 0:D], center[:], gw[:], start=True, stop=True)
            nc.tensor.matmul(pq[:, D:2 * D], lnb_rep[:], wout[:], start=True, stop=True).then_inc(s_const2, 1)
            pe.wait_ge(s_proj, 1)

            def spread(k, n, tok):
                nc.tensor.matmul(pB[:, n % 2], sel[:, n, :], bcs[:, tok], start=True, stop=True).then_inc(B_ready, 1)

            def spread_c(k, n, tok):
                nc.tensor.matmul(pC[:, n % 2], sel[:, N + n, :], bcs[:, tok], start=True, stop=True).then_inc(C_ready, 1)

            pe.wait_ge(s_b4, NCH + 2)
            pe.wait_ge(s_b2, NCH + 2)
            pe.wait_ge(s_abs, NCH + 2)
            pe.wait_ge(s_rel, NCH + 2)
            pe.wait_ge(s_dec, 1)
            pe.wait_ge(s_const, 3)
            pe.wait_ge(s_sel, 1)
            for n in range(2):
                spread(n, n, slice(0, CH))
                spread_c(n, n, slice(0, CH))

            def project(c, half):
                pe.wait_ge(y_copied, c + 1)
                if half == 1:
                    pe.wait_ge(st_done, 2 * c + 1)
                    pe.wait_ge(p_copied, 2 * c + 1)
                else:
                    pe.wait_ge(g_copied, c + 1)
                for b in range(2):
                    last = nc.tensor.matmul(pq[:, b * 2 * D:(b + 1) * 2 * D], y_sb[:, (2 * half + b) * P:(2 * half + b + 1) * P],
                                            proj[:], start=True, stop=True)
                last.then_inc(p_done, 1)

            def transposes(c):
                pe.wait_ge(x1_done, c + 1)
                pe.wait_ge(st_done, 2 * c + 2)
                pe.wait_ge(p_copied, 2 * c + 2)
                for b in range(TB):
                    last = nc.tensor.transpose(pq[:, b * P:(b + 1) * P], x1_st[:, b], ident[:])
                last.then_inc(x1T_done, 1)

            def gate_products(c, blocks):
                pe.wait_ge(x1T_copied, c + ONE)
                pe.wait_ge(ld_ctx, 16 * (c + 1))
                for b in blocks:
                    o = pq[:, b * 2 * H:(b + 1) * 2 * H]
                    nc.tensor.matmul(o, x1T_st[:, b * P:(b + 1) * P], gk[:, 0], start=True, stop=False)
                    last = nc.tensor.matmul(o, cT_st[:, b * P:(b + 1) * P], gkv[:], start=False, stop=True)
                if blocks[-1] == TB - 1:
                    last.then_inc(g_done, 1)

            def tail(c, n):
                if n in (1, 2):
                    gate_products(c, range(2 * (n - 1), 2 * n))
                if n == 4:
                    project(c, 0)
                if n == 6:
                    project(c, 1)
                if n == 15:
                    transposes(c)

            def sum_state(k, m):
                pe.wait_ge(hc_done, k - LAG + 1 + DEPTH)
                nc.tensor.matmul(py[:], ident[:], hc[:, m % DEPTH], start=(m == 0), stop=(m == N - 1)).then_inc(y_acc, 1)

            pe.wait_ge(hc_done, DEPTH)
            nc.tensor.matmul(py[:], ident[:], hc[:, DEPTH - 1], start=True, stop=False)

            with pe.Fori(0, NCH) as c:
                for n in range(N):
                    k = c * N + n
                    nxt = ds(c * CH, CH) if n < N - 2 else ds(c * CH + CH, CH)
                    m = (n + 2) % N
                    pe.wait_ge(u_done, k + 1)
                    spread(k + 2, m, nxt)
                    pe.wait_ge(C_copied, k + 1)
                    spread_c(k + 2, m, nxt)
                    if n == LAG:
                        tail(c, n)
                        pe.wait_ge(y_copied, c + 1)
                    if n == N - 4:
                        close_wait(pe)
                        nc.tensor.matmul(py[:], diag_dp[:], xT[:, ds(c * CH, CH)], start=False, stop=False)
                    sum_state(k, (n - LAG) % N)
                    if n != LAG:
                        tail(c, n)
            for n in range(N):
                tail(NCH, n)
                if n < LAG:
                    sum_state(NCH * N + n, N - LAG + n)
            tail(NCH + 1, 1)
            tail(NCH + 1, 2)
            pe.wait_ge(gate_step, 1)
            pe.wait_ge(g_const, 22)
            nc.tensor.matmul(pq[:, 0:NG], tri[:], lfg[:], start=True, stop=True).then_inc(gate_step, 1)
            pe.wait_ge(gate_step, 3)
            nc.tensor.transpose(pC[:, 0, 0:P], g_sb[:], ident[:]).then_inc(gate_step, 1)
            pe.wait_ge(gate_step, 5)
            nc.tensor.transpose(pC[:, 1, 0:P], mrow[:], ident[:]).then_inc(gate_step, 1)
            pe.wait_ge(E_ready, 1)
            HD = D // H

            def scores(c, heads):
                if heads[0] == 0:
                    pe.wait_ge(b_x1T, 32 * c + 32)
                    pe.wait_ge(C_done, c + ONE)
                for hh in heads:
                    bank = (pa if hh < 2 else pB)[:, hh % 2]
                    rows = slice(HD * hh, HD * hh + HD)
                    for b in range(TB):
                        for j in range(2):
                            t0 = b * P + S * j
                            last = nc.tensor.matmul(bank[S * j:S * j + S, b * S:b * S + S], cTc[rows, t0:t0 + S],
                                                    x1Tc[rows, t0:t0 + S], start=True, stop=True)
                if heads[-1] == H - 1:
                    last.then_inc(qk_done, 1)

            def weighted_values(c):
                pe.wait_ge(C_done, c + 1 + ONE)
                pe.wait_ge(b_v, 16 * TB * (c + 1))
                pe.wait_ge(hv_done, c + ONE)
                close_wait(pe)
                for b in range(TB):
                    for j in range(2):
                        for hh in range(H):
                            m = b * H + hh
                            last = nc.tensor.matmul(pC[S * j:S * j + S, b // 2, ((b % 2) * H + hh) * (HD + 1):((b % 2) * H + hh + 1) * (HD + 1)],
                                                    Cm[S * j:S * j + S, m * S:m * S + S], V1[S * j:S * j + S, m],
                                                    start=True, stop=True)
                last.then_inc(av_done, 1)

            def turn_x2(c):
                pe.wait_ge(x2_done, c + 1)
                pe.wait_ge(lg_copied, c + ONE)
                for b in range(TB):
                    last = nc.tensor.transpose(pq[:, b * P:(b + 1) * P], x2_st[:, b], ident[:])
                last.then_inc(x2T_done, 1)

            def logits(c):
                pe.wait_ge(x2T_copied, c + 1)
                for b in range(TB):
                    last = nc.tensor.matmul(py[:, b * E:(b + 1) * E], x2T_st[:, b * P:(b + 1) * P], rw[:], start=True,
                                            stop=True)
                last.then_inc(lg_done, 1)

            def ranks(c):
                pe.wait_ge(mask_done, c + 1)
                nc.tensor.matmul(pq[:, 0:TB * E], tri_s[:], mask[:].rearrange("p b e -> p (b e)"), start=True, stop=False)
                for b in range(TB):
                    left = TB - 1 - b
                    if left:
                        nc.tensor.matmul(pq[:, (b + 1) * E:TB * E].rearrange("p (b e) -> p b e", e=E), ones[:],
                                         mask[:, b].unsqueeze(1).to_broadcast([P, left, E]), start=False, stop=left == 1)
                for b in range(TB):
                    last = nc.tensor.matmul(py[:, TB * E:(TB + 1) * E], ones[:], mask[:, b], start=(b == 0),
                                            stop=(b == TB - 1))
                last.then_inc(rk_done, 1)

            def attend_round(c, front=True, back=True):
                if back:
                    turn_x2(c - 1)
                if front:
                    scores(c + 1, range(0, 1))
                if back:
                    logits(c - 1)
                if front:
                    scores(c + 1, range(1, H))
                    weighted_values(c + 1)
                if back:
                    ranks(c - 1)

            attend_round(-1, back=False)
            attend_round(0, back=False)
            with pe.Fori(0, NCH - 2) as c:
                attend_round(c + 1)
            attend_round(NCH - 1, front=False)
            attend_round(NCH, front=False)
            pe.wait_ge(ld_f, 64)
            pe.wait_ge(tab_done, 2)
            tiles = dict(min_val=0, max_val=(E - 1) * F)

            def up(q, slot):
                i = 4 * q + slot
                eo = pe.value_load(eoff[0:1, ds(i, 1)], **tiles)
                pe.wait_ge(xT_cp, i + 1)
                pe.wait_ge(mul_done, i - 1 + 2)
                close_wait(pe)
                lhs = xgT[:, slot % 4]
                nc.tensor.matmul(pa[:, slot % 2], lhs, w1_flat[:, ds(eo, F)], start=True, stop=True)
                nc.tensor.matmul(pB[:, slot % 2], lhs, w3_flat[:, ds(eo, F)], start=True, stop=True).then_inc(up_done, 1)

            def turn_h(q, slot):
                i = 4 * q + slot
                pe.wait_ge(mul_done, i + 1 + 2)
                pe.wait_ge(hT_cp, i + ONE)
                for f in range(FB):
                    last = nc.tensor.transpose(pC[:, 0, f * P:(f + 1) * P], hs[:, slot % 2, f * P:(f + 1) * P], ident[:])
                last.then_inc(hT_tr, 1)

            def down(q, slot):
                i = 4 * q + slot
                eo = pe.value_load(eoff[0:1, ds(i, 1)], **tiles)
                pe.wait_ge(hT_cp, i + 1 + ONE)
                pe.wait_ge(y_cp, i - 1 + 2)
                close_wait(pe)
                o = (pC[:, 1] if slot % 2 else py[:])[:, 0:D]
                for f in range(FB):
                    last = nc.tensor.matmul(o, hT[:, slot % 2, f * P:(f + 1) * P], w2_flat[:, ds(eo + f * D, D)],
                                            start=(f == 0), stop=(f == FB - 1))
                last.then_inc(dn_done, 1)

            def turn_x(q, slot):
                i = 4 * q + slot
                pe.wait_ge(x_in[slot % 4], 16 * (q + slot // 4 + 1))
                pe.wait_ge(xT_cp, i)
                nc.tensor.transpose(pq[:, 0:P], xin[:, slot % 4], ident[:]).then_inc(xT_tr, 1)

            pe.wait_ge(x_in[0], 16)
            nc.tensor.transpose(pq[:, 0:P], xin[:, 0], ident[:]).then_inc(xT_tr, 1)
            turn_x(0, 1)
            up(0, 0)
            up(0, 1)
            turn_h(0, 0)
            turn_x(0, 2)
            UNROLL = 8
            looped = (NTIL - 4) // UNROLL
            with pe.Fori(0, looped) as it:
                for r in range(UNROLL):
                    up(it * (UNROLL // 4), r + 2)
                    turn_x(it * (UNROLL // 4), r + 3)
                    turn_h(it * (UNROLL // 4), r + 1)
                    down(it * (UNROLL // 4), r)
            for i in range(looped * UNROLL + 1, NTIL):
                if i + 1 < NTIL:
                    up(0, i + 1)
                if i + 2 < NTIL:
                    turn_x(0, i + 2)
                turn_h(0, i)
                down(0, i - 1)
            down(0, NTIL - 1)

        @block.scalar
        def _(act):
            nc.scalar.preload_act_table_set("natural_log_exp_and_others")
            act.dma_start(xT[:, T // 2:], x_T[:, T // 2:]).then_inc(ld_x, 16)

            def copy_rank(c, r):
                act.wait_ge(s_dtp, c + 1)
                act.wait_ge(s_pre, c + 1)
                nc.scalar.copy(dt_sb[:, r], pa[0:R, r]).then_inc(s_dts, 1)

            def softplus(c, r):
                act.wait_ge(s_pre, c + 1 + 2)
                act.wait_ge(s_rel, c + 1 + 2)
                nc.scalar.activation(pabs[r], pB[:, r], ACT.Abs, bias=bdt[:]).then_inc(s_abs, 1)
                act.wait_ge(s_abs, c + 1 + 2)
                nc.scalar.activation(pexp[r], pabs[r], ACT.Exp, scale=-1.0).then_inc(s_ex, 1)
                act.wait_ge(s_ex, c + 1)
                nc.scalar.activation(plog[r], pexp[r], ACT.Ln, bias=1.0).then_inc(s_log, 1)

            copy_rank(0, 0)
            with act.Fori(0, NCH // 2 - 1) as it:
                for r in range(2):
                    copy_rank(2 * it + r + 1, (r + 1) % 2)
                    softplus(2 * it + r, r)
            copy_rank(NCH - 1, 1)
            softplus(NCH - 2, 0)
            softplus(NCH - 1, 1)
            act.wait_ge(ld_w, 16 * LW)
            nc.scalar.activation(Aneg[:], alog[:], ACT.Exp).then_inc(s_aexp, 1)

            def decay_exp(n, tok):
                close_wait(act)
                nc.scalar.activation(pa[:, n % 2], decay[:, tok], ACT.Exp, scale=Aneg[:, n:n + 1]).then_inc(a_ready, 1)

            def copy_c(n):
                nc.scalar.copy(c_sb[:, n % DEPTH], pC[:, n % 2]).then_inc(C_copied, 1)

            act.wait_ge(s_dec, 1)
            act.wait_ge(s_A, 2)
            act.wait_ge(s_b4, NCH + 2)
            act.wait_ge(s_const, 3)
            for n in range(2):
                decay_exp(n, slice(0, CH))
                act.wait_ge(C_ready, n + 1)
                copy_c(n)

            def tail(c, n):
                if n == 1:
                    act.wait_ge(y_acc, c * N + 4)
                    act.wait_ge(p_done, 2 * c + ONE)
                    nc.scalar.copy(y_sb[:], py[:]).then_inc(y_copied, 1)
                if n in (5, 7):
                    half = (n - 5) // 2
                    act.wait_ge(p_done, 2 * c + half + 1 + ONE)
                    act.wait_ge(z_done, c + ONE)
                    act.wait_ge(st_done, 2 * c + half + 1)
                    nc.scalar.copy(p_sb[:, 2 * half:2 * half + 2], pq[:].rearrange("p (b e) -> p b e", b=2)[:, :, 0:D]
                                   ).then_inc(p_copied, 1)
                if n == 8:
                    act.wait_ge(mv_done, c + 1 + ONE)
                    act.wait_ge(z_done, c + ONE)
                    nc.scalar.activation(lv[:], mv[:, :, 1], ACT.Ln, bias=eps5[:]).then_inc(lv_done, 1)
                    act.wait_ge(lv_done, c + 1)
                    nc.scalar.activation(rstd[:], lv[:], ACT.Exp, scale=-0.5).then_inc(rs_done, 1)
                if n == 12:
                    act.wait_ge(mv2_done, c + 1)
                    nc.scalar.activation(lv2[:], mv2[:, :, 1], ACT.Ln, bias=eps5[:]).then_inc(lv2_done, 1)
                    act.wait_ge(lv2_done, c + 1)
                    nc.scalar.activation(rstd2[:], lv2[:], ACT.Exp, scale=-0.5).then_inc(rs2_done, 1)
                if n == 15:
                    act.wait_ge(x1T_done, c + 1 + ONE)
                    act.wait_ge(x1T_kept, 16 * c + ONE)
                    nc.scalar.copy(x1T_st[:], pq[:]).then_inc(x1T_copied, 1)

            with act.Fori(0, NCH) as c:
                for n in range(N):
                    k = c * N + n
                    nxt = ds(c * CH, CH) if n < N - 2 else ds(c * CH + CH, CH)
                    act.wait_ge(h_done, k + 1 + 2)
                    decay_exp((n + 2) % N, nxt)
                    act.wait_ge(C_ready, k + 3)
                    act.wait_ge(hc_done, k + 3)
                    copy_c((n + 2) % N)
                    tail(c, n)
            for n in range(N):
                tail(NCH, n)
            act.wait_ge(g_copied, NCH + 2)
            fg = gates[:, 2:].rearrange("p c b g -> p (c b) g")[:, :, H:2 * H]
            v3 = "p (n h) -> p n h"
            nc.scalar.activation(gabs[:].rearrange(v3, h=H), fg, ACT.Abs).then_inc(act_step, 1)
            act.wait_ge(act_step, 1)
            nc.scalar.activation(gexp[:], gabs[:], ACT.Exp, scale=-1.0).then_inc(act_step, 1)
            act.wait_ge(act_step, 2)
            nc.scalar.activation(glog[:], gexp[:], ACT.Ln, bias=1.0).then_inc(act_step, 1)
            act.wait_ge(gate_step, 7)
            nc.scalar.activation(floor_[:], nlog[:], ACT.Exp, scale=-1.0).then_inc(E_ready, 1)

            def attend_round(c, front=True, middle=True, back=True):
                if back:
                    act.wait_ge(x2T_done, c + ONE)
                    nc.scalar.copy(x2T_st[:], pq[:]).then_inc(x2T_copied, 1)
                if front:
                    act.wait_ge(lm2, c + 2 + ONE)
                    act.wait_ge(C_done, c + 1 + ONE)
                    nc.scalar.activation(Dm, lmask, ACT.Exp).then_inc(D_done, 1)
                if middle:
                    act.wait_ge(cen_done, c + 1)
                    nc.scalar.activation(sq[:], cen[:], ACT.Square).then_inc(sq_done, 1)
                    act.wait_ge(vsum_done, c + 1)
                    nc.scalar.activation(vlog[:], vsum[:], ACT.Ln, scale=float(H) / D, bias=eps5[:]).then_inc(vlog_done, 1)
                    act.wait_ge(vlog_done, c + 1)
                    nc.scalar.activation(vrs[:], vlog[:], ACT.Exp, scale=-0.5).then_inc(vrs_done, 1)
                if back:
                    act.wait_ge(sc_sem, 128 * (c - 1) + 16)
                    nc.scalar.copy(x2r[:, 0, :, 0:D], x2_st[:])
                    nc.scalar.copy(x2r[:, 1, :, 0:D], x2_st[:]).then_inc(rows_done, 1)
                    act.wait_ge(r_step, NR * (c - 1) + RS)
                    nc.scalar.activation(share[:, 1], share[:, 0], ACT.Exp).then_inc(r_exp, 1)
                if middle:
                    act.wait_ge(mvb_done, c + 1)
                    nc.scalar.activation(lv[:], mv[:, :, 1], ACT.Ln, bias=eps5[:]).then_inc(lvb_done, 1)
                    act.wait_ge(lvb_done, c + 1)
                    nc.scalar.activation(rstd[:], lv[:], ACT.Exp, scale=-0.5).then_inc(rsb_done, 1)

            attend_round(-1, middle=False, back=False)
            attend_round(0, back=False)
            with act.Fori(0, NCH - 2) as c:
                attend_round(c + 1)
            attend_round(NCH - 1, front=False)
            attend_round(NCH, front=False, middle=False)

            def gate_act(q, slot):
                i = 4 * q + slot
                act.wait_ge(up_done, i + 1)
                act.wait_ge(mul_done, i - 1 + 2)
                nc.scalar.activation(sil[:, slot % 2], pa[:, slot % 2], ACT.Silu).then_inc(sil_done, 1)

            def copy_hT(q, slot):
                i = 4 * q + slot
                act.wait_ge(hT_tr, i + 1)
                act.wait_ge(dn_done, i - 1 + 1)
                nc.scalar.copy(hT[:, slot % 2], pC[:, 0]).then_inc(hT_cp, 1)

            def weigh(q, slot):
                i = 4 * q + slot
                act.wait_ge(dn_done, i + 1 + 1)
                act.wait_ge(m_in[slot % 4], 16 * (q + slot // 4 + 1))
                act.wait_ge(y_out[slot % 4], 16 * (q + slot // 4 + 1))
                o = (pC[:, 1] if slot % 2 else py[:])[:, 0:D]
                nc.scalar.activation(yt[:, slot % 4], o, ACT.Copy, scale=meta[:, slot % 4, 1:2]).then_inc(y_cp, 1)

            act.wait_ge(tab_done, 1)
            zero_rows(act, range(E // 2, E))
            gate_act(0, 0)
            gate_act(0, 1)
            copy_hT(0, 0)
            with act.Fori(0, (NTIL - 4) // 4) as it:
                for r in range(4):
                    i = it * 4 + 1 + r
                    gate_act(it, r + 2)
                    copy_hT(it, r + 1)
                    weigh(it, r)
            for i in range(NTIL - 3, NTIL):
                if i + 1 < NTIL:
                    gate_act(0, i + 1)
                copy_hT(0, i)
                weigh(0, i - 1)
            weigh(0, NTIL - 1)
            nc.scalar.preload_act_table_set("natural_log_exp_and_others")
            for r in range(4):
                act.wait_ge(y_out[r], 16 * (NTIL // 4 + 1))
            for c in range(NCH):
                act.dma_start(y1_all[:, c * CH:(c + 1) * CH].rearrange(v4, b=TB), y_blocks[1][:, c]).then_inc(y_in[c], 16)

            def scale_rows(c):
                act.wait_ge(fnm, c + 1)
                act.wait_ge(res_done, c + 1)
                for b in range(TB):
                    rows = slice((c * TB + b) * D, (c * TB + b + 1) * D)
                    last = nc.scalar.activation(y1_all[:, rows], y0_all[:, rows], ACT.Identity,
                                                scale=last_rs[c % 2][:, b:b + 1], bias=last_nm[:, c % 2, b:b + 1])
                last.then_inc(fz, 1)

            for c in range(NCH):
                act.wait_ge(fmv, c + 1)
                if c >= 2:
                    act.wait_ge(fz, c - 1)
                nc.scalar.activation(last_lv[c % 2][:], last_mv[c % 2][:, :, 1], ACT.Ln, bias=eps5[:]).then_inc(flv, 1)
                act.wait_ge(flv, c + 1)
                nc.scalar.activation(last_rs[c % 2][:], last_lv[c % 2][:], ACT.Exp, scale=-0.5).then_inc(frs, 1)
                if c:
                    scale_rows(c - 1)
            scale_rows(NCH - 1)

        @block.vector
        def _(dve):

            def split(c, r):
                tok = ds(c * CH, CH)
                dve.wait_ge(s_pre, c + 1 + 2)
                nc.vector.tensor_scalar(prel[r], pB[:, r], bdt[:], 0.0, ALU.add, ALU.max).then_inc(s_rel, 1)
                dve.wait_ge(s_bcp, c + 1)
                close_wait(dve)
                nc.vector.tensor_copy(bcs[0:32, tok], pC[0:2 * N, r]).then_inc(s_b1, 1)
                dve.wait_ge(s_b1, c + 1)
                dve.wait_ge(s_b4, c + 1)
                close_wait(dve)
                nc.vector.tensor_tensor(res1[:, r], pC[0:2 * N, r], bcs[0:32, tok], ALU.subtract).then_inc(s_b2, 1)
                dve.wait_ge(s_b2, c + 1 + 2)
                nc.vector.tensor_copy(b3t[:, r], res1[:, r]).then_inc(s_b3, 1)
                dve.wait_ge(s_rel, c + 1 + 2)
                dve.wait_ge(s_log, c + 1)
                close_wait(dve)
                nc.vector.tensor_tensor(decay[:, tok], prel[r], plog[r], ALU.add).then_inc(s_dl, 1)
                dve.wait_ge(s_b3, c + 1)
                close_wait(dve)
                nc.vector.tensor_copy(bcs[32:64, tok], b3t[:, r]).then_inc(s_bc, 1)

            dve.wait_ge(s_part, 3)
            nc.vector.tensor_copy(sel[:], part_id[:].unsqueeze(2).to_broadcast([96, 2 * N, P])).then_inc(s_sel, 1)
            dve.wait_ge(ld_x, 96)
            with dve.Fori(0, NCH // 2) as it:
                for r in range(2):
                    split(2 * it + r, r)
            dve.wait_ge(ld_w, 16 * LW)
            dve.wait_ge(s_ident, 3)
            dve.sem_inc(y_acc, 2)
            nc.vector.tensor_scalar(gw[:], wout[:], lng[:], None, ALU.mult)
            nc.vector.tensor_copy(lnb_rep[:], lnb[:].to_broadcast([D, P]))
            nc.vector.tensor_scalar(diag_dp[:], ident[:], dp[:], None, ALU.mult)
            nc.vector.tensor_copy(proj[:, D:2 * D], ident[:])
            nc.vector.tensor_tensor(gkv[:], gk[:, 1], gk[:, 2], ALU.add).then_inc(s_setup_pe, 1)
            dve.wait_ge(s_aexp, 1)
            nc.vector.tensor_scalar(Aneg[:], Aneg[:], -1.0, -1e-27, ALU.mult, ALU.min).then_inc(s_A, 2)
            dve.wait_ge(s_const2, 1)
            nc.vector.tensor_copy(proj[:, 0:D], pq[:, 0:D])
            nc.vector.tensor_copy(cvec[:], pq[:, D:2 * D]).then_inc(s_proj, 1)
            dve.wait_ge(s_dx, NCH)
            dve.wait_ge(s_dl, NCH)
            dve.wait_ge(s_bc, NCH)
            nc.vector.memset(decay[:, 0:T:S], BIG).then_inc(s_dec, 1)

            def product(n, tok):
                nc.vector.tensor_tensor(u[:, n % DEPTH], dx[:, tok], pB[:, n % 2], ALU.mult).then_inc(u_done, 1)

            dve.wait_ge(s_const, 3)
            dve.wait_ge(B_ready, 1)
            product(0, slice(0, CH))

            def residual_rows(blocks):
                for b in blocks:
                    last = nc.vector.scalar_tensor_tensor(z[:, b], p_sb[:, b], rstd[:, b:b + 1], xc[:, b],
                                                          ALU.mult, ALU.add)
                return last

            def row_stats(blocks):
                for b in blocks:
                    last = nc.vector.bn_stats(st2[:, b], z[:, b])
                return last

            def normal_rows(blocks):
                for b in blocks:
                    last = nc.vector.tensor_scalar(x1_st[:, b], z[:, b], mv2[:, b, 0:1], rstd2[:, b:b + 1],
                                                   ALU.subtract, ALU.mult)
                return last

            def tail(c, n):
                if n == 3:
                    dve.wait_ge(g_done, c + 1)
                    nc.vector.tensor_tensor(gates[:, ds(c, 1)].rearrange("p c b g -> p (c b) g"),
                                            pq[:, 0:TB * 2 * H].rearrange("p (b g) -> p b g", b=TB),
                                            gbias[:].unsqueeze(1).to_broadcast([P, TB, 2 * H]),
                                            ALU.add).then_inc(g_copied, 1)
                if n in (5, 7):
                    half = (n - 5) // 2
                    dve.wait_ge(p_done, 2 * c + half + 1 + ONE)
                    dve.wait_ge(mv_done, c + ONE)
                    for b in range(2):
                        last = nc.vector.bn_stats(st[:, 2 * half + b], pq[:, b * 2 * D + D:b * 2 * D + 2 * D])
                    last.then_inc(st_done, 1)
                if n == 8:
                    dve.wait_ge(st_done, 2 * c + 2)
                    close_wait(dve)
                    for b in range(TB):
                        last = nc.vector.bn_aggr(mv[:, b], st[:, b])
                    last.then_inc(mv_done, 1)
                if n == 9:
                    dve.wait_ge(rs_done, c + 1)
                    dve.wait_ge(p_copied, 2 * c + 2)
                    dve.wait_ge(xc_done, c + 1)
                    residual_rows(range(0, 2)).then_inc(z_half, 1)
                if n == 10:
                    residual_rows(range(2, TB)).then_inc(z_done, 1)
                    dve.wait_ge(z_half, c + 1)
                    row_stats(range(0, 2))
                if n == 11:
                    dve.wait_ge(z_done, c + 1 + ONE)
                    row_stats(range(2, TB)).then_inc(st2_done, 1)
                if n == 12:
                    dve.wait_ge(st2_done, c + 1)
                    close_wait(dve)
                    for b in range(TB):
                        last = nc.vector.bn_aggr(mv2[:, b], st2[:, b])
                    last.then_inc(mv2_done, 1)
                if n == 13:
                    dve.wait_ge(rs2_done, c + 1)
                    dve.wait_ge(x1_kept, 16 * c + ONE)
                    dve.wait_ge(x1T_done, c + ONE)
                    normal_rows(range(0, 2))
                if n == 14:
                    normal_rows(range(2, TB)).then_inc(x1_done, 1)

            with dve.Fori(0, NCH) as c:
                for n in range(N):
                    k = c * N + n
                    nxt = ds(c * CH, CH) if n < N - 1 else ds(c * CH + CH, CH)
                    dve.wait_ge(B_ready, k + 2)
                    dve.wait_ge(h_done, k + 1)
                    product((n + 1) % N, nxt)
                    dve.wait_ge(a_ready, k + 1)
                    dve.wait_ge(u_done, k + 1)
                    dve.wait_ge(hc_done, k + 1)
                    nc.vector.tensor_tensor_scan(h[:, n % DEPTH], pa[:, n % 2], u[:, n % DEPTH], 0.0, ALU.mult,
                                                 ALU.add).then_inc(h_done, 1)
                    tail(c, n)
            for n in range(N):
                tail(NCH, n)
            tail(NCH + 1, 3)
            v3 = "p (n h) -> p n h"
            gv = gates[:, 2:].rearrange("p c b g -> p (c b) g")
            dve.wait_ge(g_copied, NCH + 2)
            dve.wait_ge(act_step, 3)
            nc.vector.scalar_tensor_tensor(lfg[:].rearrange(v3, h=H), gv[:, :, H:2 * H], 0.0, glog[:].rearrange(v3, h=H),
                                           ALU.min, ALU.subtract).then_inc(gate_step, 1)
            dve.wait_ge(gate_step, 2)
            nc.vector.tensor_copy(cs_sb[:], pq[:, 0:NG])
            nc.vector.tensor_tensor(g_sb[:].rearrange(v3, h=H), gv[:, :, 0:H], pq[:, 0:NG].rearrange(v3, h=H),
                                    ALU.subtract).then_inc(gate_step, 1)
            dve.wait_ge(gate_step, 4)
            nc.vector.tensor_tensor_scan(mrow[:], fence[:], pC[:, 0, 0:P], 0.0, ALU.add, ALU.max).then_inc(gate_step, 1)
            dve.wait_ge(gate_step, 5)
            nc.vector.engine_nop().then_inc(m_ready, 1)
            dve.wait_ge(gate_step, 6)
            nc.vector.tensor_tensor(nlog[:], cs_sb[:], pC[:, 1, 0:NG], ALU.add).then_inc(gate_step, 1)
            dve.wait_ge(E_ready, 1)
            HD = D // H
            M = TB * H
            NSTEP = 8
            two = lambda v: v.rearrange("p (a m) -> p a m", a=2)
            pav = pC[:, :, 0:(M // 2) * (HD + 1)].rearrange("p a (m e) -> p a m e", e=HD + 1)
            wide = [P, TB, E]

            def add_gates(c):
                dve.wait_ge(lm1, c + 1)
                g_c = g_sb[:, ds(c * M, M)].unsqueeze(2).to_broadcast([P, M, S])
                lm = lmask.rearrange("p (m s) -> p m s", s=S)
                close_wait(dve)
                nc.vector.tensor_tensor(lm, lm, g_c, ALU.add).then_inc(lm2, 1)

            def weights(c):
                dve.wait_ge(D_done, c + 1 + ONE)
                dve.wait_ge(qk_done, c + 1)
                scale = float(HD) ** -0.5
                for hh in range(H):
                    bank = (pa if hh < 2 else pB)[:, hh % 2, 0:TB * S].rearrange("p (b s) -> p b s", s=S)
                    pick = lambda v: v.rearrange("p (b h s) -> p h b s", h=H, s=S)[:, hh]
                    last = nc.vector.scalar_tensor_tensor(pick(Cm), bank, scale, pick(Dm), ALU.mult, ALU.mult)
                last.then_inc(C_done, 1)

            def normalize(c, part):
                s0 = c * NSTEP
                if part == 0:
                    dve.wait_ge(av_done, c + 1)
                    close_wait(dve)
                    nc.vector.tensor_tensor(two(rs[:]), pav[:, :, :, HD], two(floor_[:, ds(c * M, M)]),
                                            ALU.max).then_inc(n_step, 1)
                if part == 1:
                    dve.wait_ge(n_step, s0 + 1)
                    nc.vector.scalar_tensor_tensor(two(rs[:]), pav[:, :, :, HD], -1.0, two(rs[:]),
                                                   ALU.mult, ALU.max).then_inc(n_step, 1)
                if part == 2:
                    dve.wait_ge(n_step, s0 + 2)
                    nc.vector.tensor_scalar(rs[:], rs[:], 1e-6, None, ALU.add).then_inc(n_step, 1)
                if part == 3:
                    dve.wait_ge(n_step, s0 + 3)
                    nc.vector.reciprocal(rinv[:], rs[:]).then_inc(n_step, 1)
                if part == 4:
                    dve.wait_ge(n_step, s0 + 4)
                    nc.vector.tensor_tensor(hv[:].rearrange("p (a m) e -> p a m e", a=2), pav[:, :, :, 0:HD],
                                            two(rinv[:]).unsqueeze(3).to_broadcast([P, 2, M // 2, HD]),
                                            ALU.mult).then_inc(hv_done, 1)
                if part == 5:
                    dve.wait_ge(hv_done, c + 1 + ONE)
                    nc.vector.tensor_reduce(hsum[:], hv[:], AX.X, ALU.add).then_inc(n_step, 1)
                if part == 6:
                    dve.wait_ge(n_step, s0 + 5)
                    nc.vector.scalar_tensor_tensor(cen[:], hsum[:].unsqueeze(2).to_broadcast([P, M, HD]), -1.0 / HD, hv[:],
                                                   ALU.mult, ALU.add).then_inc(cen_done, 1)
                if part == 7:
                    dve.wait_ge(sq_done, c + 1)
                    nc.vector.tensor_reduce(vsum[:], sq[:], AX.X, ALU.add).then_inc(vsum_done, 1)
                if part == 8:
                    dve.wait_ge(vrs_done, c + 1)
                    nc.vector.tensor_tensor(cen[:], cen[:], vrs[:].unsqueeze(2).to_broadcast([P, M, HD]),
                                            ALU.mult).then_inc(n_step, 1)
                if part == 9:
                    dve.wait_ge(n_step, s0 + 6)
                    nc.vector.tensor_tensor(hv[:].rearrange("p (b h) e -> p b (h e)", b=TB),
                                            cen[:].rearrange("p (b h) e -> p b (h e)", b=TB),
                                            onorm[:].unsqueeze(1).to_broadcast([P, TB, D]), ALU.mult).then_inc(n_step, 1)
                if part == 10:
                    dve.wait_ge(n_step, s0 + 7)
                    dve.wait_ge(b_x1, 16 * c + 16)
                    nc.vector.tensor_tensor(z[:], hv[:].rearrange("p (b h) e -> p b (h e)", b=TB), x1c[:],
                                            ALU.add).then_inc(zb_done, 1)
                if part == 11:
                    dve.wait_ge(zb_done, c + 1)
                    for b in range(TB):
                        last = nc.vector.bn_stats(st[:, b], z[:, b])
                    last.then_inc(n_step, 1)
                if part == 12:
                    dve.wait_ge(n_step, s0 + 8)
                    close_wait(dve)
                    for b in range(TB):
                        last = nc.vector.bn_aggr(mv[:, b], st[:, b])
                    last.then_inc(mvb_done, 1)
                if part == 13:
                    dve.wait_ge(rsb_done, c + 1)
                    dve.wait_ge(x2_kept, 16 * c + ONE)
                    dve.wait_ge(x2T_done, c + ONE)
                    dve.wait_ge(rows_done, c + ONE)
                    for b in range(TB):
                        last = nc.vector.tensor_scalar(x2_st[:, b], z[:, b], mv[:, b, 0:1], rstd[:, b:b + 1],
                                                       ALU.subtract, ALU.mult)
                    last.then_inc(x2_done, 1)

            done = [0]

            def route_wait(c):
                dve.wait_ge(r_step, NR * c + done[0])
                done[0] += 1

            def route(c, part):
                if part == 0:
                    done[0] = 1
                    dve.wait_ge(lg_done, c + 1)
                    nc.vector.tensor_copy(lgc[:], py[:, 0:TB * E].rearrange("p (b e) -> p b e", e=E)).then_inc(r_step, 1)
                if 1 <= part <= 10:
                    k, what = (part - 1) // 5, (part - 1) % 5
                    src = rest[:] if k else lgc[:]
                    route_wait(c)
                    if what == 0:
                        nc.vector.tensor_reduce(top[:, k], src, AX.X, ALU.max).then_inc(r_step, 1)
                    if what == 1:
                        nc.vector.tensor_tensor(tie[:], src, top[:, k].unsqueeze(2).to_broadcast(wide),
                                                ALU.is_equal).then_inc(r_step, 1)
                    if what == 2:
                        nc.vector.tensor_tensor(tie[:], tie[:], rank[:].unsqueeze(1).to_broadcast(wide),
                                                ALU.mult).then_inc(r_step, 1)
                    if what == 3:
                        nc.vector.tensor_reduce(tmax[:], tie[:], AX.X, ALU.max).then_inc(r_step, 1)
                    if what == 4:
                        nc.vector.tensor_tensor(hot[:, k], tie[:], tmax[:].unsqueeze(2).to_broadcast(wide),
                                                ALU.is_equal).then_inc(r_step, 1)
                        if k == 0:
                            route_wait(c)
                            nc.vector.scalar_tensor_tensor(rest[:], hot[:, 0], -BIG, lgc[:], ALU.mult,
                                                           ALU.add).then_inc(r_step, 1)
                if part == 11:
                    route_wait(c)
                    nc.vector.tensor_tensor(mask[:], hot[:, 0], hot[:, 1], ALU.add).then_inc(mask_done, 1)
                    nc.vector.tensor_tensor(share[:, 0], top[:, 1], top[:, 0], ALU.subtract).then_inc(r_step, 1)
                    assert done[0] == RS
                if part == 12:
                    dve.wait_ge(sc_sem, 128 * c + 16)
                    route_wait(c)
                    nc.vector.tensor_copy(x2r[:, :, :, D].bitcast(i32), destf[:]).then_inc(r_step, 1)
                if part == 13:
                    dve.wait_ge(r_exp, c + 1 + ONE)
                    nc.vector.tensor_scalar(share[:, 0], share[:, 1], 1.0, None, ALU.add).then_inc(r_step, 1)
                    done[0] += 1
                if part == 14:
                    route_wait(c)
                    nc.vector.reciprocal(share[:, 2], share[:, 0]).then_inc(r_step, 1)
                if part == 15:
                    nc.vector.tensor_scalar(destf[:], destf[:], float(CH), None, ALU.add).then_inc(r_step, 1)
                    done[0] += 1
                if part == 16:
                    route_wait(c)
                    nc.vector.tensor_copy(x2r[:, 0, :, D + 1], share[:, 2]).then_inc(r_step, 1)
                    nc.vector.tensor_tensor(x2r[:, 1, :, D + 1], share[:, 1], share[:, 2], ALU.mult).then_inc(r_step, 1)
                    done[0] += 1
                if part == 17:
                    dve.wait_ge(rk_done, c + 1)
                    dve.wait_ge(lg_copied, c + ONE)
                    nc.vector.tensor_tensor(pos[:], pq[:, 0:TB * E].rearrange("p (b e) -> p b e", e=E),
                                            carry[:].unsqueeze(1).to_broadcast(wide), ALU.add).then_inc(r_step, 1)
                    done[0] += 1
                    dve.wait_ge(r_step, NR * c + done[0])
                    nc.vector.tensor_tensor(carry[:], carry[:], py[:, TB * E:(TB + 1) * E], ALU.add).then_inc(lg_copied, 1)
                if part == 18:
                    route_wait(c)
                    for k in range(K2):
                        last = nc.vector.tensor_tensor(hp[:, k * TB:(k + 1) * TB], hot[:, k], pos[:], ALU.mult)
                    last.then_inc(r_step, 1)
                if part == 19:
                    route_wait(c)
                    nc.vector.tensor_reduce(posf[:], hp[:], AX.X, ALU.add).then_inc(r_step, 1)
                if part == 20:
                    route_wait(c)
                    nc.vector.tensor_copy(idx[:], posf[:]).then_inc(idx_done, 1)
                    assert done[0] - 1 == NR, done[0]

            def attend_round(c, front=True, middle=True, back=True):
                def mid(*parts):
                    for part in parts if middle else ():
                        normalize(c, part)

                def rt(*parts):
                    for part in parts if back else ():
                        route(c - 1, part)

                mid(0)
                if front:
                    add_gates(c + 1)
                mid(1)
                mid(2)
                mid(3)
                mid(4)
                mid(5)
                rt(0)
                mid(6)
                rt(1)
                rt(2)
                rt(3)
                rt(4)
                mid(7)
                rt(5)
                rt(6)
                mid(8)
                if front:
                    weights(c + 1)
                rt(7)
                mid(9)
                rt(8)
                mid(10)
                rt(9)
                mid(11)
                rt(10)
                mid(12)
                rt(11)
                rt(12)
                rt(13)
                rt(14)
                rt(15)
                rt(16)
                mid(13)
                rt(17)
                rt(18)
                rt(19)
                rt(20)

            attend_round(-1, middle=False, back=False)
            attend_round(0, back=False)
            with dve.Fori(0, NCH - 2) as c:
                attend_round(c + 1)
            attend_round(NCH - 1, front=False)
            attend_round(NCH, front=False, middle=False)
            steps = [0]

            def tlink(ins):
                steps[0] += 1
                ins.then_inc(t_step, 1)
                dve.wait_ge(t_step, steps[0])

            dve.wait_ge(idx_done, NCH)
            tlink(nc.vector.tensor_copy(zidx[:], carry[:]))
            dve.sem_inc(tab_done, 1)
            tlink(nc.vector.tensor_tensor(cnt[:], carry[:], regbase[:], ALU.subtract))
            tlink(nc.vector.tensor_tensor(kcmp[:], cnt[:].unsqueeze(2).to_broadcast([P, E, T // P]), kstep[:], ALU.is_gt))
            tlink(nc.vector.tensor_reduce(ntl[:], kcmp[:], AX.X, ALU.add))
            tlink(nc.vector.tensor_tensor_scan(cum[:], onesf[:], ntl[:], 0.0, ALU.mult, ALU.add))
            tlink(nc.vector.tensor_scalar(skip[:], ntl[:], -float(P), float(REG), ALU.mult, ALU.add))
            tshape = [P, NTAB, E]
            tlink(nc.vector.tensor_tensor(tge, tix[:].unsqueeze(2).to_broadcast(tshape),
                                          cum[:].unsqueeze(1).to_broadcast(tshape), ALU.is_ge))
            tlink(nc.vector.tensor_tensor(tw, tge, skip[:].unsqueeze(1).to_broadcast(tshape), ALU.mult))
            tlink(nc.vector.tensor_reduce(tsum[:, 0], tge, AX.X, ALU.add))
            tlink(nc.vector.tensor_reduce(tsum[:, 1], tw, AX.X, ALU.add))
            tlink(nc.vector.tensor_scalar(tsum[:, 0], tsum[:, 0], float(E - 1), float(F), ALU.min, ALU.mult))
            tlink(nc.vector.scalar_tensor_tensor(tsum[:, 1], tix[:], float(P), tsum[:, 1], ALU.mult, ALU.add))
            tlink(nc.vector.tensor_copy(eoff[:], tsum[:, 0]))
            tlink(nc.vector.tensor_copy(rowt[:], tsum[:, 1]))
            dve.sem_inc(tab_done, 1)

            def product_h(q, slot):
                i = 4 * q + slot
                dve.wait_ge(sil_done, i + 1)
                nc.vector.tensor_tensor(hs[:, slot % 2], sil[:, slot % 2], pB[:, slot % 2], ALU.mult).then_inc(mul_done, 1)

            def copy_xT(q, slot):
                i = 4 * q + slot
                dve.wait_ge(xT_tr, i + 1 + 4)
                nc.vector.tensor_copy(xgT[:, slot % 4], pq[:, 0:P]).then_inc(xT_cp, 1)

            copy_xT(0, 0)
            copy_xT(0, 1)
            product_h(0, 0)
            product_h(0, 1)
            copy_xT(0, 2)
            with dve.Fori(0, (NTIL - 4) // 4) as it:
                for r in range(4):
                    i = it * 4 + 1 + r
                    copy_xT(it, r + 3)
                    product_h(it, r + 2)
            for i in range(NTIL - 3, NTIL):
                if i + 2 < NTIL:
                    copy_xT(0, i + 2)
                if i + 1 < NTIL:
                    product_h(0, i + 1)

            def add_rows(c):
                tok = slice(c * CH, (c + 1) * CH)
                dve.wait_ge(res_done, c + 1)
                dve.wait_ge(y_in[c], 32)
                nc.vector.tensor_tensor(y0_all[:, tok], y0_all[:, tok], x2_all[:, tok], ALU.add).then_inc(zsum, 1)

            def shift(c):
                dve.wait_ge(frs, c + 1)
                if c >= 2:
                    dve.wait_ge(fz, c - 1)
                nc.vector.scalar_tensor_tensor(last_nm[:, c % 2], last_mv[c % 2][:, :, 0], -1.0, last_rs[c % 2][:],
                                               ALU.mult, ALU.mult).then_inc(fnm, 1)

            add_rows(0)
            for c in range(NCH):
                dve.wait_ge(zsum, c + 1)
                if c >= 2:
                    dve.wait_ge(fmv, c - 1)
                for b in range(TB):
                    last = nc.vector.bn_stats(last_st[c % 2][:, b], y0_all[:, (c * TB + b) * D:(c * TB + b + 1) * D])
                last.then_inc(fst, 1)
                if c + 1 < NCH:
                    add_rows(c + 1)
                dve.wait_ge(fst, c + 1)
                if c >= 2:
                    dve.wait_ge(fnm, c - 1)
                close_wait(dve)
                for b in range(TB):
                    last = nc.vector.bn_aggr(last_mv[c % 2][:, b], last_st[c % 2][:, b])
                last.then_inc(fmv, 1)
                if c:
                    shift(c - 1)
            shift(NCH - 1)


_LAYOUT = [
    ("x_tok", lambda i: i["x"].reshape(4096, 128)),
    ("x_T", lambda i: i["x"].reshape(4096, 128).T),
    ("ctx_tok", lambda i: i["ctx_1024"].reshape(4096, 128)),
    ("ctx_T", lambda i: i["ctx_1024"].reshape(4096, 128).T),
    ("W_dtw_T", lambda i: i["L0_attn_W_dtw"].T),
    ("W_dt_T", lambda i: i["L0_attn_W_dt"].T),
    ("b_dt", lambda i: i["L0_attn_b_dt"][:, None]),
    ("A_log", lambda i: i["L0_attn_A_log"]),
    ("W_BC_T", "bc"),
    ("Dp", lambda i: i["L0_attn_Dp"][:, None]),
    ("ln_g", lambda i: i["L0_attn_ln_g"][:, None]),
    ("ln_b", lambda i: i["L0_attn_ln_b"][:, None]),
    ("W_out_T", lambda i: i["L0_attn_W_out"].T),
    ("gate_kernel", "gk"),
    ("gate_bias", "gb"),
    ("outnorm", lambda i: i["L0_xattn_outnorm_scale"][None, :]),
    ("router_w", lambda i: i["L0_ffn_gate_w"]),
    ("w1", lambda i: i["L0_ffn_w1"]),
    ("w3", lambda i: i["L0_ffn_w3"]),
    ("w2", lambda i: i["L0_ffn_w2"]),
]


def kernel(**inputs):
    import numpy as np
    import concourse.bacc as bacc
    from concourse.bass_utils import run_bass_kernel_spmd

    i = {k: np.asarray(v) for k, v in inputs.items()}
    joined = {
        "bc": lambda: np.concatenate([i["L0_attn_W_B"].T, i["L0_attn_W_C"].T], axis=1),
        "gk": lambda: np.concatenate([i["L0_xattn_igate_kernel"], i["L0_xattn_fgate_kernel"]], axis=1),
        "gb": lambda: np.concatenate([i["L0_xattn_igate_bias"], i["L0_xattn_fgate_bias"]])[None, :],
    }
    nc = bacc.Bacc("TRN2", target_bir_lowering=False, num_devices=1)
    arrays, args = {}, []
    for name, make in _LAYOUT:
        a = np.ascontiguousarray(joined[make]() if isinstance(make, str) else make(i))
        arrays[f"in_{name}"] = a
        args.append(nc.dram_tensor(f"in_{name}", a.shape, mybir.dt.from_np(a.dtype), kind="ExternalInput").ap())
    args.append(nc.dram_tensor("out_0", (4096, 128), mybir.dt.float32, kind="ExternalOutput").ap())
    decoder_layer(nc, *args)
    r = run_bass_kernel_spmd(nc, [arrays], core_ids=[0])
    return r.results[0]["out_0"].reshape(64, 64, 128)
```
